# Optimizing a Trainium2 kernel written in Bass

```python
import numpy as np
import jax
import jax.numpy as jnp

def _softmax(x, axis=-1):
    return jax.nn.softmax(x, axis=axis)

def _gelu(x):
    return jax.nn.gelu(x, approximate=True)

def _silu(x):
    return jax.nn.silu(x)

def _sigmoid(x):
    return jax.nn.sigmoid(x)

def _layernorm(x, axis=-1, eps=1e-05):
    m = jnp.mean(x, axis=axis, keepdims=True)
    v = jnp.var(x, axis=axis, keepdims=True)
    return (x - m) / jnp.sqrt(v + eps)

def _scatter_add(tgt, idx, src, axis=0):
    return tgt.at[idx].add(src)

def _segment_sum(src, seg, n):
    return jax.ops.segment_sum(src, seg, n)
kernel_name = 'mk_perceiver_d2_seqx_r8_0c69f4'

def setup_inputs(seed: int=0):
    np.random.seed(seed)
    _w = jnp.asarray

    def _rec_inputs():
        import jax
        import jax.numpy as jnp
        _rk = jax.random.key(seed)
        x = 7.22e-05 + 1 * jax.random.normal(jax.random.fold_in(_rk, 1), (64, 32, 128), jnp.float32)
        _lenS = 32 - jax.random.randint(jax.random.fold_in(_rk, 7), (64,), 0, max(1, 32 // 4) + 1, jnp.int32)
        _lenS2 = 257 - jax.random.randint(jax.random.fold_in(_rk, 8), (64,), 0, max(1, 257 // 4) + 1, jnp.int32)
        _ctx_1024P = jax.random.normal(jax.random.fold_in(_rk, 11), (64, 16, 128), jnp.float32)
        _ctx_1024c = jax.random.dirichlet(jax.random.fold_in(_rk, 511), 0.3 * jnp.ones((16,), jnp.float32), (64, 257))
        _ctx_1024t = jnp.einsum('bsk,bkd->bsd', _ctx_1024c, _ctx_1024P)
        _ctx_1024t = _ctx_1024t * jax.lax.rsqrt(jnp.mean(jnp.square(_ctx_1024t)) + 1e-12) * 0.953939
        ctx_1024 = 4.13588e-05 + 0.999923 * (_ctx_1024t + 0.3 * jax.random.normal(jax.random.fold_in(_rk, 611), (64, 257, 128), jnp.float32))
        return (x, ctx_1024)
    x, ctx_1024 = _rec_inputs()

    def _L0_xattn_setup():
        import jax, jax.numpy as jnp
        import numpy as np
        import math
        D = 128
        H = 8
        HD = D // H
        TEMP = math.sqrt(D)
        EPS = 1e-05

        def _layernorm(x, g, b):
            mu = jnp.mean(x, axis=-1, keepdims=True)
            var = jnp.var(x, axis=-1, keepdims=True)
            return (x - mu) * jax.lax.rsqrt(var + EPS) * g + b
        key = jax.random.key(seed)
        ks = jax.random.split(key, 8)
        B, Lq, Lk = (4, 256, 256)
        Q = jax.random.normal(ks[0], (B, Lq, D), dtype=jnp.float32)
        K = jax.random.normal(ks[1], (B, Lk, D), dtype=jnp.float32)
        V = jax.random.normal(ks[2], (B, Lk, D), dtype=jnp.float32)
        Wq = jax.random.normal(ks[3], (D, D), dtype=jnp.float32) * 0.02
        Wk = jax.random.normal(ks[4], (D, D), dtype=jnp.float32) * 0.02
        Wv = jax.random.normal(ks[5], (D, D), dtype=jnp.float32) * 0.02
        Wo = jax.random.normal(ks[6], (D, D), dtype=jnp.float32) * 0.02
        pre_g = jnp.ones((D,), jnp.float32)
        pre_b = jnp.zeros((D,), jnp.float32)
        ln_g = jnp.ones((D,), jnp.float32)
        ln_b = jnp.zeros((D,), jnp.float32)
        return {'Q': Q, 'K': K, 'V': V, 'Wq': Wq, 'Wk': Wk, 'Wv': Wv, 'Wo': Wo, 'pre_g': pre_g, 'pre_b': pre_b, 'ln_g': ln_g, 'ln_b': ln_b}
    _L0_xattn_all = _L0_xattn_setup()
    _L0_xattn_in = {k: v for k, v in _L0_xattn_all.items() if k in ('Wq', 'Wk', 'Wv', 'Wo', 'pre_g', 'pre_b', 'ln_g', 'ln_b')}
    del _L0_xattn_all

    def _L0_attn_setup():
        import jax, jax.numpy as jnp
        import numpy as np
        B, S, D = (4, 256, 128)
        key = jax.random.key(seed)
        k1, k2, k3, k4 = jax.random.split(key, 4)
        x = jax.random.normal(k1, (B, S, D), dtype=jnp.float32)
        scale = 1.0 / np.sqrt(D)
        wq = jax.random.uniform(k2, (D, D), dtype=jnp.float32, minval=-scale, maxval=scale)
        wk = jax.random.uniform(k3, (D, D), dtype=jnp.float32, minval=-scale, maxval=scale)
        wv = jax.random.uniform(k4, (D, D), dtype=jnp.float32, minval=-scale, maxval=scale)
        return {'x': x, 'wq': wq, 'wk': wk, 'wv': wv}
    _L0_attn_all = _L0_attn_setup()
    _L0_attn_in = {k: v for k, v in _L0_attn_all.items() if k in ('wq', 'wk', 'wv')}
    del _L0_attn_all

    def _L0_ffn_setup():
        import jax, jax.numpy as jnp
        import numpy as np
        B, S, D, E, K = (4, 256, 128, 8, 2)
        H = 4 * D
        key = jax.random.key(seed)
        k0, k1, k2, k3 = jax.random.split(key, 4)
        x = jax.random.normal(k0, (B, S, D), dtype=jnp.float32)
        router_w = jax.random.normal(k1, (E, D), dtype=jnp.float32) * 0.02
        w1 = jax.random.normal(k2, (E, H, D), dtype=jnp.float32) * 0.02
        w2 = jax.random.normal(k3, (E, D, H), dtype=jnp.float32) * 0.02
        return {'x': x, 'router_w': router_w, 'w1': w1, 'w2': w2}
    _L0_ffn_all = _L0_ffn_setup()
    _L0_ffn_in = {k: v for k, v in _L0_ffn_all.items() if k in ('router_w', 'w1', 'w2')}
    del _L0_ffn_all

    def _L1_xattn_setup():
        import jax, jax.numpy as jnp
        import numpy as np
        DIM = 128
        HEADS = 16
        DIM_HEAD = 64
        INNER = HEADS * DIM_HEAD
        EPS = 1e-05

        def _layernorm(x, w, b):
            m = jnp.mean(x, axis=-1, keepdims=True)
            v = jnp.mean(jnp.square(x - m), axis=-1, keepdims=True)
            return (x - m) * jax.lax.rsqrt(v + EPS) * w + b
        key = jax.random.key(seed)
        ks = jax.random.split(key, 9)
        B, N, L = (8, 512, 64)
        x = jax.random.normal(ks[0], (B, N, DIM), dtype=jnp.float32)
        latents = jax.random.normal(ks[1], (B, L, DIM), dtype=jnp.float32)
        s = 1.0 / np.sqrt(DIM)
        Wq = jax.random.normal(ks[2], (DIM, INNER), dtype=jnp.float32) * s
        Wkv = jax.random.normal(ks[3], (DIM, 2 * INNER), dtype=jnp.float32) * s
        Wo = jax.random.normal(ks[4], (INNER, DIM), dtype=jnp.float32) * (1.0 / np.sqrt(INNER))
        ln1_w = jnp.ones((DIM,), jnp.float32)
        ln1_b = jnp.zeros((DIM,), jnp.float32)
        ln2_w = jnp.ones((DIM,), jnp.float32)
        ln2_b = jnp.zeros((DIM,), jnp.float32)
        return {'x': x, 'latents': latents, 'Wq': Wq, 'Wkv': Wkv, 'Wo': Wo, 'ln1_w': ln1_w, 'ln1_b': ln1_b, 'ln2_w': ln2_w, 'ln2_b': ln2_b}
    _L1_xattn_all = _L1_xattn_setup()
    _L1_xattn_in = {k: v for k, v in _L1_xattn_all.items() if k in ('Wq', 'Wkv', 'Wo', 'ln1_w', 'ln1_b', 'ln2_w', 'ln2_b')}
    del _L1_xattn_all

    def _L1_attn_setup():
        import jax, jax.numpy as jnp
        import numpy as np
        B, L = (2, 128)
        D_MODEL, D_INNER, D_STATE, D_CONV, DT_RANK, D_FF = (128, 256, 16, 4, 64, 512)
        EPS = 1e-06

        def rmsnorm(x, w):
            return x * jax.lax.rsqrt(jnp.mean(x * x, axis=-1, keepdims=True) + EPS) * w

        def _ste(x, q):
            return x + jax.lax.stop_gradient(q - x)

        def bitlinear(x, w):
            ws = jnp.maximum(jnp.mean(jnp.abs(w)), 1e-05)
            wq = jnp.clip(jnp.round(w / ws), -1.0, 1.0) * ws
            xm = jnp.maximum(jnp.max(jnp.abs(x), axis=-1, keepdims=True), 1e-05)
            xq = jnp.clip(jnp.round(x * (127.0 / xm)), -128.0, 127.0) * (xm / 127.0)
            return _ste(x, xq) @ _ste(w, wq).T

        def mamba_block(x, in_proj_w, conv_w, conv_b, x_proj_w, dt_proj_w, dt_proj_b, A_log, D, out_proj_w):
            b, l, _ = x.shape
            u, res = jnp.split(x @ in_proj_w.T, 2, axis=-1)
            u_c = jnp.transpose(u, (0, 2, 1))
            u_c = jnp.pad(u_c, ((0, 0), (0, 0), (D_CONV - 1, 0)))
            u_c = jax.lax.conv_general_dilated(u_c, conv_w[:, None, :], (1,), 'VALID', dimension_numbers=('NCH', 'OIH', 'NCH'), feature_group_count=D_INNER) + conv_b[None, :, None]
            u = jax.nn.silu(jnp.transpose(u_c, (0, 2, 1)))
            x_dbl = u @ x_proj_w.T
            dt, Bm, Cm = jnp.split(x_dbl, [DT_RANK, DT_RANK + D_STATE], axis=-1)
            delta = jax.nn.softplus(dt @ dt_proj_w.T + dt_proj_b)
            A = -jnp.exp(A_log)
            deltaA = jnp.exp(delta[..., None] * A)
            deltaBu = delta[..., None] * Bm[:, :, None, :] * u[..., None]

            def step(h, inp):
                dA, dBu, Ct = inp
                h = dA * h + dBu
                return (h, jnp.einsum('bdn,bn->bd', h, Ct))
            h0 = jnp.zeros((b, D_INNER, D_STATE), x.dtype)
            xs = (jnp.transpose(deltaA, (1, 0, 2, 3)), jnp.transpose(deltaBu, (1, 0, 2, 3)), jnp.transpose(Cm, (1, 0, 2)))
            _, ys = jax.lax.scan(step, h0, xs)
            y = jnp.transpose(ys, (1, 0, 2)) + u * D
            y = y * jax.nn.silu(res)
            return y @ out_proj_w.T
        key = jax.random.key(seed)
        ks = jax.random.split(key, 12)
        g = lambda k, shape, s: jax.random.normal(k, shape, jnp.float32) * s
        A_log = jnp.log(jnp.broadcast_to(jnp.arange(1, D_STATE + 1, dtype=jnp.float32), (D_INNER, D_STATE)))
        return {'x': jax.random.normal(ks[0], (B, L, D_MODEL), jnp.float32), 'in_proj_w': g(ks[1], (2 * D_INNER, D_MODEL), 0.02), 'conv_w': g(ks[2], (D_INNER, D_CONV), 0.2), 'conv_b': jnp.zeros((D_INNER,), jnp.float32), 'x_proj_w': g(ks[3], (DT_RANK + 2 * D_STATE, D_INNER), 0.02), 'dt_proj_w': g(ks[4], (D_INNER, DT_RANK), 0.05), 'dt_proj_b': jnp.full((D_INNER,), float(np.log(np.expm1(0.01))), jnp.float32), 'A_log': A_log, 'D': jnp.ones((D_INNER,), jnp.float32), 'out_proj_w': g(ks[5], (D_MODEL, D_INNER), 0.02), 'norm1_w': jnp.ones((D_MODEL,), jnp.float32), 'gate_w': g(ks[6], (D_FF, D_MODEL), 0.02), 'up_w': g(ks[7], (D_FF, D_MODEL), 0.02), 'down_w': g(ks[8], (D_MODEL, D_FF), 0.02), 'norm2_w': jnp.ones((D_MODEL,), jnp.float32)}
    _L1_attn_all = _L1_attn_setup()
    _L1_attn_in = {k: v for k, v in _L1_attn_all.items() if k in ('in_proj_w', 'conv_w', 'conv_b', 'x_proj_w', 'dt_proj_w', 'dt_proj_b', 'A_log', 'D', 'out_proj_w', 'norm1_w', 'gate_w', 'up_w', 'down_w', 'norm2_w')}
    del _L1_attn_all

    def _L1_ffn_setup():
        import jax, jax.numpy as jnp
        import numpy as np
        B, L, D, E, K, DFF = (2, 256, 128, 8, 2, 512)
        key = jax.random.key(seed)
        kx, kr, kg, ku, kd = jax.random.split(key, 5)
        scale = 0.02
        return {'x': jax.random.normal(kx, (B, L, D), dtype=jnp.float32), 'Wr': jax.random.normal(kr, (E, D), dtype=jnp.float32) * scale, 'Wg': jax.random.normal(kg, (E, DFF, D), dtype=jnp.float32) * scale, 'Wu': jax.random.normal(ku, (E, DFF, D), dtype=jnp.float32) * scale, 'Wd': jax.random.normal(kd, (E, D, DFF), dtype=jnp.float32) * scale}
    _L1_ffn_all = _L1_ffn_setup()
    _L1_ffn_in = {k: v for k, v in _L1_ffn_all.items() if k in ('Wr', 'Wg', 'Wu', 'Wd')}
    del _L1_ffn_all
    return {'x': x, 'ctx_1024': ctx_1024, 'L0_xattn_Wq': _L0_xattn_in['Wq'], 'L0_xattn_Wk': _L0_xattn_in['Wk'], 'L0_xattn_Wv': _L0_xattn_in['Wv'], 'L0_xattn_Wo': _L0_xattn_in['Wo'], 'L0_xattn_pre_g': _L0_xattn_in['pre_g'], 'L0_xattn_pre_b': _L0_xattn_in['pre_b'], 'L0_xattn_ln_g': _L0_xattn_in['ln_g'], 'L0_xattn_ln_b': _L0_xattn_in['ln_b'], 'L0_attn_wq': _L0_attn_in['wq'], 'L0_attn_wk': _L0_attn_in['wk'], 'L0_attn_wv': _L0_attn_in['wv'], 'L0_ffn_router_w': _L0_ffn_in['router_w'], 'L0_ffn_w1': _L0_ffn_in['w1'], 'L0_ffn_w2': _L0_ffn_in['w2'], 'L1_xattn_Wq': _L1_xattn_in['Wq'], 'L1_xattn_Wkv': _L1_xattn_in['Wkv'], 'L1_xattn_Wo': _L1_xattn_in['Wo'], 'L1_xattn_ln1_w': _L1_xattn_in['ln1_w'], 'L1_xattn_ln1_b': _L1_xattn_in['ln1_b'], 'L1_xattn_ln2_w': _L1_xattn_in['ln2_w'], 'L1_xattn_ln2_b': _L1_xattn_in['ln2_b'], 'L1_attn_in_proj_w': _L1_attn_in['in_proj_w'], 'L1_attn_conv_w': _L1_attn_in['conv_w'], 'L1_attn_conv_b': _L1_attn_in['conv_b'], 'L1_attn_x_proj_w': _L1_attn_in['x_proj_w'], 'L1_attn_dt_proj_w': _L1_attn_in['dt_proj_w'], 'L1_attn_dt_proj_b': _L1_attn_in['dt_proj_b'], 'L1_attn_A_log': _L1_attn_in['A_log'], 'L1_attn_D': _L1_attn_in['D'], 'L1_attn_out_proj_w': _L1_attn_in['out_proj_w'], 'L1_attn_norm1_w': _L1_attn_in['norm1_w'], 'L1_attn_gate_w': _L1_attn_in['gate_w'], 'L1_attn_up_w': _L1_attn_in['up_w'], 'L1_attn_down_w': _L1_attn_in['down_w'], 'L1_attn_norm2_w': _L1_attn_in['norm2_w'], 'L1_ffn_Wr': _L1_ffn_in['Wr'], 'L1_ffn_Wg': _L1_ffn_in['Wg'], 'L1_ffn_Wu': _L1_ffn_in['Wu'], 'L1_ffn_Wd': _L1_ffn_in['Wd']}

def reference(x, ctx_1024, L0_xattn_Wq, L0_xattn_Wk, L0_xattn_Wv, L0_xattn_Wo, L0_xattn_pre_g, L0_xattn_pre_b, L0_xattn_ln_g, L0_xattn_ln_b, L0_attn_wq, L0_attn_wk, L0_attn_wv, L0_ffn_router_w, L0_ffn_w1, L0_ffn_w2, L1_xattn_Wq, L1_xattn_Wkv, L1_xattn_Wo, L1_xattn_ln1_w, L1_xattn_ln1_b, L1_xattn_ln2_w, L1_xattn_ln2_b, L1_attn_in_proj_w, L1_attn_conv_w, L1_attn_conv_b, L1_attn_x_proj_w, L1_attn_dt_proj_w, L1_attn_dt_proj_b, L1_attn_A_log, L1_attn_D, L1_attn_out_proj_w, L1_attn_norm1_w, L1_attn_gate_w, L1_attn_up_w, L1_attn_down_w, L1_attn_norm2_w, L1_ffn_Wr, L1_ffn_Wg, L1_ffn_Wu, L1_ffn_Wd):
    import jax
    import jax.numpy as jnp

    def _L0_xattn_ref(Q, K, V, Wq, Wk, Wv, Wo, pre_g, pre_b, ln_g, ln_b):
        import jax, jax.numpy as jnp
        import numpy as np
        import math
        D = 128
        H = 8
        HD = D // H
        TEMP = math.sqrt(D)
        EPS = 1e-05

        def _layernorm(x, g, b):
            mu = jnp.mean(x, axis=-1, keepdims=True)
            var = jnp.var(x, axis=-1, keepdims=True)
            return (x - mu) * jax.lax.rsqrt(var + EPS) * g + b
        B, Lq, _ = Q.shape
        Lk = K.shape[1]
        Qn = _layernorm(Q, pre_g, pre_b)
        Kn = _layernorm(K, pre_g, pre_b)
        q = (Qn @ Wq).reshape(B, Lq, H, HD)
        k = (Kn @ Wk).reshape(B, Lk, H, HD)
        v = (V @ Wv).reshape(B, Lk, H, HD)
        scores = jnp.einsum('bqhd,bkhd->bhqk', q, k) / TEMP
        scores = jnp.clip(scores, -10000.0, 10000.0)
        A = jax.nn.softmax(scores, axis=-1)
        O = jnp.einsum('bhqk,bkhd->bqhd', A, v).reshape(B, Lq, D)
        O = _layernorm(O, ln_g, ln_b)
        O = O + jax.nn.gelu(O @ Wo, approximate=False)
        return O

    def _L0_attn_ref(x, wq, wk, wv):
        import jax, jax.numpy as jnp
        import numpy as np
        B, S, D = (4, 256, 128)
        d = wq.shape[0]
        q = x @ wq.T
        k = x @ wk.T
        v = x @ wv.T
        scores = jnp.einsum('bqd,bkd->bqk', q, k) / np.sqrt(float(d))
        a = jax.nn.softmax(scores, axis=-2)
        a = jnp.triu(a)
        attn = jnp.swapaxes(a, -2, -1) @ v
        return attn

    def _L0_ffn_ref(x, router_w, w1, w2):
        import jax, jax.numpy as jnp
        import numpy as np
        B, S, D, E, K = (4, 256, 128, 8, 2)
        H = 4 * D
        b, s, d = x.shape
        e = router_w.shape[0]
        logits = jnp.einsum('bsd,ed->bse', x, router_w)
        probs = jax.nn.softmax(logits, axis=-1)
        topk_vals, topk_idx = jax.lax.top_k(probs, K)
        x_flat = x.reshape(b * s, d)
        vals = topk_vals.reshape(b * s, K)
        idx = topk_idx.reshape(b * s, K)
        out = jnp.zeros_like(x_flat)
        for eid in range(e):
            w = jnp.sum(jnp.where(idx == eid, vals, jnp.zeros((), x.dtype)), axis=-1)
            h = jax.nn.gelu(x_flat @ w1[eid].T, approximate=False)
            y = h @ w2[eid].T
            out = out + w[:, None] * y
        return out.reshape(b, s, d)

    def _L1_xattn_ref(x, latents, Wq, Wkv, Wo, ln1_w, ln1_b, ln2_w, ln2_b):
        import jax, jax.numpy as jnp
        import numpy as np
        DIM = 128
        HEADS = 16
        DIM_HEAD = 64
        INNER = HEADS * DIM_HEAD
        EPS = 1e-05

        def _layernorm(x, w, b):
            m = jnp.mean(x, axis=-1, keepdims=True)
            v = jnp.mean(jnp.square(x - m), axis=-1, keepdims=True)
            return (x - m) * jax.lax.rsqrt(v + EPS) * w + b
        B, L, _ = latents.shape
        xn = _layernorm(x, ln1_w, ln1_b)
        ln = _layernorm(latents, ln2_w, ln2_b)
        q = ln @ Wq
        kv_input = jnp.concatenate([xn, ln], axis=-2)
        kv = kv_input @ Wkv
        k, v = jnp.split(kv, 2, axis=-1)

        def heads(t):
            b, s, _ = t.shape
            return t.reshape(b, s, HEADS, DIM_HEAD).transpose(0, 2, 1, 3)
        q, k, v = (heads(q), heads(k), heads(v))
        scale = 1.0 / np.sqrt(np.sqrt(DIM_HEAD))
        logits = jnp.einsum('bhld,bhsd->bhls', q * scale, k * scale)
        w = jax.nn.softmax(logits.astype(jnp.float32), axis=-1).astype(logits.dtype)
        out = jnp.einsum('bhls,bhsd->bhld', w, v)
        out = out.transpose(0, 2, 1, 3).reshape(B, L, INNER)
        return out @ Wo

    def _L1_attn_ref(x, in_proj_w, conv_w, conv_b, x_proj_w, dt_proj_w, dt_proj_b, A_log, D, out_proj_w, norm1_w, gate_w, up_w, down_w, norm2_w):
        import jax, jax.numpy as jnp
        import numpy as np
        B, L = (2, 128)
        D_MODEL, D_INNER, D_STATE, D_CONV, DT_RANK, D_FF = (128, 256, 16, 4, 64, 512)
        EPS = 1e-06

        def rmsnorm(x, w):
            return x * jax.lax.rsqrt(jnp.mean(x * x, axis=-1, keepdims=True) + EPS) * w

        def _ste(x, q):
            return x + jax.lax.stop_gradient(q - x)

        def bitlinear(x, w):
            ws = jnp.maximum(jnp.mean(jnp.abs(w)), 1e-05)
            wq = jnp.clip(jnp.round(w / ws), -1.0, 1.0) * ws
            xm = jnp.maximum(jnp.max(jnp.abs(x), axis=-1, keepdims=True), 1e-05)
            xq = jnp.clip(jnp.round(x * (127.0 / xm)), -128.0, 127.0) * (xm / 127.0)
            return _ste(x, xq) @ _ste(w, wq).T

        def mamba_block(x, in_proj_w, conv_w, conv_b, x_proj_w, dt_proj_w, dt_proj_b, A_log, D, out_proj_w):
            b, l, _ = x.shape
            u, res = jnp.split(x @ in_proj_w.T, 2, axis=-1)
            u_c = jnp.transpose(u, (0, 2, 1))
            u_c = jnp.pad(u_c, ((0, 0), (0, 0), (D_CONV - 1, 0)))
            u_c = jax.lax.conv_general_dilated(u_c, conv_w[:, None, :], (1,), 'VALID', dimension_numbers=('NCH', 'OIH', 'NCH'), feature_group_count=D_INNER) + conv_b[None, :, None]
            u = jax.nn.silu(jnp.transpose(u_c, (0, 2, 1)))
            x_dbl = u @ x_proj_w.T
            dt, Bm, Cm = jnp.split(x_dbl, [DT_RANK, DT_RANK + D_STATE], axis=-1)
            delta = jax.nn.softplus(dt @ dt_proj_w.T + dt_proj_b)
            A = -jnp.exp(A_log)
            deltaA = jnp.exp(delta[..., None] * A)
            deltaBu = delta[..., None] * Bm[:, :, None, :] * u[..., None]

            def step(h, inp):
                dA, dBu, Ct = inp
                h = dA * h + dBu
                return (h, jnp.einsum('bdn,bn->bd', h, Ct))
            h0 = jnp.zeros((b, D_INNER, D_STATE), x.dtype)
            xs = (jnp.transpose(deltaA, (1, 0, 2, 3)), jnp.transpose(deltaBu, (1, 0, 2, 3)), jnp.transpose(Cm, (1, 0, 2)))
            _, ys = jax.lax.scan(step, h0, xs)
            y = jnp.transpose(ys, (1, 0, 2)) + u * D
            y = y * jax.nn.silu(res)
            return y @ out_proj_w.T
        h = rmsnorm(x + mamba_block(x, in_proj_w, conv_w, conv_b, x_proj_w, dt_proj_w, dt_proj_b, A_log, D, out_proj_w), norm1_w)
        gate = jax.nn.sigmoid(bitlinear(h, gate_w))
        up = bitlinear(h, up_w)
        f = bitlinear(gate * up, down_w)
        return rmsnorm(h + f, norm2_w)

    def _L1_ffn_ref(x, Wr, Wg, Wu, Wd):
        import jax, jax.numpy as jnp
        import numpy as np
        B, L, D, E, K, DFF = (2, 256, 128, 8, 2, 512)
        Bb, Ll, Dd = x.shape
        T = Bb * Ll
        xt = x.reshape(T, Dd)
        logits = jnp.einsum('td,ed->te', xt, Wr)
        scores = jax.nn.softmax(logits, axis=-1)
        k_scores, k_ids = jax.lax.top_k(scores, K)
        eps = jnp.finfo(x.dtype).eps
        k_w = k_scores / (k_scores.sum(axis=-1, keepdims=True) + eps)
        combine = jnp.sum(jax.nn.one_hot(k_ids, E, dtype=x.dtype) * k_w[..., None], axis=1)
        g = jnp.einsum('td,efd->etf', xt, Wg)
        u = jnp.einsum('td,efd->etf', xt, Wu)
        h = jax.nn.relu(g) * u
        out_e = jnp.einsum('etf,edf->etd', h, Wd)
        out = jnp.einsum('te,etd->td', combine, out_e)
        return out.reshape(Bb, Ll, Dd)
    x = x + _L0_xattn_ref(_layernorm(x, axis=-1), ctx_1024, ctx_1024, L0_xattn_Wq, L0_xattn_Wk, L0_xattn_Wv, L0_xattn_Wo, L0_xattn_pre_g, L0_xattn_pre_b, L0_xattn_ln_g, L0_xattn_ln_b)
    x = x + _L0_attn_ref(_layernorm(x, axis=-1), L0_attn_wq, L0_attn_wk, L0_attn_wv)
    x = x + _L0_ffn_ref(_layernorm(x, axis=-1), L0_ffn_router_w, L0_ffn_w1, L0_ffn_w2)
    x = x + _L1_xattn_ref(ctx_1024, _layernorm(x, axis=-1), L1_xattn_Wq, L1_xattn_Wkv, L1_xattn_Wo, L1_xattn_ln1_w, L1_xattn_ln1_b, L1_xattn_ln2_w, L1_xattn_ln2_b)
    x = x + _L1_attn_ref(_layernorm(x, axis=-1), L1_attn_in_proj_w, L1_attn_conv_w, L1_attn_conv_b, L1_attn_x_proj_w, L1_attn_dt_proj_w, L1_attn_dt_proj_b, L1_attn_A_log, L1_attn_D, L1_attn_out_proj_w, L1_attn_norm1_w, L1_attn_gate_w, L1_attn_up_w, L1_attn_down_w, L1_attn_norm2_w)
    x = x + _L1_ffn_ref(_layernorm(x, axis=-1), L1_ffn_Wr, L1_ffn_Wg, L1_ffn_Wu, L1_ffn_Wd)
    return x

_drawn_inputs = setup_inputs


def setup_inputs(seed=0):
    import zlib

    import numpy as np

    out = dict(_drawn_inputs(seed))
    spreads = {'L0_xattn_pre_g': (1.0, 0.6),
     'L0_xattn_pre_b': (0.0, 0.8),
     'L0_xattn_ln_g': (1.0, 0.2),
     'L0_xattn_ln_b': (0.0, 0.1),
     'L1_xattn_ln1_w': (1.0, 0.2),
     'L1_xattn_ln1_b': (0.0, 0.1),
     'L1_xattn_ln2_w': (1.0, 0.2),
     'L1_xattn_ln2_b': (0.0, 0.443),
     'L1_attn_conv_b': (0.0, 0.8),
     'L1_attn_dt_proj_b': (-4.600165843963623, 0.6),
     'L1_attn_D': (1.0, 0.6),
     'L1_attn_norm1_w': (1.0, 0.2),
     'L1_attn_norm2_w': (1.0, 0.2)}
    factors = {'L0_xattn_Wq': 8.0,
     'L0_xattn_Wk': 8.0,
     'L0_attn_wq': 6.004,
     'L0_attn_wk': 5.911,
     'L0_ffn_router_w': 8.0,
     'L0_ffn_w1': 7.116,
     'L0_ffn_w2': 7.113,
     'L1_attn_in_proj_w': 8.0,
     'L1_attn_conv_w': 8.0,
     'L1_attn_x_proj_w': 8.0,
     'L1_attn_dt_proj_w': 8.0,
     'L1_attn_A_log': 8.0,
     'L1_attn_out_proj_w': 8.0,
     'L1_attn_gate_w': 8.0,
     'L1_attn_up_w': 6.255,
     'L1_attn_down_w': 6.287,
     'L1_ffn_Wr': 8.0,
     'L1_ffn_Wg': 8.0,
     'L1_ffn_Wu': 8.0,
     'L1_ffn_Wd': 8.0}
    for name, (base, spread) in spreads.items():
        noise = np.random.default_rng([zlib.crc32(name.encode()), seed]).standard_normal(out[name].shape)
        drawn = base * np.exp(spread * noise) if base else spread * noise
        out[name] = jnp.asarray(drawn.astype(out[name].dtype))
    for name, factor in factors.items():
        out[name] = (out[name] * factor).astype(out[name].dtype)
    return out
```

```python
from contextlib import ExitStack

import numpy as np

import concourse.bass as bass
from concourse import mybir

F32 = mybir.dt.float32
F32R = mybir.dt.float32r
BF16 = mybir.dt.bfloat16
I32 = mybir.dt.int32
ALU = mybir.AluOpType
ACT = mybir.ActivationFunctionType
AX = mybir.AxisListType

P = 128
D = 128
B = 64
L = 32
T = B * L
NT = T // P
BT = P // L
S_CTX = 257
KC = 86
KR = S_CTX - 2 * KC
EPS5 = 1e-5


def chain(eng, sem):
    count = [0]

    def link(ins):
        ins.then_inc(sem, 1)
        count[0] += 1
        eng.wait_ge(sem, count[0])
    return link


RELEASED = []


def place(nc, ctx, tag):
    def sb(name, shape, dt=F32):
        return ctx.enter_context(nc.sbuf_tensor(f"{tag}_{name}", shape, dt))

    def ps(name, shape, dt=F32):
        return ctx.enter_context(nc.psum_tensor(f"{tag}_{name}", shape, dt))

    def sem(name):
        s = ctx.enter_context(nc.semaphore(f"{tag}_{name}"))
        if tag != "all":
            RELEASED.append(s)
        return s
    return sb, ps, sem


def clear_stage(nc):
    with nc.Block() as block:
        @block.gpsimd
        def _(pool):
            for s in RELEASED:
                pool.sem_clear(s)
    del RELEASED[:]


def wait(eng, sem, value):
    if isinstance(value, int) and value <= 0:
        return
    eng.wait_ge(sem, value)


def attention_stage(nc, w, cross, dram):
    first = cross == 0
    tag = f"x{cross}"
    UB = 1 if first else 2
    NU = BT * UB
    GB = 2
    NUB = NU * GB
    NB = BT * GB
    TURNS = NT // GB
    KEYS = S_CTX if first else S_CTX + L
    rows = [KC, KC, KR if first else KR + L]
    cols = [0, KC, 2 * KC]
    pieces = 2 * UB
    HPG = BT + pieces
    ZPG = NU + 1
    scale = float(D) ** -0.5 if first else 0.125
    LA = 3 if first else 2
    H0 = LA + pieces
    CTX_DMAS = 2 if first else 3
    fold_slot = 0 if first else 1

    with ExitStack() as ctx:
        sb, ps, sem = place(nc, ctx, tag)
        KMAX = rows[2] if not first else KC
        Cx = sb("ctx_rows", [max(KMAX, KC), NB, 3, D])
        KT = sb("keys_T", [P, 2, KEYS])
        QF = sb("folded_q", [P, GB, BT, 8 * UB, L])
        Pr = sb("probs", [P, 2, 2, KEYS])
        PT = sb("probs_T", [max(KMAX, KC), 2, 3, 256])
        ZT = sb("values_T", [P, 8 * UB, BT, L])
        NM = sb("neg_max", [P, 2, 2])
        DEN = sb("denominator", [P, 2, 2])
        RD = sb("recip_den", [P, 2, 2])
        S = [ps(f"scores{i}", [P, 2, 512]) for i in range(2)]
        Tp = ps("probs_T_ps", [P, 2, 512])
        Hp = ps("keys_T_ps", [P, 512])
        Zp = ps("values_ps", [P, 512])
        s_ctx = [sem(f"ctx_loaded{i}") for i in range(NB)]
        s_hfull, s_hfree = sem("h_bank_full"), sem("h_bank_free")
        s_zfull, s_zfree = sem("z_bank_full"), sem("z_bank_free")
        s_s, s_max, s_exp, s_rd, s_p = (sem(n) for n in ("scores", "max", "exp", "recip", "probs"))
        s_t, s_pt = sem("probs_T_ps"), sem("probs_T")
        if first:
            Hat = sb("normed_rows", [KC, 4, 3, D])
            Sc = sb("clipped", [P, 2, KEYS])
            stats = sb("stats", [KC, 2, 3, 6])
            mv = sb("mean_var", [KC, 4, 3, 2])
            var = sb("var_eps", [KC, 2, 3])
            rstd = sb("rstd", [KC, 4, 3])
            s_clip, s_bn, s_stats, s_var, s_rstd, s_hat = (
                sem(n) for n in ("clipped", "bn_stats", "mean_var", "var_eps", "rstd", "normed"))
            s_zero = sem("ctx_zeroed")
            s_store = [sem(f"rows_stored{i}") for i in range(4)]
        else:
            s_gain, s_aff = sem("rows_gained"), sem("key_rows")

        def unit(g, j):
            return g * NUB + j

        def batch(g, i):
            return g * NB + i

        def z_before(g, j):
            return g * (ZPG * GB) + j + j // NU

        def o_before(g, grp):
            return g * (ZPG * GB) + grp * ZPG - 1

        def h_kt_before(g, i):
            grp, r = i // BT, i % BT
            skip = min(r, 2) if first else (0, 1, 3, 4)[r]
            if isinstance(g, int) and g * GB + grp == NT - 1:
                skip = 0
            return g * (HPG * GB) + grp * HPG + r + skip + H0

        def h_piece_before(g, grp, n):
            return g * (HPG * GB) + grp * HPG + H0 + n + (n + 1 if first else (n + 1) // 2 + 1)

        def keys_out(g, i):
            if isinstance(g, int) and g * NB + i < LA:
                n = g * NB + i
                return n + 1 if n < 2 else H0
            if i >= LA:
                return h_kt_before(g, i - LA) + 1
            return h_kt_before(g - 1, i - LA + NB) + 1

        def run(eng, body):
            body(0, True, False)
            with eng.Fori(1, TURNS - 1) as g:
                body(g, False, False)
            body(TURNS - 1, False, True)

        def par(j):
            return j % 2

        with nc.Block() as block:

            @block.sync
            def _(sp):
                def load(g, i):
                    n = i % NB
                    b = batch(g, i)
                    if not (isinstance(g, int) and g * NB + i < NB):
                        wait(sp, s_zfull, z_before(g, (i - NB) * UB + UB - 1) + 1)
                    if first:
                        if isinstance(b, int) and b < NB:
                            sp.wait_ge(s_zero, 1)
                        src = dram["ctx"][bass.ds(b, 1), 0:2 * KC, :].rearrange("b (c p) d -> (b p) c d", p=KC)
                        sp.dma_start(Cx[0:KC, n, 0:2, :], src).then_inc(s_ctx[n], 16)
                        src = dram["ctx"][bass.ds(b, 1), 2 * KC:S_CTX, :].rearrange("b p d -> (b p) d")
                        sp.dma_start(Cx[0:KR, n, 2, :], src).then_inc(s_ctx[n], 16)
                    else:
                        src = dram["kv_a"][bass.ds(b, 1), :, :].rearrange("b p (c d) -> (b p) c d", c=2)
                        sp.dma_start(Cx[0:KC, n, 0:2, :], src).then_inc(s_ctx[n], 16)
                        src = dram["kv_b"][bass.ds(b, 1), :, :].rearrange("b p d -> (b p) d")
                        sp.dma_start(Cx[0:KR, n, 2, :], src).then_inc(s_ctx[n], 16)
                        src = dram["kv_lat"][bass.ds(b, 1), :, :].rearrange("b p d -> (b p) d")
                        sp.dma_start(Cx[KR:KR + L, n, 2, :], src).then_inc(s_ctx[n], 16)

                def store(g, i):
                    b = batch(g, i)
                    wait(sp, s_hat, b + 1)
                    sp.dma_start(dram["kv_a"][bass.ds(b, 1), :, :].rearrange("b p (c d) -> (b p) c d", c=2),
                                 Hat[:, i % 4, 0:2, :]).then_inc(s_store[i % 4], 16)
                    sp.dma_start(dram["kv_b"][bass.ds(b, 1), :, :].rearrange("b p d -> (b p) d"),
                                 Hat[0:KR, i % 4, 2, :]).then_inc(s_store[i % 4], 16)

                ahead = 6 if first else 3
                for i in range(ahead):
                    load(0, i)
                if first:
                    for i in range(4):
                        store(0, i)

                def body(g, is_first, is_last):
                    for i in range(NB):
                        if not (is_last and i + ahead >= NB):
                            load(g, i + ahead)
                        if first and not (is_last and i + 4 >= NB):
                            store(g, i + 4)
                run(sp, body)
                if first:
                    for q in s_store:
                        sp.wait_ge(q, 32 * B // 4)

            @block.tensor
            def _(pe):
                def keys_T(g, i, before):
                    wait(pe, s_hat if first else s_aff, batch(g, i) + 1)
                    wait(pe, s_hfree, before)
                    src = Hat[:, i % 4] if first else Cx[:, i % NB]
                    for c in range(3):
                        last = pe.transpose(Hp[:, cols[c]:cols[c] + rows[c]], src[0:rows[c], c, :],
                                            w["ident"][0:rows[c], 0:rows[c]])
                    last.then_inc(s_hfull, 1)

                def fold_q(g, grp, n, before):
                    wait(pe, s_hfree, before)
                    rhs = w["QT"][:, bass.ds((g * GB + grp) * P, P)]
                    for h in range(4):
                        last = pe.matmul(Hp[:, h * P:(h + 1) * P], w["M"][:, 4 * n + h, :], rhs,
                                         start=True, stop=True)
                    last.then_inc(s_hfull, 1)

                def scores(g, j):
                    i = j // UB
                    if j % UB == 0:
                        wait(pe, s_hfree, keys_out(g, i))
                    if j % NU == 0:
                        wait(pe, s_hfree, fold_done(g, j // NU))
                    wait(pe, s_clip if first else s_exp, unit(g, j) - 1)
                    for r in range(2):
                        h0 = 8 * (j % UB) + 4 * r
                        lhsT = QF[:, j // NU % GB, i % BT, h0:h0 + 4, :].rearrange("p h l -> p (h l)")
                        last = pe.matmul(S[par(j)][:, r, 0:KEYS], lhsT, KT[:, i % 2, :], start=True, stop=True)
                    last.then_inc(s_s, 1)

                def fold_done(g, grp):
                    if isinstance(g, int) and g == 0 and grp == 0:
                        return 2 + pieces
                    if grp >= 1:
                        return h_piece_before(g, grp - 1, pieces - 1) + 1
                    return h_piece_before(g - 1, GB - 1, pieces - 1) + 1

                def probs_T(g, j):
                    wait(pe, s_p, unit(g, j) + 1)
                    wait(pe, s_pt, unit(g, j))
                    for r in range(2):
                        for c in range(3):
                            o = c * 256 + r * P
                            last = pe.transpose(Tp[0:rows[c], o // 512, o % 512:o % 512 + P],
                                                Pr[:, par(j), r, cols[c]:cols[c] + rows[c]], w["ident"][:])
                    last.then_inc(s_t, 1)

                def values(g, j):
                    i = j // UB
                    wait(pe, s_pt, unit(g, j) + 1)
                    wait(pe, s_zfree, z_before(g, j))
                    for c in range(3):
                        last = pe.matmul(Zp[:, 0:256], Cx[0:rows[c], i % NB, c, :], PT[0:rows[c], par(j), c, :],
                                         start=(c == 0), stop=(c == 2))
                    last.then_inc(s_zfull, 1)

                def outputs(g, grp):
                    wait(pe, s_zfree, o_before(g, grp))
                    for h in range(8 * UB):
                        lhsT = ZT[:, h].rearrange("p b l -> p (b l)")
                        if first:
                            last = pe.matmul(Zp[:, 16 * h:16 * h + 16], lhsT, w["V"][:, 16 * h:16 * h + 16],
                                             start=True, stop=True)
                        else:
                            last = pe.matmul(Zp[:, 0:D], lhsT, w["V"][:, h, :], start=(h == 0),
                                             stop=(h == 8 * UB - 1))
                    last.then_inc(s_zfull, 1)

                keys_T(0, 0, 0)
                keys_T(0, 1, 1)
                for n in range(pieces):
                    fold_q(0, 0, n, 2 + n)
                scores(0, 0)
                if LA == 3:
                    keys_T(0, 2, 2 + pieces)
                scores(0, 1)

                def body(g, is_first, is_last):
                    for j in range(NUB):
                        grp, r = j // NU, j % NU
                        more_groups = not (is_last and grp == GB - 1)
                        probs_T(g, j)
                        if not (is_last and j + 2 >= NUB):
                            scores(g, j + 2)
                        if j % UB == 0 and not (is_last and j // UB + LA >= NB):
                            keys_T(g, j // UB + LA, h_kt_before(g, j // UB))
                        if r == 1 and not (is_first and grp == 0):
                            outputs(g, grp)
                        piece = r - fold_slot
                        folds = more_groups and 0 <= piece < pieces
                        early = first and piece == pieces - 1
                        if folds and early:
                            fold_q(g, grp + 1, piece, h_piece_before(g, grp, piece))
                        if not (is_first and j == 0):
                            values(g, j - 1)
                        if folds and not early:
                            fold_q(g, grp + 1, piece, h_piece_before(g, grp, piece))
                run(pe, body)
                values(TURNS - 1, NUB - 1)
                outputs(TURNS, 0)

            @block.scalar
            def _(act):
                def keys_T(g, i, before):
                    wait(act, s_hfull, before + 1)
                    wait(act, s_s, unit(g, (i - 2) * UB + UB - 1) + 1)
                    if first:
                        act.activation(KT[:, i % 2, :], Hp[:, 0:KEYS], ACT.Identity, bias=w["pre_b"][:, 0:1],
                                       scale=w["pre_g"][:, 0:1]).then_inc(s_hfree, 1)
                    else:
                        act.activation(KT[:, i % 2, :], Hp[:, 0:KEYS], ACT.Copy).then_inc(s_hfree, 1)

                def fold_q(grp, n, before):
                    wait(act, s_hfull, before + 1)
                    act.activation(QF[:, grp % GB, :, 4 * n:4 * n + 4, :].rearrange("p b h l -> p h b l"),
                                   Hp[:, :].rearrange("p (h b l) -> p h b l", h=4, b=BT), ACT.Copy,
                                   scale=scale).then_inc(s_hfree, 1)

                def exps(g, j):
                    wait(act, s_max, unit(g, j) + 1)
                    wait(act, s_t, unit(g, j) - 1)
                    src = Sc if first else S[par(j)]
                    for r in range(2):
                        last = act.activation(Pr[:, par(j), r, :], src[:, r, 0:KEYS], ACT.Exp,
                                              bias=NM[:, par(j), r:r + 1], accum_out=DEN[:, par(j), r:r + 1])
                    last.then_inc(s_exp, 1)

                def probs_T(g, j):
                    wait(act, s_t, unit(g, j) + 1)
                    wait(act, s_zfull, z_before(g, j - 2) + 1)
                    act.activation(PT[0:KC, par(j)], Tp[0:KC].rearrange("p a (b c) -> p (a b) c", b=2)[:, 0:3, :],
                                   ACT.Copy).then_inc(s_pt, 1)

                def values(g, j):
                    wait(act, s_zfull, z_before(g, j) + 1)
                    h0 = 8 * (j % UB)
                    act.activation(ZT[:, h0:h0 + 8, (j // UB) % BT, :],
                                   Zp[:, 0:256].rearrange("p (h l) -> p h l", h=8), ACT.Copy).then_inc(s_zfree, 1)

                def outputs(g, grp):
                    wait(act, s_zfull, o_before(g, grp) + 1)
                    act.activation(w["O"][:, bass.ds(g * GB + grp - 1, 1), :].rearrange("p a d -> p (a d)"),
                                   Zp[:, 0:D], ACT.Copy).then_inc(s_zfree, 1)

                keys_T(0, 0, 0)
                keys_T(0, 1, 1)
                for n in range(pieces):
                    fold_q(0, n, 2 + n)
                if LA == 3:
                    keys_T(0, 2, 2 + pieces)
                exps(0, 0)
                exps(0, 1)

                def body(g, is_first, is_last):
                    for j in range(NUB):
                        grp, r = j // NU, j % NU
                        more_groups = not (is_last and grp == GB - 1)
                        if first:
                            probs_T(g, j)
                        if j % UB == 0 and not (is_last and j // UB + LA >= NB):
                            keys_T(g, j // UB + LA, h_kt_before(g, j // UB))

                        def exps_ahead():
                            if not (is_last and j + 2 >= NUB):
                                exps(g, j + 2)
                        piece = r - fold_slot
                        folds = more_groups and 0 <= piece < pieces
                        early = first and piece == pieces - 1
                        if r == 1:
                            exps_ahead()
                            if not (is_first and grp == 0):
                                outputs(g, grp)
                        if folds and early:
                            fold_q(grp + 1, piece, h_piece_before(g, grp, piece))
                        if not (is_first and j == 0):
                            values(g, j - 1)
                        if r != 1:
                            exps_ahead()
                        if folds and not early:
                            fold_q(grp + 1, piece, h_piece_before(g, grp, piece))
                run(act, body)
                values(TURNS - 1, NUB - 1)
                outputs(TURNS, 0)

            @block.vector
            def _(dve):
                def row_stats(g, i):
                    dve.wait_ge(s_ctx[i % NB], CTX_DMAS * 16 * (g + i // NB + 1))
                    wait(dve, s_rstd, batch(g, i) - 1)
                    for c in range(3):
                        last = dve.bn_stats(stats[:, i % 2, c, :], Cx[0:KC, i % NB, c, :])
                    last.then_inc(s_bn, 1)

                def row_stats_end(g, i):
                    for c in range(3):
                        last = dve.bn_aggr(mv[:, i % 4, c, :], stats[:, i % 2, c, :])
                    last.then_inc(s_stats, 1)

                def normed(g, i):
                    wait(dve, s_rstd, batch(g, i) + 1)
                    if not (isinstance(g, int) and batch(g, i) < 4):
                        wait(dve, s_hfull, keys_out(g, i - 4))
                        wait(dve, s_store[i % 4], (g * (NB // 4) + i // 4) * 32)
                    for c in range(3):
                        last = dve.tensor_scalar(Hat[:, i % 4, c, :], Cx[0:KC, i % NB, c, :],
                                                 mv[:, i % 4, c, 0:1], rstd[:, i % 4, c:c + 1],
                                                 ALU.subtract, ALU.mult)
                    last.then_inc(s_hat, 1)

                def softmax_max(g, j, bn=None):
                    wait(dve, s_s, unit(g, j) + 1)
                    if first:
                        wait(dve, s_exp, unit(g, j))
                        dve.tensor_scalar(Sc[:], S[par(j)][:, :, 0:KEYS], -10000.0, 10000.0, ALU.max,
                                          ALU.min).then_inc(s_clip, 1)
                        wait(dve, s_clip, unit(g, j) + 1)
                    if bn is not None:
                        wait(dve, s_bn, bn)
                    src = Sc if first else S[par(j)]
                    dve.tensor_reduce(NM[:, par(j), :], src[:, :, 0:KEYS], AX.X, ALU.max,
                                      negate=True).then_inc(s_max, 1)

                def recip(g, j):
                    wait(dve, s_exp, unit(g, j) + 1)
                    wait(dve, s_p, unit(g, j) - 1)
                    dve.reciprocal(RD[:, par(j), :], DEN[:, par(j), :]).then_inc(s_rd, 1)

                def probs_T(g, j):
                    wait(dve, s_t, unit(g, j) + 1)
                    wait(dve, s_zfull, z_before(g, j - 2) + 1)
                    src = Tp[0:KMAX].rearrange("p a (b c) -> p (a b) c", b=2)
                    dve.tensor_copy(PT[0:KC, par(j), 0:2], src[0:KC, 0:2])
                    dve.tensor_copy(PT[0:rows[2], par(j), 2], src[0:rows[2], 2]).then_inc(s_pt, 1)

                if first:
                    dve.memset(Tp[:], 0.0)
                    dve.memset(Cx[:], 0.0).then_inc(s_zero, 1)
                    for i in range(5):
                        row_stats(0, i)
                        dve.wait_ge(s_bn, i + 1)
                        row_stats_end(0, i)
                        if i >= 1:
                            normed(0, i - 1)
                softmax_max(0, 0)
                softmax_max(0, 1)
                recip(0, 0)

                def body(g, is_first, is_last):
                    for j in range(NUB):
                        stats_ahead = first and not (is_last and j + 5 >= NB)
                        if stats_ahead:
                            row_stats(g, j + 5)
                        if not (is_last and j == NUB - 1):
                            recip(g, j + 1)
                        if not first:
                            probs_T(g, j)
                        if not (is_last and j + 2 >= NUB):
                            softmax_max(g, j + 2, batch(g, j + 5) + 1 if stats_ahead else None)
                        if stats_ahead:
                            row_stats_end(g, j + 5)
                        if first and not (is_last and j + 4 >= NB):
                            normed(g, j + 4)
                run(dve, body)

            @block.gpsimd
            def _(pool):
                def norm(g, j):
                    wait(pool, s_rd, unit(g, j) + 1)
                    pool.tensor_tensor(Pr[:, par(j)], Pr[:, par(j)],
                                       RD[:, par(j), :].rearrange("p (r o) -> p r o", o=1).to_broadcast([P, 2, KEYS]),
                                       ALU.mult).then_inc(s_p, 1)

                def rsqrt(g, i):
                    wait(pool, s_stats, batch(g, i) + 1)
                    pool.tensor_tensor(var[:, i % 2], mv[:, i % 4, :, 1], w["eps"][0:KC, 0:3],
                                       ALU.add).then_inc(s_var, 1)
                    wait(pool, s_var, batch(g, i) + 1)
                    wait(pool, s_hat, batch(g, i) - 3)
                    pool.tensor_tensor(rstd[:, i % 4], var[:, i % 2], w["minus_half"][0:KC, 0:3],
                                       ALU.pow).then_inc(s_rstd, 1)

                def key_rows(g, i):
                    n = i % NB
                    pool.wait_ge(s_ctx[n], CTX_DMAS * 16 * (g + i // NB + 1))
                    wide = [w[k][0:KC, :].rearrange("p (o d) -> p o d", o=1).to_broadcast([KC, 2, D])
                            for k in ("ln1_w", "ln1_b")]
                    a, b = Cx[0:KC, n, 0:2, :], Cx[0:KR, n, 2, :]
                    pool.tensor_tensor(a, a, wide[0], ALU.mult).then_inc(s_gain, 1)
                    pool.tensor_tensor(b, b, w["ln1_w"][0:KR, :], ALU.mult).then_inc(s_gain, 1)
                    wait(pool, s_gain, 2 * batch(g, i) + 2)
                    pool.tensor_tensor(a, a, wide[1], ALU.add)
                    pool.tensor_tensor(b, b, w["ln1_b"][0:KR, :], ALU.add).then_inc(s_aff, 1)

                if first:
                    for i in range(5):
                        rsqrt(0, i)
                else:
                    for i in range(3):
                        key_rows(0, i)
                norm(0, 0)

                def body(g, is_first, is_last):
                    for j in range(NUB):
                        if not (is_last and j == NUB - 1):
                            norm(g, j + 1)
                        if first and not (is_last and j + 5 >= NB):
                            rsqrt(g, j + 5)
                        if not first and j % UB == 1 and not (is_last and j // UB + 3 >= NB):
                            key_rows(g, j // UB + 3)
                run(pool, body)


Q = 4
TQ = NT // Q
NQ = T // Q


def spread(ap, n):
    return ap.rearrange("p (n o) -> p n o", o=1).to_broadcast([ap.shape[0], n, D])


def norm_buffers(sb, sem, name):
    n = {"stats": sb(f"{name}_stats", [P, NT, 6]), "mv": sb(f"{name}_mean_var", [P, NT, 2]),
         "var": sb(f"{name}_var_eps", [P, NT]), "rstd": sb(f"{name}_rstd", [P, NT])}
    for k in ("s_bn", "s_stats", "s_var", "s_rstd"):
        n[k] = sem(f"{name}{k[1:]}")
    return n


def norm_measure(dve, n, src, q):
    for t in range(q * TQ, q * TQ + TQ):
        last = dve.bn_stats(n["stats"][:, t, :], src[:, t, :])
    last.then_inc(n["s_bn"], 1)
    dve.wait_ge(n["s_bn"], q + 1)
    for t in range(q * TQ, q * TQ + TQ):
        last = dve.bn_aggr(n["mv"][:, t, :], n["stats"][:, t, :])
    last.then_inc(n["s_stats"], 1)


def norm_rsqrt(pool, n, w, q):
    a, b = q * TQ, q * TQ + TQ
    pool.wait_ge(n["s_stats"], q + 1)
    pool.tensor_tensor(n["var"][:, a:b], n["mv"][:, a:b, 1], w["eps"][:, 0:TQ], ALU.add).then_inc(n["s_var"], 1)
    pool.wait_ge(n["s_var"], q + 1)
    pool.tensor_tensor(n["rstd"][:, a:b], n["var"][:, a:b], w["minus_half"][:, 0:TQ],
                       ALU.pow).then_inc(n["s_rstd"], 1)


def norm_apply(dve, n, src, dst, q):
    dve.wait_ge(n["s_rstd"], q + 1)
    for t in range(q * TQ, q * TQ + TQ):
        last = dve.tensor_scalar(dst[:, t, :], src[:, t, :], n["mv"][:, t, 0:1], n["rstd"][:, t:t + 1],
                                 ALU.subtract, ALU.mult)
    return last


def norm_stage(nc, w, tag, src, rows, dst_T, gain=None, shift=None, twice=False, add=None, row_affine=None,
               rows_out=None, rows_T=None):
    with ExitStack() as ctx:
        sb, ps, sem = place(nc, ctx, tag)
        norms = [norm_buffers(sb, sem, f"n{i}") for i in range(2 if twice else 1)]
        bank = ps("rows_T_ps", [P, Q, NQ])
        s_add, s_mid, s_rows, s_T, s_out, s_gain, s_aff, s_st = (
            sem(n) for n in ("added", "normed_once", "normed", "transposed", "out", "gained", "affine", "stored"))
        with nc.Block() as block:
            @block.vector
            def _(dve):
                for q in range(Q):
                    a, b = q * TQ, q * TQ + TQ
                    if add is not None:
                        dve.tensor_tensor(src[:, a:b, :], src[:, a:b, :], add[:, a:b, :], ALU.add).then_inc(s_add, 1)
                        dve.wait_ge(s_add, q + 1)
                    norm_measure(dve, norms[0], src, q)
                for q in range(Q):
                    last = norm_apply(dve, norms[0], src, rows, q)
                    last.then_inc(s_mid if twice else s_rows, 1)
                if twice:
                    for q in range(Q):
                        dve.wait_ge(s_mid, q + 1)
                        norm_measure(dve, norms[1], rows, q)
                    for q in range(Q):
                        norm_apply(dve, norms[1], rows, rows, q).then_inc(s_rows, 1)

            @block.gpsimd
            def _(pool):
                for n in norms:
                    for q in range(Q):
                        norm_rsqrt(pool, n, w, q)
                if row_affine is not None:
                    g3, b3 = (x[:, :].rearrange("p (o d) -> p o d", o=1).to_broadcast([P, TQ, D]) for x in row_affine)
                    for q in range(Q):
                        a, b = q * TQ, q * TQ + TQ
                        pool.wait_ge(s_rows, q + 1)
                        pool.tensor_tensor(rows_out[:, a:b, :], rows[:, a:b, :], g3, ALU.mult).then_inc(s_gain, 1)
                        pool.wait_ge(s_gain, q + 1)
                        pool.tensor_tensor(rows_out[:, a:b, :], rows_out[:, a:b, :], b3, ALU.add).then_inc(s_aff, 1)

            @block.tensor
            def _(pe):
                for q in range(Q):
                    pe.wait_ge(s_rows, q + 1)
                    for i in range(TQ):
                        last = pe.transpose(bank[:, q, i * P:(i + 1) * P], rows[:, q * TQ + i, :], w["ident"][:])
                    last.then_inc(s_T, 1)

            @block.scalar
            def _(act):
                for q in range(Q):
                    act.wait_ge(s_T, q + 1)
                    if gain is None:
                        act.activation(dst_T[:, q * NQ:(q + 1) * NQ], bank[:, q, :], ACT.Copy)
                    else:
                        act.activation(dst_T[:, q * NQ:(q + 1) * NQ], bank[:, q, :], ACT.Identity,
                                       bias=shift[:, 0:1], scale=gain[:, 0:1])

            if rows_T is not None:
                @block.sync
                def _(sp):
                    for q in range(Q):
                        sp.wait_ge(s_aff, q + 1)
                        sp.dma_start(rows_T[q * TQ:(q + 1) * TQ, :, :].rearrange("t p d -> p t d"),
                                     rows_out[:, q * TQ:(q + 1) * TQ, :]).then_inc(s_st, 16)
                    sp.wait_ge(s_st, 16 * Q)


def gelu_stage(nc, w):
    with ExitStack() as ctx:
        sb, ps, sem = place(nc, ctx, "g0")
        G = sb("gelu", [P, NT, D])
        bank = ps("proj", [P, Q, NQ])
        s_mm, s_gelu, s_add = sem("proj"), sem("gelu"), sem("added")
        with nc.Block() as block:
            @block.tensor
            def _(pe):
                for q in range(Q):
                    for i in range(TQ):
                        t = q * TQ + i
                        last = pe.matmul(bank[:, q, i * D:(i + 1) * D], w["QT"][:, t * P:(t + 1) * P], w["Wo0"][:],
                                         start=True, stop=True)
                    last.then_inc(s_mm, 1)

            @block.scalar
            def _(act):
                for q in range(Q):
                    act.wait_ge(s_mm, q + 1)
                    act.activation(G[:, q * TQ:(q + 1) * TQ, :].rearrange("p t d -> p (t d)"), bank[:, q, :],
                                   ACT.Gelu).then_inc(s_gelu, 1)

            @block.vector
            def _(dve):
                for q in range(Q):
                    x = w["X"][:, q * TQ:(q + 1) * TQ, :]
                    dve.tensor_tensor(x, x, w["N"][:, q * TQ:(q + 1) * TQ, :], ALU.add).then_inc(s_add, 1)
                for q in range(Q):
                    x = w["X"][:, q * TQ:(q + 1) * TQ, :]
                    dve.wait_ge(s_gelu, q + 1)
                    dve.wait_ge(s_add, q + 1)
                    dve.tensor_tensor(x, x, G[:, q * TQ:(q + 1) * TQ, :], ALU.add)


def self_attention_stage(nc, w, ins):
    with ExitStack() as ctx:
        sb, ps, sem = place(nc, ctx, "sa")
        W = sb("weights_T", [D, 3, D])
        qk = sb("qk_T", [D, 2, T])
        V = sb("v_rows", [P, NT, D])
        A = sb("probs", [P, NT, L])
        AT = sb("probs_T", [P, NT, L])
        BD = sb("probs_diagonal", [P, NT, P])
        M = sb("max", [P, NT])
        den = sb("den", [P, NT])
        rden = sb("recip_den", [P, NT])
        bank = ps("proj", [P, 4, NQ])
        Sb = ps("scores", [P, NT, L])
        s_w, s_mm, s_out, s_s, s_dve, s_exp, s_mask, s_bd, s_o = (
            sem(n) for n in ("weights", "proj_ps", "proj", "scores", "chain", "exp", "masked", "diagonal", "out_ps"))
        with nc.Block() as block:
            @block.sync
            def _(sp):
                for n, name in enumerate(("L0_attn_wqT", "L0_attn_wkT", "L0_attn_wvT")):
                    sp.dma_start(W[:, n, :], ins[name]).then_inc(s_w, 16)

            @block.tensor
            def _(pe):
                pe.wait_ge(s_w, 48)
                n = 0
                for m in range(2):
                    for q in range(Q):
                        if n >= 4:
                            pe.wait_ge(s_out, n - 3)
                        pe.matmul(bank[:, n % 4, :], W[:, m, :], w["QT"][:, q * NQ:(q + 1) * NQ], start=True,
                                  stop=True).then_inc(s_mm, 1)
                        n += 1
                for q in range(Q):
                    pe.wait_ge(s_out, n - 3)
                    for i in range(TQ):
                        t = q * TQ + i
                        last = pe.matmul(bank[:, n % 4, i * D:(i + 1) * D], w["QT"][:, t * P:(t + 1) * P], W[:, 2, :],
                                         start=True, stop=True)
                    last.then_inc(s_mm, 1)
                    n += 1
                for b in range(B):
                    c = slice(b * L, (b + 1) * L)
                    o = (b % BT) * L
                    last = pe.matmul(Sb[o:o + L, b // BT, :], qk[:, 1, c], qk[:, 0, c], start=True, stop=True)
                last.then_inc(s_s, 1)
                pe.wait_ge(s_out, 12)
                pe.wait_ge(s_bd, 1)
                for q in range(Q):
                    for i in range(TQ):
                        t = q * TQ + i
                        last = pe.matmul(bank[:, q, i * D:(i + 1) * D], BD[:, t, :], V[:, t, :], start=True, stop=True)
                    last.then_inc(s_o, 1)

            @block.scalar
            def _(act):
                for n in range(12):
                    act.wait_ge(s_mm, n + 1)
                    q = n % Q
                    dst = qk[:, n // Q, q * NQ:(q + 1) * NQ] if n < 8 else V[:, q * TQ:(q + 1) * TQ, :].rearrange(
                        "p t d -> p (t d)")
                    act.activation(dst, bank[:, n % 4, :], ACT.Copy).then_inc(s_out, 1)
                act.wait_ge(s_dve, 3)
                act.activation(A[:], A[:], ACT.Exp, scale=float(D) ** -0.5).then_inc(s_exp, 1)

            @block.gpsimd
            def _(pool):
                pool.wait_ge(s_dve, 6)
                for j in range(BT):
                    a = A[j * L:(j + 1) * L]
                    last = pool.affine_select(out=a, in_=a, compare_op=ALU.is_ge, fill=0.0, base=0,
                                              pattern=[[0, NT], [-1, L]], channel_multiplier=1)
                last.then_inc(s_mask, 1)

            @block.vector
            def _(dve):
                link = chain(dve, s_dve)
                link(dve.memset(BD[:], 0.0))
                dve.wait_ge(s_s, 1)
                link(dve.tensor_reduce(M[:], Sb[:], AX.X, ALU.max))
                over = lambda v: v[:, :].rearrange("p (t o) -> p t o", o=1).to_broadcast([P, NT, L])
                link(dve.tensor_tensor(A[:], Sb[:], over(M), ALU.subtract))
                dve.wait_ge(s_exp, 1)
                link(dve.tensor_reduce(den[:], A[:], AX.X, ALU.add))
                link(dve.reciprocal(rden[:], den[:]))
                link(dve.tensor_tensor(A[:], A[:], over(rden), ALU.mult))
                dve.wait_ge(s_mask, 1)
                link(dve.transpose(AT[:, :, :].rearrange("p t l -> p (t l)"), A[:, :, :].rearrange("p t l -> p (t l)")))
                for j in range(BT):
                    r = slice(j * L, (j + 1) * L)
                    last = dve.tensor_copy(BD[r, :, r], AT[r, :, :])
                last.then_inc(s_bd, 1)
                for q in range(Q):
                    dve.wait_ge(s_o, q + 1)
                    x = w["X"][:, q * TQ:(q + 1) * TQ, :]
                    dve.tensor_tensor(x, bank[:, q, :].rearrange("p (t d) -> p t d", d=D), x, ALU.add)


def moe_stage(nc, w, ins, layer):
    E, FF = 8, 4 * D
    FC = FF // P
    tag = f"moe{layer}"
    gated = layer == 1
    UN = E * Q
    with ExitStack() as ctx:
        sb, ps, sem = place(nc, ctx, tag)
        R = sb("router_T", [D, E])
        W1 = sb("w_in_T", [D, 2, 2 if gated else 1, FF])
        W2 = sb("w_out_T", [P, 2, FC, D])
        Hd = sb("hidden_T", [P, 2, FC, NQ])
        Rl = sb("relu", [P, 2, NQ]) if gated else None
        pr = sb("probs", [P, NT, E])
        gt = sb("greater", [P, NT, E, E])
        eq = sb("equal", [P, NT, E, E])
        low = sb("lower", [P, E, E])
        mx, den, rden = (sb(n, [P, NT]) for n in ("max", "den", "recip_den"))
        rank = sb("rank", [P, NT, E])
        Wt = sb("weights", [P, NT, E])
        We = sb("weights_e", [P, 2, NT])
        Hb = [ps(f"hidden_ps{i}", [P, NQ]) for i in range(4)]
        Yb = [ps(f"out_ps{i}", [P, NQ]) for i in range(2)]
        Rb = ps("router_ps", [P, NT, E])
        s_r, s_rm, s_dve, s_exp, s_low = (sem(n) for n in ("router", "logits", "chain", "exp", "lower"))
        s_w = [sem(f"weights{i}") for i in range(2)]
        s_h, s_act, s_y, s_x, s_we, s_relu = (
            sem(n) for n in ("hidden_ps", "hidden", "out_ps", "added", "weights_e", "relu"))

        with nc.Block() as block:
            @block.sync
            def _(sp):
                sp.dma_start(R[:], ins[f"{tag}_router_T"]).then_inc(s_r, 16)

                def load(e, par):
                    if not isinstance(e, int) or e >= 2:
                        sp.wait_ge(s_y, (e - 1) * Q)
                    for n in range(2 if gated else 1):
                        src = ins[f"{tag}_w_in_T"][bass.ds(e * (2 if gated else 1) + n, 1), :, :].rearrange("e d f -> (e d) f")
                        sp.dma_start(W1[:, par, n, :], src).then_inc(s_w[par], 16)
                    src = ins[f"{tag}_w_out_T"][bass.ds(e, 1), :, :].rearrange("e (c p) d -> p (e c) d", p=P)
                    sp.dma_start(W2[:, par], src).then_inc(s_w[par], 16)
                load(0, 0)
                load(1, 1)
                with sp.Fori(1, E // 2) as i:
                    load(i * 2, 0)
                    load(i * 2 + 1, 1)

            WD = 16 * (3 if gated else 2)

            @block.tensor
            def _(pe):
                pe.wait_ge(s_r, 16)
                for t in range(NT):
                    last = pe.matmul(Rb[:, t, :], w["QT"][:, t * P:(t + 1) * P], R[:], start=True, stop=True)
                last.then_inc(s_rm, 1)

                def hidden(i, j):
                    i, j = i + j // (2 * Q), j % (2 * Q)
                    par, q = j // Q, j % Q
                    u = i * 2 * Q + j
                    if q == 0:
                        pe.wait_ge(s_w[par], (i + 1) * WD)
                    for c in range(FC):
                        n = u * FC + c
                        if not gated:
                            wait(pe, s_act, n - 3)
                            pe.matmul(Hb[c][:], W1[:, par, 0, c * P:(c + 1) * P], w["QT"][:, q * NQ:(q + 1) * NQ],
                                      start=True, stop=True).then_inc(s_h, 1)
                        else:
                            wait(pe, s_act, n - 1)
                            for k in range(2):
                                last = pe.matmul(Hb[2 * (c % 2) + k][:], W1[:, par, k, c * P:(c + 1) * P],
                                                 w["QT"][:, q * NQ:(q + 1) * NQ], start=True, stop=True)
                            last.then_inc(s_h, 1)

                def output(i, j):
                    par, q = j // Q, j % Q
                    u = i * 2 * Q + j
                    wait(pe, s_act, (u + 1) * FC)
                    wait(pe, s_x, u - 1)
                    for t in range(TQ):
                        for c in range(FC):
                            last = pe.matmul(Yb[j % 2][:, t * D:(t + 1) * D], Hd[:, j % 2, c, t * P:(t + 1) * P],
                                             W2[:, par, c, :], start=(c == 0), stop=(c == FC - 1))
                    last.then_inc(s_y, 1)

                hidden(0, 0)

                def body(i, is_last=False):
                    for j in range(2 * Q):
                        if not (is_last and j == 2 * Q - 1):
                            hidden(i, j + 1)
                        output(i, j)
                body(0)
                with pe.Fori(1, E // 2 - 1) as i:
                    body(i)
                body(E // 2 - 1, True)

            @block.scalar
            def _(act):
                act.wait_ge(s_dve, 2)
                act.activation(pr[:], pr[:], ACT.Exp).then_inc(s_exp, 1)

                def body(i):
                    for j in range(2 * Q):
                        u = i * 2 * Q + j
                        for c in range(FC):
                            n = u * FC + c
                            act.wait_ge(s_h, n + 1)
                            if gated:
                                wait(act, s_act, n - 1)
                                act.activation(Rl[:, c % 2, :], Hb[2 * (c % 2)][:], ACT.Relu).then_inc(s_relu, 1)
                            else:
                                wait(act, s_y, u - 1)
                                act.activation(Hd[:, j % 2, c, :], Hb[c][:], ACT.Gelu).then_inc(s_act, 1)
                body(0)
                with act.Fori(1, E // 2) as i:
                    body(i)

            @block.gpsimd
            def _(pool):
                pool.memset(low[:], 1.0).then_inc(s_low, 1)
                pool.wait_ge(s_low, 1)
                pool.affine_select(out=low[:], in_=low[:], compare_op=ALU.is_gt, fill=0.0, base=0,
                                   pattern=[[1, E], [-1, E]], channel_multiplier=0).then_inc(s_low, 1)

            @block.vector
            def _(dve):
                link = chain(dve, s_dve)
                over = lambda v: v[:, :].rearrange("p (t o) -> p t o", o=1).to_broadcast([P, NT, E])
                dve.wait_ge(s_rm, 1)
                link(dve.tensor_reduce(mx[:], Rb[:], AX.X, ALU.max))
                link(dve.tensor_tensor(pr[:], Rb[:], over(mx), ALU.subtract))
                dve.wait_ge(s_exp, 1)
                link(dve.tensor_reduce(den[:], pr[:], AX.X, ALU.add))
                link(dve.reciprocal(rden[:], den[:]))
                link(dve.tensor_tensor(pr[:], pr[:], over(rden), ALU.mult))
                mine = pr[:, :, :].rearrange("p t (e o) -> p t e o", o=1).to_broadcast([P, NT, E, E])
                other = pr[:, :, :].rearrange("p t (o j) -> p t o j", o=1).to_broadcast([P, NT, E, E])
                dve.tensor_tensor(gt[:], other, mine, ALU.is_gt)
                link(dve.tensor_tensor(eq[:], other, mine, ALU.is_equal))
                dve.wait_ge(s_low, 2)
                link(dve.tensor_tensor(eq[:], eq[:], low[:, :, :].rearrange("p (o e) j -> p o e j", o=1).to_broadcast(
                    [P, NT, E, E]), ALU.mult))
                link(dve.tensor_tensor(gt[:], gt[:], eq[:], ALU.add))
                link(dve.tensor_reduce(rank[:], gt[:], AX.X, ALU.add))
                link(dve.scalar_tensor_tensor(out=Wt[:], in0=rank[:], scalar=1.5, in1=pr[:], op0=ALU.is_lt,
                                              op1=ALU.mult))
                if gated:
                    link(dve.tensor_reduce(den[:], Wt[:], AX.X, ALU.add))
                    link(dve.tensor_scalar(den[:], den[:], float(np.finfo(np.float32).eps), None, ALU.add))
                    link(dve.reciprocal(rden[:], den[:]))
                    link(dve.tensor_tensor(Wt[:], Wt[:], over(rden), ALU.mult))

                def gate(i, j):
                    u = i * 2 * Q + j
                    for c in range(FC):
                        n = u * FC + c
                        dve.wait_ge(s_relu, n + 1)
                        wait(dve, s_y, u - 1)
                        dve.tensor_tensor(Hd[:, j % 2, c, :], Hb[2 * (c % 2) + 1][:], Rl[:, c % 2, :],
                                          ALU.mult).then_inc(s_act, 1)

                def add(i, j):
                    par, q = j // Q, j % Q
                    u = i * 2 * Q + j
                    if q == 0:
                        dve.tensor_copy(We[:, par, :], Wt[:, :, bass.ds(i * 2 + par, 1)].rearrange(
                            "p t o -> p (t o)")).then_inc(s_we, 1)
                        dve.wait_ge(s_we, i * 2 + par + 1)
                    dve.wait_ge(s_y, u + 1)
                    for t in range(TQ):
                        n = q * TQ + t
                        last = dve.scalar_tensor_tensor(
                            out=w["X"][:, n, :], in0=Yb[j % 2][:, t * D:(t + 1) * D],
                            scalar=We[:, par, n:n + 1], in1=w["X"][:, n, :], op0=ALU.mult, op1=ALU.add)
                    last.then_inc(s_x, 1)

                if gated:
                    gate(0, 0)

                def body(i, is_last=False):
                    for j in range(2 * Q):
                        if gated and not (is_last and j == 2 * Q - 1):
                            gate(i + (j + 1) // (2 * Q), (j + 1) % (2 * Q))
                        add(i, j)
                body(0)
                with dve.Fori(1, E // 2 - 1) as i:
                    body(i)
                body(E // 2 - 1, True)


DI = 2 * D
NS = 16
RANK = 64
FD = 4 * D
BLK = 1024
ROUND = 1.5 * 2.0 ** 23


def ssm_in_stage(nc, w, ins, v):
    with ExitStack() as ctx:
        sb, ps, sem = place(nc, ctx, "si")
        W = sb("in_T", [D, 2 * DI])
        WX = sb("x_T", [P, 2, RANK + 2 * NS])
        WD = sb("dt_T", [RANK, DI])
        cw = sb("conv_w", [P, 2, 4])
        cb = sb("conv_b", [P, 2])
        db = sb("dt_b", [P, 2])
        XD = sb("x_dbl", [RANK + 2 * NS, T])
        pre = v["delta"]
        z = v["du"]
        neg = sb("neg_abs", [P, 2, T])
        tiny = sb("tiny", [P, T])
        mask = sb("mask", [P, T], mybir.dt.uint8)
        bank = ps("proj", [P, 4, NQ])
        xb = ps("x_ps", [P, 2, NQ])
        zb = ps("z_ps", [P, 2, NQ])
        s_w, s_mm, s_out, s_dve, s_conv, s_u, s_xm, s_xd, s_zm, s_z, s_neg, s_e, s_ln, s_a, s_sp = (
            sem(n) for n in ("weights", "proj_ps", "proj", "chain", "conv", "u", "x_ps", "x_dbl", "z_ps", "z",
                               "neg_abs", "exp", "ln", "a", "softplus"))
        s_split, s_sel, s_p = sem("split"), sem("selector"), sem("pool")
        with nc.Block() as block:
            @block.sync
            def _(sp):
                sp.dma_start(W[:], ins["in_proj_T"]).then_inc(s_w, 16)
                sp.dma_start(WX[:], ins["x_proj_T"].rearrange("(h p) n -> p h n", p=P)).then_inc(s_w, 16)
                sp.dma_start(WD[:], ins["dt_proj_T"]).then_inc(s_w, 16)
                sp.dma_start(cw[:], ins["conv_w"].rearrange("(h p) n -> p h n", p=P)).then_inc(s_w, 16)
                with nc.allow_non_contiguous_dma(reason="one value per partition"):
                    sp.dma_start(cb[:], ins["conv_b"].rearrange("(h p) -> p h", p=P)).then_inc(s_w, 16)
                    sp.dma_start(db[:], ins["dt_proj_b"].rearrange("(h p) -> p h", p=P)).then_inc(s_w, 16)
                    sp.dma_start(v["D"][:], ins["D"].rearrange("(h p) -> p h", p=P)).then_inc(s_w, 16)
                sp.dma_start(v["a"][:], ins["A_log"].rearrange("(h p) n -> p h n", p=P)).then_inc(s_w, 16)
                sp.wait_ge(s_w, 128)

            @block.tensor
            def _(pe):
                pe.wait_ge(s_w, 128)
                for q in range(Q):
                    for m in range(4):
                        if q >= 1:
                            pe.wait_ge(s_out, 4 * (q - 1) + m + 1)
                        pe.matmul(bank[:, m, :], W[:, m * P:(m + 1) * P], w["QT"][:, q * NQ:(q + 1) * NQ],
                                  start=True, stop=True).then_inc(s_mm, 1)
                for q in range(Q):
                    c = slice(q * NQ, (q + 1) * NQ)
                    pe.wait_ge(s_u, 2)
                    if q >= 2:
                        pe.wait_ge(s_xd, q - 1)
                    for h in range(2):
                        last = pe.matmul(xb[0:RANK + 2 * NS, q % 2, :], WX[:, h, :], v["u"][:, h, c], start=(h == 0),
                                         stop=(h == 1))
                    last.then_inc(s_xm, 1)
                for q in range(Q):
                    c = slice(q * NQ, (q + 1) * NQ)
                    pe.wait_ge(s_xd, q + 1)
                    for h in range(2):
                        n = 2 * q + h
                        if n >= 2:
                            pe.wait_ge(s_z, n - 1)
                        pe.matmul(zb[:, h, :], WD[:, h * P:(h + 1) * P], XD[0:RANK, c], start=True,
                                  stop=True).then_inc(s_zm, 1)

            @block.scalar
            def _(act):
                for q in range(Q):
                    c = slice(q * NQ, (q + 1) * NQ)
                    for m in range(4):
                        act.wait_ge(s_mm, 4 * q + m + 1)
                        if m < 2:
                            act.activation(pre[:, m, c], bank[:, m, :], ACT.Copy).then_inc(s_out, 1)
                        else:
                            act.activation(v["gate"][:, m - 2, c], bank[:, m, :], ACT.Silu).then_inc(s_out, 1)
                for h in range(2):
                    act.wait_ge(s_conv, h + 1)
                    act.activation(v["u"][:, h, :], v["u"][:, h, :], ACT.Silu).then_inc(s_u, 1)
                for q in range(Q):
                    c = slice(q * NQ, (q + 1) * NQ)
                    act.wait_ge(s_xm, q + 1)
                    act.activation(XD[:, c], xb[0:RANK + 2 * NS, q % 2, :], ACT.Copy).then_inc(s_xd, 1)
                for q in range(Q):
                    c = slice(q * NQ, (q + 1) * NQ)
                    for h in range(2):
                        act.wait_ge(s_zm, 2 * q + h + 1)
                        act.activation(z[:, h, c], zb[:, h, :], ACT.Identity, bias=db[:, h:h + 1]).then_inc(s_z, 1)
                act.activation(v["a"][:], v["a"][:], ACT.Exp).then_inc(s_a, 1)
                for h in range(2):
                    act.wait_ge(s_neg, h + 1)
                    act.activation(neg[:, h, :], neg[:, h, :], ACT.Exp).then_inc(s_e, 1)
                for h in range(2):
                    act.wait_ge(s_e, h + 1)
                    act.activation(v["delta"][:, h, :], neg[:, h, :], ACT.Ln, bias=1.0).then_inc(s_ln, 1)

            @block.gpsimd
            def _(pool):
                sel = v["sel32"]
                pool.memset(sel[:], 0.0).then_inc(s_p, 1)
                pool.wait_ge(s_p, 1)
                for o in (64, 96):
                    s = sel[o:o + 2 * NS]
                    last = pool.affine_select(out=s, in_=s, compare_op=ALU.not_equal, fill=1.0, base=0,
                                              pattern=[[-1, 2 * NS], [0, P]], channel_multiplier=1)
                last.then_inc(s_sel, 1)

            @block.vector
            def _(dve):
                link = chain(dve, s_dve)
                dve.wait_ge(s_out, 16)
                dve.wait_ge(s_w, 128)
                u3 = [v["u"][:, h, :].rearrange("p (b l) -> p b l", l=L) for h in range(2)]
                x3 = [pre[:, h, :].rearrange("p (b l) -> p b l", l=L) for h in range(2)]
                for h in range(2):
                    link(dve.tensor_scalar(v["u"][:, h, :], pre[:, h, :], cw[:, h, 3:4], cb[:, h:h + 1], ALU.mult,
                                           ALU.add))
                    for s in range(1, 4):
                        last = dve.scalar_tensor_tensor(out=u3[h][:, :, s:], in0=x3[h][:, :, :L - s],
                                                        scalar=cw[:, h, 3 - s:4 - s], in1=u3[h][:, :, s:],
                                                        op0=ALU.mult, op1=ALU.add)
                        if s < 3:
                            link(last)
                    last.then_inc(s_conv, 1)
                dve.wait_ge(s_a, 1)
                link(dve.tensor_scalar(v["a"][:], v["a"][:], -1.0, None, ALU.mult))
                dve.wait_ge(s_sel, 1)
                link(dve.tensor_copy(v["sel"][64:128], v["sel32"][64:128]))
                dve.wait_ge(s_xd, Q)
                hi, lo = v["bc"][64:96, :], v["bc"][96:128, :]
                link(dve.tensor_copy(hi, XD[64:96, :]))
                dve.tensor_tensor(lo, XD[64:96, :], hi.bitcast(F32), ALU.subtract)
                dve.wait_ge(s_z, 2 * Q)
                for h in range(2):
                    dve.scalar_tensor_tensor(out=neg[:, h, :], in0=z[:, h, :], scalar=-1.0, in1=z[:, h, :],
                                             op0=ALU.mult, op1=ALU.min).then_inc(s_neg, 1)
                for h in range(2):
                    e = neg[:, h, :]
                    dve.wait_ge(s_e, h + 1)
                    dve.tensor_scalar(mask[:], e, 1.0 / 32, None, ALU.is_lt)
                    link(dve.tensor_scalar(tiny[:], e, -0.25, 1.0 / 3, ALU.mult, ALU.add))
                    link(dve.tensor_tensor(tiny[:], tiny[:], e, ALU.mult))
                    link(dve.scalar_tensor_tensor(out=tiny[:], in0=tiny[:], scalar=-0.5, in1=e, op0=ALU.add,
                                                  op1=ALU.mult))
                    link(dve.scalar_tensor_tensor(out=tiny[:], in0=tiny[:], scalar=1.0, in1=e, op0=ALU.add,
                                                  op1=ALU.mult))
                    dve.wait_ge(s_ln, h + 1)
                    link(dve.copy_predicated(v["delta"][:, h, :], mask[:], tiny[:]))
                    link(dve.scalar_tensor_tensor(out=v["delta"][:, h, :], in0=z[:, h, :], scalar=0.0,
                                                  in1=v["delta"][:, h, :], op0=ALU.max, op1=ALU.add))
                    link(dve.tensor_tensor(v["du"][:, h, :], v["delta"][:, h, :], v["u"][:, h, :], ALU.mult))


def ssm_scan_stage(nc, w, v):
    NBK = T // BLK
    NBB = BLK // L
    with ExitStack() as ctx:
        sb, ps, sem = place(nc, ctx, "ss")
        bs = w["O"][:, :, :].rearrange("p (a t) d -> p a (t d)", a=2)
        cs = w["N"][:, :, :].rearrange("p (a t) d -> p a (t d)", a=2)
        dA = sb("decay", [P, 2, 2, BLK])
        dB = sb("drive", [P, 2, 2, BLK])
        H = sb("states", [P, 2, 2, BLK])
        HC = sb("states_c", [P, 2, 2, BLK])
        Bp = ps("b_ps", [P, BLK])
        Cp = ps("c_ps", [P, BLK])
        Yp = [ps(f"y_ps{h}", [P, BLK]) for h in range(2)]
        s_bm, s_cm, s_b, s_c, s_da, s_db, s_h, s_hc, s_y, s_yu, s_yg, s_z = (
            sem(n) for n in ("b_ps", "c_ps", "b_spread", "c_spread", "decay", "drive", "states", "states_c",
                               "y_ps", "y_u", "y_gated", "decay_zero"))
        steps = [(k, n) for k in range(NBK) for n in range(NS)]
        with nc.Block() as block:
            @block.tensor
            def _(pe):
                def spread_bc(i):
                    k, n = steps[i]
                    for dst, row, full, out in ((Bp, n, s_bm, s_b), (Cp, NS + n, s_cm, s_c)):
                        wait(pe, out, i)
                        for c in range(BLK // 512):
                            cols = slice(k * BLK + c * 512, k * BLK + (c + 1) * 512)
                            last = pe.matmul(dst[:, c * 512:(c + 1) * 512], v["sel"][64:128, row, :],
                                             v["bc"][64:128, cols], start=True, stop=True)
                        last.then_inc(full, 1)

                def add_up(i):
                    k, n = steps[i]
                    if n == 0 and k > 0:
                        pe.wait_ge(s_yu, 2 * k)
                    for h in range(2):
                        pe.wait_ge(s_hc, 2 * i + h + 1)
                        for c in range(BLK // 512):
                            last = pe.matmul(Yp[h][:, c * 512:(c + 1) * 512], w["ident"][:],
                                             HC[:, i % 2, h, c * 512:(c + 1) * 512], start=(n == 0), stop=(n == NS - 1))
                        last.then_inc(s_y, 1)
                spread_bc(0)
                for i in range(len(steps)):
                    if i + 1 < len(steps):
                        spread_bc(i + 1)
                    add_up(i)

            @block.scalar
            def _(act):
                act.wait_ge(s_z, 1)
                for i, (k, n) in enumerate(steps):
                    act.wait_ge(s_bm, i + 1)
                    wait(act, s_db, 2 * i - 2)
                    act.activation(bs[:, i % 2, :], Bp[:], ACT.Copy).then_inc(s_b, 1)
                    for h in range(2):
                        wait(act, s_h, 2 * (i - 2) + h + 1)
                        act.activation(dA[:, i % 2, h, :].rearrange("p (b l) -> p b l", l=L)[:, :, 1:],
                                       v["delta"][:, h, k * BLK:(k + 1) * BLK].rearrange("p (b l) -> p b l", l=L)[:, :, 1:],
                                       ACT.Exp, scale=v["a"][:, h, n:n + 1]).then_inc(s_da, 1)
                    act.wait_ge(s_cm, i + 1)
                    wait(act, s_hc, 2 * i - 2)
                    act.activation(cs[:, i % 2, :], Cp[:], ACT.Copy).then_inc(s_c, 1)

            @block.vector
            def _(dve):
                dve.memset(dA[:], 0.0).then_inc(s_z, 1)

                def finish(k):
                    dve.wait_ge(s_y, 2 * NS * (k + 1))
                    c = slice(k * BLK, (k + 1) * BLK)
                    for h in range(2):
                        dve.scalar_tensor_tensor(out=v["du"][:, h, c], in0=v["u"][:, h, c], scalar=v["D"][:, h:h + 1],
                                                 in1=Yp[h][:], op0=ALU.mult, op1=ALU.add).then_inc(s_yu, 1)
                    dve.wait_ge(s_yu, 2 * (k + 1))
                    for h in range(2):
                        dve.tensor_tensor(v["du"][:, h, c], v["du"][:, h, c], v["gate"][:, h, c], ALU.mult)

                for i, (k, n) in enumerate(steps):
                    for h in range(2):
                        dve.wait_ge(s_b, i + 1)
                        wait(dve, s_h, 2 * (i - 2) + h + 1)
                        dve.tensor_tensor(dB[:, i % 2, h, :], v["du"][:, h, k * BLK:(k + 1) * BLK], bs[:, i % 2, :],
                                          ALU.mult).then_inc(s_db, 1)
                    for h in range(2):
                        dve.wait_ge(s_da, 2 * i + h + 1)
                        dve.wait_ge(s_db, 2 * i + h + 1)
                        wait(dve, s_hc, 2 * (i - 2) + h + 1)
                        dve.tensor_tensor_scan(H[:, i % 2, h, :], dA[:, i % 2, h, :], dB[:, i % 2, h, :], 0.0,
                                               ALU.mult, ALU.add).then_inc(s_h, 1)
                    if n == 1 and k > 0:
                        finish(k - 1)
                finish(NBK - 1)

            @block.gpsimd
            def _(pool):
                for i in range(len(steps)):
                    pool.wait_ge(s_c, i + 1)
                    for h in range(2):
                        pool.wait_ge(s_h, 2 * i + h + 1)
                        wait(pool, s_y, 2 * (i - 2) + h + 1)
                        pool.tensor_tensor(HC[:, i % 2, h, :], H[:, i % 2, h, :], cs[:, i % 2, :],
                                           ALU.mult).then_inc(s_hc, 1)


def ssm_out_stage(nc, w, ins, v):
    with ExitStack() as ctx:
        sb, ps, sem = place(nc, ctx, "so")
        WO = sb("out_T", [P, 2, D])
        raw = sb("ffn_w", [P, 3, FD])
        wq = sb("ffn_w_rounded", [P, 3, FD], BF16)
        wsum = sb("w_abs_sum", [P, 3])
        wscale = sb("w_scale", [P, 3])
        wrec = sb("w_recip", [P, 3])
        ones = sb("ones", [P, P])
        idb = sb("ident_bf16", [P, P], BF16)
        R = sb("rows", [P, NT, D])
        Hn = sb("normed", [P, NT, D])
        stats = sb("stats", [P, 2, NT, 6])
        mv = sb("mean_var", [P, 2, NT, 2])
        ms = sb("mean_square", [P, 2, NT])
        rs = sb("rsqrt", [P, 2, NT])
        am = sb("abs_max", [P, 2, NT])
        ar = sb("abs_recip", [P, 2, NT])
        sc = sb("scales", [P, 3, NT])
        qa = sb("q_in", [P, NT, D])
        qb = sb("q_in_bf16", [P, NT, D], BF16)
        qT = sb("q_in_T", [P, T], BF16)
        gate = sb("gate", [P, 2, FD])
        gu = sb("gate_up", [P, 2, FD])
        g2 = sb("gate_up_rounded", [P, 2, FD])
        gb = sb("gate_up_bf16", [P, 2, FD], BF16)
        gT = sb("gate_up_T", [P, 2, 4, P], BF16)
        yb = ps("y_ps", [P, 2, NQ])
        gp = ps("gate_ps", [P, FD])
        up = ps("up_ps", [P, FD])
        tb = ps("T_ps", [P, 2, 2 * FD], BF16)
        wb = ps("w_sum_ps", [P, 4])
        s_w, s_one, s_y, s_yout, s_dve, s_ms, s_rs, s_wm, s_wq, s_q, s_tm, s_qT, s_id = (
            sem(n) for n in ("weights", "ones", "y_ps", "y_out", "chain", "mean_square", "rsqrt", "w_sum", "w_rounded",
                               "rounded", "T_ps", "rounded_T", "ident"))
        s_gm, s_um, s_gate, s_gu, s_gq, s_gtm, s_gT, s_dm, s_dout, s_ms2, s_rs2, s_po = (
            sem(n) for n in ("gate_ps", "up_ps", "gate", "gate_up", "gu_rounded", "gu_T_ps", "gu_T", "down_ps",
                               "down_out", "mean_square2", "rsqrt2", "pool"))
        with nc.Block() as block:
            @block.sync
            def _(sp):
                sp.dma_start(WO[:], ins["out_proj_T"].rearrange("(h p) n -> p h n", p=P)).then_inc(s_w, 16)
                sp.dma_start(raw[:, 0, :], ins["gate_T"]).then_inc(s_w, 16)
                sp.dma_start(raw[:, 1, :], ins["up_T"]).then_inc(s_w, 16)
                sp.dma_start(raw[:, 2, :].rearrange("p (c d) -> p c d", d=D),
                             ins["down_T"].rearrange("(c p) d -> p c d", p=P)).then_inc(s_w, 16)

            @block.gpsimd
            def _(pool):
                pool.memset(ones[:], 1.0).then_inc(s_one, 1)
                pool.wait_ge(s_ms, 1)
                pool.tensor_tensor(rs[:, 0, :], ms[:, 0, :], w["minus_half"][:], ALU.pow).then_inc(s_rs, 1)
                pool.wait_ge(s_ms2, 1)
                pool.tensor_tensor(rs[:, 1, :], ms[:, 1, :], w["minus_half"][:], ALU.pow).then_inc(s_rs2, 1)

            @block.tensor
            def _(pe):
                pe.wait_ge(s_w, 64)
                for q in range(Q):
                    if q >= 2:
                        pe.wait_ge(s_yout, q - 1)
                    for i in range(TQ):
                        t = q * TQ + i
                        for h in range(2):
                            last = pe.matmul(yb[:, q % 2, i * D:(i + 1) * D], v["du"][:, h, t * P:(t + 1) * P],
                                             WO[:, h, :], start=(h == 0), stop=(h == 1))
                    last.then_inc(s_y, 1)
                pe.wait_ge(s_one, 1)
                pe.wait_ge(s_dve, 1)
                pe.matmul(wb[:, 0:3], ones[:], wsum[:], start=True, stop=True).then_inc(s_wm, 1)
                pe.wait_ge(s_id, 1)
                pe.wait_ge(s_q, 1)
                for k in range(2):
                    for i in range(8):
                        t = 8 * k + i
                        last = pe.transpose(tb[:, k, i * P:(i + 1) * P], qb[:, t, :], idb[:])
                    last.then_inc(s_tm, 1)
                pe.wait_ge(s_wq, 1)
                for t in range(NT + 2):
                    if t < NT:
                        if t == 0:
                            pe.wait_ge(s_qT, 2)
                        wait(pe, s_gate, t)
                        pe.matmul(gp[:], qT[:, t * P:(t + 1) * P], wq[:, 0, :], start=True, stop=True).then_inc(s_gm, 1)
                        wait(pe, s_gu, t)
                        pe.matmul(up[:], qT[:, t * P:(t + 1) * P], wq[:, 1, :], start=True, stop=True).then_inc(s_um, 1)
                    if 1 <= t <= NT:
                        n = t - 1
                        pe.wait_ge(s_gq, n + 1)
                        wait(pe, s_gT, n - 1)
                        for c in range(4):
                            last = pe.transpose(tb[:, n % 2, c * P:(c + 1) * P], gb[:, n % 2, c * P:(c + 1) * P], idb[:])
                        last.then_inc(s_gtm, 1)
                    if t >= 2:
                        n = t - 2
                        pe.wait_ge(s_gT, n + 1)
                        wait(pe, s_dout, n - 1)
                        for c in range(4):
                            last = pe.matmul(yb[:, n % 2, 0:D], gT[:, n % 2, c, :], wq[:, 2, c * D:(c + 1) * D],
                                             start=(c == 0), stop=(c == 3))
                        last.then_inc(s_dm, 1)

            @block.scalar
            def _(act):
                for k in range(2):
                    act.wait_ge(s_tm, k + 1)
                    act.activation(qT[:, k * BLK:(k + 1) * BLK], tb[:, k, :], ACT.Copy).then_inc(s_qT, 1)
                for t in range(NT + 1):
                    if t < NT:
                        act.wait_ge(s_gm, t + 1)
                        wait(act, s_gu, t - 1)
                        act.activation(gate[:, t % 2, :], gp[:], ACT.Sigmoid, scale=sc[:, 0, t:t + 1]).then_inc(s_gate, 1)
                    if t >= 1:
                        n = t - 1
                        act.wait_ge(s_gtm, n + 1)
                        wait(act, s_dm, n - 1)
                        act.activation(gT[:, n % 2].rearrange("p c t -> p (c t)"), tb[:, n % 2, 0:FD],
                                       ACT.Copy).then_inc(s_gT, 1)

            @block.vector
            def _(dve):
                link = chain(dve, s_dve)
                over = lambda x, n=NT: x.rearrange("p (t o) -> p t o", o=1).to_broadcast([P, n, D])
                dve.wait_ge(s_w, 64)
                link(dve.tensor_reduce(wsum[:], raw[:], AX.X, ALU.add, apply_absolute_value=True))
                dve.tensor_copy(idb[:], w["ident"][:]).then_inc(s_id, 1)

                def rounded(dst, src, width):
                    lo, hi = width
                    link(dve.tensor_scalar(src, src, ROUND + lo, ROUND + hi, ALU.max, ALU.min))
                    return dve.tensor_scalar(dst, src, ROUND, None, ALU.subtract)

                def mean_square(k, q):
                    for t in range(q * TQ, q * TQ + TQ):
                        last = dve.bn_stats(stats[:, k, t, :], R[:, t, :])
                    link(last)
                    for t in range(q * TQ, q * TQ + TQ):
                        last = dve.bn_aggr(mv[:, k, t, :], stats[:, k, t, :])
                    link(last)

                def mean_squares_end(k, sem):
                    link(dve.tensor_tensor(ms[:, k, :], mv[:, k, :, 0], mv[:, k, :, 0], ALU.mult))
                    link(dve.tensor_tensor(ms[:, k, :], ms[:, k, :], mv[:, k, :, 1], ALU.add))
                    dve.tensor_scalar(ms[:, k, :], ms[:, k, :], 1e-6, None, ALU.add).then_inc(sem, 1)

                for q in range(Q):
                    a, b = q * TQ, q * TQ + TQ
                    dve.wait_ge(s_y, q + 1)
                    dve.tensor_tensor(R[:, a:b, :], yb[:, q % 2, :].rearrange("p (t d) -> p t d", d=D),
                                      w["Y"][:, a:b, :], ALU.add).then_inc(s_yout, 1)
                    dve.wait_ge(s_yout, q + 1)
                    mean_square(0, q)
                mean_squares_end(0, s_ms)
                dve.wait_ge(s_wm, 1)
                link(dve.tensor_scalar(wscale[:], wb[:, 0:3], 1.0 / (D * FD), 1e-5, ALU.mult, ALU.max))
                link(dve.reciprocal(wrec[:], wscale[:]))
                for k in range(3):
                    link(dve.tensor_scalar(raw[:, k, :], raw[:, k, :], wrec[:, k:k + 1], ROUND, ALU.mult, ALU.add))
                rounded(wq[:], raw[:], (-1.0, 1.0)).then_inc(s_wq, 1)
                dve.wait_ge(s_rs, 1)
                for t in range(NT):
                    last = dve.scalar_tensor_tensor(out=Hn[:, t, :], in0=R[:, t, :], scalar=rs[:, 0, t:t + 1],
                                                    in1=w["norm1_row"][:], op0=ALU.mult, op1=ALU.mult)
                link(last)
                link(dve.tensor_reduce(am[:, 0, :], Hn[:], AX.X, ALU.max, apply_absolute_value=True))
                link(dve.tensor_scalar(am[:, 0, :], am[:, 0, :], 1e-5, None, ALU.max))
                link(dve.reciprocal(ar[:, 0, :], am[:, 0, :]))
                link(dve.tensor_scalar(ar[:, 0, :], ar[:, 0, :], 127.0, None, ALU.mult))
                for t in range(NT):
                    last = dve.tensor_scalar(qa[:, t, :], Hn[:, t, :], ar[:, 0, t:t + 1], ROUND, ALU.mult, ALU.add)
                link(last)
                for k in range(2):
                    link(dve.tensor_scalar(sc[:, k, :], am[:, 0, :], wscale[:, k:k + 1], 1.0 / 127, ALU.mult, ALU.mult))
                rounded(qb[:], qa[:], (-128.0, 127.0)).then_inc(s_q, 1)

                def second(t):
                    i = t % 2
                    dve.wait_ge(s_gate, t + 1)
                    dve.wait_ge(s_um, t + 1)
                    dve.scalar_tensor_tensor(out=gu[:, i, :], in0=up[:], scalar=sc[:, 1, t:t + 1], in1=gate[:, i, :],
                                             op0=ALU.mult, op1=ALU.mult).then_inc(s_gu, 1)
                    dve.wait_ge(s_gu, t + 1)
                    a, r = am[:, 1, t:t + 1], ar[:, 1, t:t + 1]
                    link(dve.tensor_reduce(a, gu[:, i, :], AX.X, ALU.max, apply_absolute_value=True))
                    link(dve.tensor_scalar(a, a, 1e-5, None, ALU.max))
                    link(dve.reciprocal(r, a))
                    link(dve.tensor_scalar(r, r, 127.0, None, ALU.mult))
                    link(dve.tensor_scalar(g2[:, i, :], gu[:, i, :], r, ROUND, ALU.mult, ALU.add))
                    wait(dve, s_gtm, t - 1)
                    rounded(gb[:, i, :], g2[:, i, :], (-128.0, 127.0)).then_inc(s_gq, 1)
                    link(dve.tensor_scalar(sc[:, 2, t:t + 1], a, wscale[:, 2:3], 1.0 / 127, ALU.mult, ALU.mult))

                def third(t):
                    dve.wait_ge(s_dm, t + 1)
                    dve.scalar_tensor_tensor(out=R[:, t, :], in0=yb[:, t % 2, 0:D], scalar=sc[:, 2, t:t + 1],
                                             in1=Hn[:, t, :], op0=ALU.mult, op1=ALU.add).then_inc(s_dout, 1)
                for t in range(NT + 2):
                    if t < NT:
                        second(t)
                    if t >= 2:
                        third(t - 2)
                dve.wait_ge(s_dout, NT)
                for q in range(Q):
                    mean_square(1, q)
                mean_squares_end(1, s_ms2)
                dve.wait_ge(s_rs2, 1)
                for t in range(NT):
                    last = dve.scalar_tensor_tensor(out=Hn[:, t, :], in0=R[:, t, :], scalar=rs[:, 1, t:t + 1],
                                                    in1=w["norm2_row"][:], op0=ALU.mult, op1=ALU.mult)
                link(last)
                dve.tensor_tensor(w["X"][:], w["X"][:], Hn[:], ALU.add)


def ssm_stages(nc, w, ins):
    with ExitStack() as ctx:
        sb, ps, sem = place(nc, ctx, "ssm")
        v = {name: sb(name, [P, 2, T]) for name in ("u", "gate", "delta", "du")}
        with ExitStack() as inner:
            sb, ps, sem = place(nc, inner, "ssmi")
            v["D"] = sb("D", [P, 2])
            v["a"] = sb("a", [P, 2, NS])
            v["bc"] = sb("bc", [P, T], F32R)
            v["sel"] = sb("sel", [P, 2 * NS, P], F32R)
            with ExitStack() as tmp:
                v["sel32"] = place(nc, tmp, "ssmt")[0]("sel32", [P, 2 * NS, P])
                ssm_in_stage(nc, w, ins, v)
            ssm_scan_stage(nc, w, v)
        ssm_out_stage(nc, w, ins, v)


def prepare_stage(nc, w, ins):
    parts = {
        "M": ("L0_xattn_WqT", "L0_xattn_WkT", 16, 8, w["M0"]),
        "M1": ("L1_xattn_WqT", "L1_xattn_WkT", 64, 16, w["M1"]),
        "VO": ("L1_xattn_WvT", "L1_xattn_Wo", 64, 16, w["VO"]),
    }
    with ExitStack() as ctx:
        sb, ps, sem = place(nc, ctx, "prep")
        ops = {}
        for name, (a, b, k, h, _) in parts.items():
            ops[name] = (sb(f"{name}_a", [k, h, D]), sb(f"{name}_b", [k, h, D]))
        bank = [ps(f"fold{i}", [P, 512]) for i in range(2)]
        s_in = {name: sem(f"in_{name}") for name in parts}
        s_small, s_id, s_mm, s_out = sem("small"), sem("ident"), sem("folded_ps"), sem("folded")
        s_x = sem("x")
        small = []
        with nc.Block() as block:
            @block.sync
            def _(sp):
                for q in range(Q):
                    sp.dma_start(w["X"][:, q * TQ:(q + 1) * TQ, :],
                                 ins["x"].rearrange("(t a) l d -> (a l) t d", a=BT)[:, q * TQ:(q + 1) * TQ, :]).then_inc(s_x, 16)
                for name, (a, b, k, h, _) in parts.items():
                    for buf, src in zip(ops[name], (a, b)):
                        sp.dma_start(buf[:], ins[src].rearrange("h c d -> c h d")).then_inc(s_in[name], 16)
                sp.wait_ge(s_x, 16 * Q)

            @block.scalar
            def _(act):
                n = 0
                for key, src in (("pre_g", "L0_xattn_pre_g"), ("pre_b", "L0_xattn_pre_b"), ("ln_g", "L0_xattn_ln_g"),
                                 ("ln_b", "L0_xattn_ln_b"), ("ln2_w", "L1_xattn_ln2_w"), ("ln2_b", "L1_xattn_ln2_b")):
                    act.dma_start(w[key][:], ins[src].rearrange("(p o) -> p o", o=1)).then_inc(s_small, 16)
                    n += 1
                for key, src in (("ln1_w", "L1_xattn_ln1_w"), ("ln1_b", "L1_xattn_ln1_b"),
                                 ("ln_g_row", "L0_xattn_ln_g"), ("ln_b_row", "L0_xattn_ln_b"),
                                 ("ln2_w_row", "L1_xattn_ln2_w"), ("ln2_b_row", "L1_xattn_ln2_b"),
                                 ("norm1_row", "L1_attn_norm1_w"), ("norm2_row", "L1_attn_norm2_w")):
                    act.dma_start(w[key][:], ins[src].rearrange("(o d) -> o d", o=1).to_broadcast([P, D])).then_inc(s_small, 16)
                    n += 1
                for key, src in (("V0", "L0_xattn_Wv"), ("Wo0", "L0_xattn_Wo")):
                    act.dma_start(w[key][:], ins[src]).then_inc(s_small, 16)
                    n += 1
                k = 0
                for name, (_, _, _, h, dst) in parts.items():
                    for c in range(h // 4):
                        act.wait_ge(s_mm, k + 1)
                        act.activation(dst[:, 4 * c:4 * c + 4, :], bank[k % 2][:, :].rearrange("p (h d) -> p h d", h=4),
                                       ACT.Copy).then_inc(s_out, 1)
                        k += 1
                act.wait_ge(s_small, 16 * n)

            @block.tensor
            def _(pe):
                k = 0
                for name, (_, _, _, h, _) in parts.items():
                    a, b = ops[name]
                    pe.wait_ge(s_in[name], 32)
                    for c in range(h // 4):
                        if k >= 2:
                            pe.wait_ge(s_out, k - 1)
                        for i in range(4):
                            last = pe.matmul(bank[k % 2][:, i * D:(i + 1) * D], a[:, 4 * c + i, :], b[:, 4 * c + i, :],
                                             start=True, stop=True)
                        last.then_inc(s_mm, 1)
                        k += 1

            @block.gpsimd
            def _(pool):
                pool.memset(w["minus_half"][:], -0.5)
                pool.memset(w["eps"][:], EPS5)
                pool.memset(w["ident"][:], 0.0).then_inc(s_id, 1)
                pool.wait_ge(s_id, 1)
                pool.affine_select(out=w["ident"][:], in_=w["ident"][:], compare_op=ALU.not_equal, fill=1.0, base=0,
                                   pattern=[[-1, P]], channel_multiplier=1).then_inc(s_id, 1)


def build(nc, ins, out, upto=99, dbg=None):
    with ExitStack() as ctx:
        sb, ps, sem = place(nc, ctx, "all")
        w = {}
        folded = ExitStack()
        del RELEASED[:]
        for name, shape in (("X", [P, NT, D]), ("O", [P, NT, D]), ("Y", [P, NT, D]), ("N", [P, NT, D]), ("QT", [P, T]),
                            ("ident", [P, P]), ("minus_half", [P, NT]), ("eps", [P, 4]), ("pre_g", [D, 1]), ("pre_b", [D, 1]),
                            ("ln_g", [D, 1]), ("ln_b", [D, 1]), ("ln2_w", [D, 1]), ("ln2_b", [D, 1]),
                            ("ln1_w", [P, D]), ("ln1_b", [P, D]), ("ln_g_row", [P, D]), ("ln_b_row", [P, D]),
                            ("ln2_w_row", [P, D]), ("ln2_b_row", [P, D]), ("norm1_row", [P, D]), ("norm2_row", [P, D])):
            w[name] = sb(name, shape)
        fold_sb, _, _ = place(nc, folded, "all")
        for name, shape in (("M0", [P, 8, D]), ("M1", [P, 16, D]), ("VO", [P, 16, D]), ("V0", [D, D]),
                            ("Wo0", [D, D])):
            w[name] = fold_sb(name, shape)
        dram = {
            "ctx": ins["ctx_1024"],
            "kv_a": nc.dram_tensor("kv_a", (B, KC, 2 * D), F32, kind="Internal").ap(),
            "kv_b": nc.dram_tensor("kv_b", (B, KR, D), F32, kind="Internal").ap(),
            "kv_lat": nc.dram_tensor("kv_lat", (B, L, D), F32, kind="Internal").ap(),
        }
        def finish(buf):
            s_done = sem("result_stored")
            with nc.Block() as block:
                @block.sync
                def _(sp):
                    for q in range(Q):
                        sp.dma_start(out.rearrange("(t a) l d -> (a l) t d", a=BT)[:, q * TQ:(q + 1) * TQ, :],
                                     buf[:, q * TQ:(q + 1) * TQ, :]).then_inc(s_done, 16)
                    sp.wait_ge(s_done, 16 * Q)

        prepare_stage(nc, w, ins)
        norm_stage(nc, w, "q0", w["X"], w["Y"], w["QT"], gain=w["pre_g"], shift=w["pre_b"], twice=True)
        w["M"], w["V"] = w["M0"], w["V0"]
        attention_stage(nc, w, 0, dram)
        if upto == 1:
            folded.close()
            return finish(w["O"][:])
        norm_stage(nc, w, "o0", w["O"], w["Y"], w["QT"], gain=w["ln_g"], shift=w["ln_b"],
                   row_affine=(w["ln_g_row"], w["ln_b_row"]), rows_out=w["N"])
        gelu_stage(nc, w)
        clear_stage(nc)
        if upto == 2:
            folded.close()
            return finish(w["X"][:])
        norm_stage(nc, w, "sa_n", w["X"], w["Y"], w["QT"])
        self_attention_stage(nc, w, ins)
        if upto == 3:
            folded.close()
            return finish(w["X"][:])
        norm_stage(nc, w, "moe0_n", w["X"], w["Y"], w["QT"])
        moe_stage(nc, w, ins, 0)
        clear_stage(nc)
        if upto == 4:
            folded.close()
            return finish(w["X"][:])
        norm_stage(nc, w, "q1", w["X"], w["Y"], w["QT"], gain=w["ln2_w"], shift=w["ln2_b"], twice=True,
                   row_affine=(w["ln2_w_row"], w["ln2_b_row"]), rows_out=w["N"],
                   rows_T=dram["kv_lat"].rearrange("(t a) l d -> t (a l) d", a=BT))
        w["M"], w["V"] = w["M1"], w["VO"]
        attention_stage(nc, w, 1, dram)
        folded.close()
        norm_stage(nc, w, "ssm_n", w["X"], w["Y"], w["QT"], add=w["O"])
        if upto == 5:
            return finish(w["X"][:])
        clear_stage(nc)
        ssm_stages(nc, w, ins)
        clear_stage(nc)
        if upto == 6:
            return finish(w["X"][:])
        norm_stage(nc, w, "moe1_n", w["X"], w["Y"], w["QT"])
        moe_stage(nc, w, ins, 1)
        finish(w["X"][:])


def layout(inputs):
    a = {k: np.asarray(v) for k, v in inputs.items()}
    wkv = a["L1_xattn_Wkv"]
    inner = wkv.shape[1] // 2

    def heads(m, h):
        return np.ascontiguousarray(m.T.reshape(h, -1, m.shape[0]))

    out = {
        "x": a["x"], "ctx_1024": a["ctx_1024"],
        "L0_xattn_WqT": heads(a["L0_xattn_Wq"], 8), "L0_xattn_WkT": heads(a["L0_xattn_Wk"], 8),
        "L1_xattn_WqT": heads(a["L1_xattn_Wq"], 16), "L1_xattn_WkT": heads(wkv[:, :inner], 16),
        "L1_xattn_WvT": heads(wkv[:, inner:], 16), "L1_xattn_Wo": a["L1_xattn_Wo"].reshape(16, 64, D),
    }
    for k in ("L0_xattn_Wv", "L0_xattn_Wo", "L0_xattn_pre_g", "L0_xattn_pre_b", "L0_xattn_ln_g", "L0_xattn_ln_b",
              "L1_xattn_ln1_w", "L1_xattn_ln1_b", "L1_xattn_ln2_w", "L1_xattn_ln2_b", "L1_attn_norm1_w",
              "L1_attn_norm2_w"):
        out[k] = a[k]
    for k in ("q", "k", "v"):
        out[f"L0_attn_w{k}T"] = a[f"L0_attn_w{k}"].T
    out["moe0_router_T"], out["moe1_router_T"] = a["L0_ffn_router_w"].T, a["L1_ffn_Wr"].T
    out["moe0_w_in_T"] = a["L0_ffn_w1"].transpose(0, 2, 1)
    out["moe0_w_out_T"] = a["L0_ffn_w2"].transpose(0, 2, 1)
    out["moe1_w_in_T"] = np.stack([a["L1_ffn_Wg"], a["L1_ffn_Wu"]], 1).transpose(0, 1, 3, 2).reshape(16, D, 4 * D)
    out["moe1_w_out_T"] = a["L1_ffn_Wd"].transpose(0, 2, 1)
    out["in_proj_T"], out["out_proj_T"] = a["L1_attn_in_proj_w"].T, a["L1_attn_out_proj_w"].T
    out["x_proj_T"], out["dt_proj_T"] = a["L1_attn_x_proj_w"].T, a["L1_attn_dt_proj_w"].T
    for k in ("gate", "up", "down"):
        out[f"{k}_T"] = a[f"L1_attn_{k}_w"].T
    for k in ("conv_w", "conv_b", "dt_proj_b", "A_log", "D"):
        out[k] = a[f"L1_attn_{k}"]
    return {k: np.ascontiguousarray(v) for k, v in out.items()}


def kernel(**inputs):
    import concourse.bacc as _bacc
    from concourse.bass_utils import run_bass_kernel_spmd as _run

    nc = _bacc.Bacc("TRN2", target_bir_lowering=False, num_devices=1)
    arrays, ins = {}, {}
    for name, a in layout(inputs).items():
        arrays[f"in_{name}"] = a
        ins[name] = nc.dram_tensor(f"in_{name}", a.shape, mybir.dt.from_np(a.dtype), kind="ExternalInput").ap()
    out = nc.dram_tensor("out_x", (B, L, D), F32, kind="ExternalOutput").ap()
    build(nc, ins, out)
    r = _run(nc, [arrays], core_ids=[0])
    return r.results[0]["out_x"]
```

```python
from contextlib import ExitStack

import numpy as np

import concourse.bass as bass
from concourse import mybir

F32 = mybir.dt.float32
F32R = mybir.dt.float32r
BF16 = mybir.dt.bfloat16
I32 = mybir.dt.int32
ALU = mybir.AluOpType
ACT = mybir.ActivationFunctionType
AX = mybir.AxisListType

P = 128
D = 128
B = 64
L = 32
T = B * L
NT = T // P
BT = P // L
S_CTX = 257
KC = 86
KR = S_CTX - 2 * KC
EPS5 = 1e-5


def chain(eng, sem):
    count = [0]

    def link(ins):
        ins.then_inc(sem, 1)
        count[0] += 1
        eng.wait_ge(sem, count[0])
    return link


TAKEN = []


def place(nc, ctx, tag):
    def sb(name, shape, dt=F32):
        return ctx.enter_context(nc.sbuf_tensor(f"{tag}_{name}", shape, dt))

    def ps(name, shape, dt=F32):
        return ctx.enter_context(nc.psum_tensor(f"{tag}_{name}", shape, dt))

    def sem(name):
        s = ctx.enter_context(nc.semaphore(f"{tag}_{name}"))
        if tag != "all":
            TAKEN.append(s)
        return s
    return sb, ps, sem


def ended():
    old = list(TAKEN)
    del TAKEN[:]
    return old


def clear(pool, old):
    for s in old:
        pool.sem_clear(s)


def wait(eng, sem, value):
    if isinstance(value, int) and value <= 0:
        return
    eng.wait_ge(sem, value)


def attention_stage(nc, w, cross, dram):
    first = cross == 0
    tag = f"x{cross}"
    UB = 1 if first else 2
    NU = BT * UB
    GB = 2
    NUB = NU * GB
    NB = BT * GB
    TURNS = NT // GB
    KEYS = S_CTX if first else S_CTX + L
    rows = [KC, KC, KR if first else KR + L]
    cols = [0, KC, 2 * KC]
    pieces = 2 * UB
    HPG = BT + pieces
    ZPG = NU + 1
    scale = float(D) ** -0.5 if first else 1.0
    LA = 3 if first else 2
    H0 = LA + pieces
    CTX_DMAS = 2 if first else 3
    fold_slot = 0 if first else 1

    with ExitStack() as ctx:
        sb, ps, sem = place(nc, ctx, tag)
        KMAX = KC if first else rows[2]
        Cx = sb("ctx_rows", [max(KMAX, KC), NB, 3, D])
        PARTS = (("", F32),) if first else (("_hi", F32R), ("_lo", F32R))
        KW = KEYS + KEYS % 2 if not first else KEYS
        KT = [sb(f"keys_T{n}", [P, 2, KW], t) for n, t in PARTS]
        QF = [sb(f"folded_q{n}", [P, GB, BT, 8 * UB, L], t) for n, t in PARTS]
        Pr = sb("probs", [P, 2, 2, KEYS])
        PT = [sb(f"probs_T{n}", [max(KMAX, KC), 2, 3, 256], t) for n, t in PARTS]
        CV = [Cx] if first else [sb(f"ctx_rows{n}", [KMAX, 4, 3, D], t) for n, t in PARTS]
        PAIRS = ((0, 0),) if first else ((0, 0), (0, 1), (1, 0))
        ZT = sb("values_T", [P, 8 * UB, BT, L])
        NM = sb("neg_max", [P, 2, 2])
        DEN = sb("denominator", [P, 2, 2])
        RD = sb("recip_den", [P, 2, 2])
        S = [ps(f"scores{i}", [P, 2, 512]) for i in range(2)]
        Tp = ps("probs_T_ps", [P, 2, 512])
        Hp = ps("keys_T_ps", [P, 512])
        Zp = ps("values_ps", [P, 512])
        s_ctx = [sem(f"ctx_loaded{i}") for i in range(NB)]
        s_hfull, s_hfree = sem("h_bank_full"), sem("h_bank_free")
        s_zfull, s_zfree = sem("z_bank_full"), sem("z_bank_free")
        s_s, s_max, s_exp, s_rd, s_p = (sem(n) for n in ("scores", "max", "exp", "recip", "probs"))
        s_t, s_pt, s_zero = sem("probs_T_ps"), sem("probs_T"), sem("ctx_zeroed")
        if first:
            Hat = sb("normed_rows", [KC, 4, 3, D])
            Sc = sb("clipped", [P, 2, KEYS])
            stats = sb("stats", [KC, 2, 3, 6])
            mv = sb("mean_var", [KC, 4, 3, 2])
            var = sb("var_eps", [KC, 2, 3])
            rstd = sb("rstd", [KC, 4, 3])
            s_clip, s_bn, s_stats, s_var, s_rstd, s_hat = (
                sem(n) for n in ("clipped", "bn_stats", "mean_var", "var_eps", "rstd", "normed"))
            s_store = [sem(f"rows_stored{i}") for i in range(4)]
        else:
            s_gain, s_aff = sem("rows_gained"), sem("key_rows")
            s_hhi, s_phi, s_chi, s_clo, s_pad = (
                sem(n) for n in ("h_bank_hi", "probs_T_hi", "ctx_hi", "ctx_lo", "keys_padded"))

        def unit(g, j):
            return g * NUB + j

        def batch(g, i):
            return g * NB + i

        def z_before(g, j):
            return g * (ZPG * GB) + j + j // NU

        def o_before(g, grp):
            return g * (ZPG * GB) + grp * ZPG - 1

        def h_kt_before(g, i):
            grp, r = i // BT, i % BT
            skip = min(r, 2) if first else (0, 1, 3, 4)[r]
            if isinstance(g, int) and g * GB + grp == NT - 1:
                skip = 0
            return g * (HPG * GB) + grp * HPG + r + skip + H0

        def h_piece_before(g, grp, n):
            return g * (HPG * GB) + grp * HPG + H0 + n + (n + 1 if first else (n + 1) // 2 + 1)

        def keys_out(g, i):
            if isinstance(g, int) and g * NB + i < LA:
                n = g * NB + i
                return n + 1 if n < 2 else H0
            if i >= LA:
                return h_kt_before(g, i - LA) + 1
            return h_kt_before(g - 1, i - LA + NB) + 1

        def run(eng, body):
            body(0, True, False)
            with eng.Fori(1, TURNS - 1) as g:
                body(g, False, False)
            body(TURNS - 1, False, True)

        def par(j):
            return j % 2

        with nc.Block() as block:

            @block.sync
            def _(sp):
                def load(g, i):
                    n = i % NB
                    b = batch(g, i)
                    if not (isinstance(g, int) and g * NB + i < NB):
                        wait(sp, s_zfull, z_before(g, (i - NB) * UB + UB - 1) + 1)
                    if isinstance(b, int) and b < NB:
                        sp.wait_ge(s_zero, 1)
                    if first:
                        src = dram["ctx"][bass.ds(b, 1), 0:2 * KC, :].rearrange("b (c p) d -> (b p) c d", p=KC)
                        sp.dma_start(Cx[0:KC, n, 0:2, :], src).then_inc(s_ctx[n], 16)
                        src = dram["ctx"][bass.ds(b, 1), 2 * KC:S_CTX, :].rearrange("b p d -> (b p) d")
                        sp.dma_start(Cx[0:KR, n, 2, :], src).then_inc(s_ctx[n], 16)
                    else:
                        src = dram["kv_a"][bass.ds(b, 1), :, :].rearrange("b p (c d) -> (b p) c d", c=2)
                        sp.dma_start(Cx[0:KC, n, 0:2, :], src).then_inc(s_ctx[n], 16)
                        src = dram["kv_b"][bass.ds(b, 1), :, :].rearrange("b p d -> (b p) d")
                        sp.dma_start(Cx[0:KR, n, 2, :], src).then_inc(s_ctx[n], 16)
                        src = dram["kv_lat"][bass.ds(b, 1), :, :].rearrange("b p d -> (b p) d")
                        sp.dma_start(Cx[KR:KR + L, n, 2, :], src).then_inc(s_ctx[n], 16)

                def store(g, i):
                    b = batch(g, i)
                    wait(sp, s_hat, b + 1)
                    sp.dma_start(dram["kv_a"][bass.ds(b, 1), :, :].rearrange("b p (c d) -> (b p) c d", c=2),
                                 Hat[:, i % 4, 0:2, :]).then_inc(s_store[i % 4], 16)
                    sp.dma_start(dram["kv_b"][bass.ds(b, 1), :, :].rearrange("b p d -> (b p) d"),
                                 Hat[0:KR, i % 4, 2, :]).then_inc(s_store[i % 4], 16)

                ahead = 6 if first else 3
                for i in range(ahead):
                    load(0, i)
                if first:
                    for i in range(4):
                        store(0, i)

                def body(g, is_first, is_last):
                    for i in range(NB):
                        if not (is_last and i + ahead >= NB):
                            load(g, i + ahead)
                        if first and not (is_last and i + 4 >= NB):
                            store(g, i + 4)
                run(sp, body)
                if first:
                    for q in s_store:
                        sp.wait_ge(q, 32 * B // 4)

            @block.tensor
            def _(pe):
                def keys_T(g, i, before):
                    wait(pe, s_hat if first else s_aff, batch(g, i) + 1)
                    wait(pe, s_hfree, before)
                    src = Hat[:, i % 4] if first else Cx[:, i % NB]
                    for c in range(3):
                        last = pe.transpose(Hp[:, cols[c]:cols[c] + rows[c]], src[0:rows[c], c, :],
                                            w["ident"][0:rows[c], 0:rows[c]])
                    last.then_inc(s_hfull, 1)

                def fold_q(g, grp, n, before):
                    wait(pe, s_hfree, before)
                    rhs = w["QT"][:, bass.ds((g * GB + grp) * P, P)]
                    for h in range(4):
                        last = pe.matmul(Hp[:, h * P:(h + 1) * P], w["M"][:, 4 * n + h, :], rhs,
                                         start=True, stop=True)
                    last.then_inc(s_hfull, 1)

                def scores(g, j):
                    i = j // UB
                    if j % UB == 0:
                        wait(pe, s_hfree, keys_out(g, i))
                    if j % NU == 0:
                        wait(pe, s_hfree, fold_done(g, j // NU))
                    wait(pe, s_clip if first else s_exp, unit(g, j) - 1)
                    for r in range(2):
                        h0 = 8 * (j % UB) + 4 * r
                        for n, (a, b) in enumerate(PAIRS):
                            lhsT = QF[a][:, j // NU % GB, i % BT, h0:h0 + 4, :].rearrange("p h l -> p (h l)")
                            last = pe.matmul(S[par(j)][:, r, 0:KW], lhsT, KT[b][:, i % 2, :], start=(n == 0),
                                             stop=(n == len(PAIRS) - 1))
                    last.then_inc(s_s, 1)

                def fold_done(g, grp):
                    if isinstance(g, int) and g == 0 and grp == 0:
                        return 2 + pieces
                    if grp >= 1:
                        return h_piece_before(g, grp - 1, pieces - 1) + 1
                    return h_piece_before(g - 1, GB - 1, pieces - 1) + 1

                def probs_T(g, j):
                    wait(pe, s_p, unit(g, j) + 1)
                    wait(pe, s_pt, unit(g, j))
                    for r in range(2):
                        for c in range(3):
                            o = c * 256 + r * P
                            last = pe.transpose(Tp[0:rows[c], o // 512, o % 512:o % 512 + P],
                                                Pr[:, par(j), r, cols[c]:cols[c] + rows[c]], w["ident"][:])
                    last.then_inc(s_t, 1)

                def values(g, j):
                    i = j // UB
                    wait(pe, s_pt, unit(g, j) + 1)
                    wait(pe, s_zfree, z_before(g, j))
                    if not first:
                        wait(pe, s_clo, batch(g, i) + 1)
                    for c in range(3):
                        for n, (a, b) in enumerate(PAIRS):
                            last = pe.matmul(Zp[:, 0:256], CV[a][0:rows[c], i % (NB if first else 4), c, :],
                                             PT[b][0:rows[c], par(j), c, :], start=(c == 0 and n == 0),
                                             stop=(c == 2 and n == len(PAIRS) - 1))
                    last.then_inc(s_zfull, 1)

                def outputs(g, grp):
                    wait(pe, s_zfree, o_before(g, grp))
                    for h in range(8 * UB):
                        lhsT = ZT[:, h].rearrange("p b l -> p (b l)")
                        if first:
                            last = pe.matmul(Zp[:, 16 * h:16 * h + 16], lhsT, w["V"][:, 16 * h:16 * h + 16],
                                             start=True, stop=True)
                        else:
                            last = pe.matmul(Zp[:, 0:D], lhsT, w["V"][:, h, :], start=(h == 0),
                                             stop=(h == 8 * UB - 1))
                    last.then_inc(s_zfull, 1)

                keys_T(0, 0, 0)
                keys_T(0, 1, 1)
                for n in range(pieces):
                    fold_q(0, 0, n, 2 + n)
                if not first:
                    pe.wait_ge(s_pad, 1)
                scores(0, 0)
                if LA == 3:
                    keys_T(0, 2, 2 + pieces)
                scores(0, 1)

                def body(g, is_first, is_last):
                    for j in range(NUB):
                        grp, r = j // NU, j % NU
                        more_groups = not (is_last and grp == GB - 1)
                        piece = r - fold_slot
                        folds = more_groups and 0 <= piece < pieces
                        early = not first or piece == pieces - 1

                        def keys_ahead():
                            if j % UB == 0 and not (is_last and j // UB + LA >= NB):
                                keys_T(g, j // UB + LA, h_kt_before(g, j // UB))

                        def scores_ahead():
                            if not (is_last and j + 2 >= NUB):
                                scores(g, j + 2)
                        if first:
                            probs_T(g, j)
                            scores_ahead()
                            keys_ahead()
                        else:
                            keys_ahead()
                            scores_ahead()
                            probs_T(g, j)
                        if r == 1 and not (is_first and grp == 0):
                            outputs(g, grp)
                        if folds and early:
                            fold_q(g, grp + 1, piece, h_piece_before(g, grp, piece))
                        if not (is_first and j == 0):
                            values(g, j - 1)
                        if folds and not early:
                            fold_q(g, grp + 1, piece, h_piece_before(g, grp, piece))
                run(pe, body)
                values(TURNS - 1, NUB - 1)
                outputs(TURNS, 0)

            @block.scalar
            def _(act):
                def keys_T(g, i, before):
                    wait(act, s_hfull, before + 1)
                    wait(act, s_s, unit(g, (i - 2) * UB + UB - 1) + 1)
                    if first:
                        act.activation(KT[0][:, i % 2, :], Hp[:, 0:KEYS], ACT.Identity, bias=w["pre_b"][:, 0:1],
                                       scale=w["pre_g"][:, 0:1]).then_inc(s_hfree, 1)
                    else:
                        act.activation(KT[0][:, i % 2, 0:KEYS], Hp[:, 0:KEYS], ACT.Copy).then_inc(s_hhi, 1)

                def fold_q(grp, n, before):
                    wait(act, s_hfull, before + 1)
                    act.activation(QF[0][:, grp % GB, :, 4 * n:4 * n + 4, :].rearrange("p b h l -> p h b l"),
                                   Hp[:, :].rearrange("p (h b l) -> p h b l", h=4, b=BT), ACT.Copy,
                                   scale=scale).then_inc(s_hfree if first else s_hhi, 1)

                def exps(g, j):
                    wait(act, s_max, unit(g, j) + 1)
                    wait(act, s_t, unit(g, j) - 1)
                    src = Sc if first else S[par(j)]
                    for r in range(2):
                        last = act.activation(Pr[:, par(j), r, :], src[:, r, 0:KEYS], ACT.Exp,
                                              bias=NM[:, par(j), r:r + 1], accum_out=DEN[:, par(j), r:r + 1])
                    last.then_inc(s_exp, 1)

                def probs_T(g, j):
                    wait(act, s_t, unit(g, j) + 1)
                    wait(act, s_zfull, z_before(g, j - 2) + 1)
                    src = Tp[0:KMAX].rearrange("p a (b c) -> p (a b) c", b=2)[:, 0:3, :]
                    act.activation(PT[0][:, par(j)], src, ACT.Copy).then_inc(s_pt if first else s_phi, 1)

                def values(g, j):
                    wait(act, s_zfull, z_before(g, j) + 1)
                    h0 = 8 * (j % UB)
                    act.activation(ZT[:, h0:h0 + 8, (j // UB) % BT, :],
                                   Zp[:, 0:256].rearrange("p (h l) -> p h l", h=8), ACT.Copy).then_inc(s_zfree, 1)

                def outputs(g, grp):
                    wait(act, s_zfull, o_before(g, grp) + 1)
                    act.activation(w["O"][:, bass.ds(g * GB + grp - 1, 1), :].rearrange("p a d -> p (a d)"),
                                   Zp[:, 0:D], ACT.Copy).then_inc(s_zfree, 1)

                keys_T(0, 0, 0)
                keys_T(0, 1, 1)
                for n in range(pieces):
                    fold_q(0, n, 2 + n)
                if LA == 3:
                    keys_T(0, 2, 2 + pieces)
                exps(0, 0)
                exps(0, 1)

                def body(g, is_first, is_last):
                    for j in range(NUB):
                        grp, r = j // NU, j % NU
                        more_groups = not (is_last and grp == GB - 1)
                        piece = r - fold_slot
                        folds = more_groups and 0 <= piece < pieces

                        def keys_ahead():
                            if j % UB == 0 and not (is_last and j // UB + LA >= NB):
                                keys_T(g, j // UB + LA, h_kt_before(g, j // UB))

                        def exps_ahead():
                            if not (is_last and j + 2 >= NUB):
                                exps(g, j + 2)

                        def values_behind():
                            if not (is_first and j == 0):
                                values(g, j - 1)

                        def fold():
                            if folds:
                                fold_q(grp + 1, piece, h_piece_before(g, grp, piece))
                        if first:
                            probs_T(g, j)
                            keys_ahead()
                        else:
                            keys_ahead()
                            probs_T(g, j)
                        if r == 1:
                            exps_ahead()
                            if not (is_first and grp == 0):
                                outputs(g, grp)
                            fold()
                            values_behind()
                        elif first:
                            values_behind()
                            exps_ahead()
                            fold()
                        else:
                            fold()
                            exps_ahead()
                            values_behind()
                run(act, body)
                values(TURNS - 1, NUB - 1)
                outputs(TURNS, 0)

            @block.vector
            def _(dve):
                def row_stats(g, i):
                    dve.wait_ge(s_ctx[i % NB], CTX_DMAS * 16 * (g + i // NB + 1))
                    wait(dve, s_rstd, batch(g, i) - 1)
                    for c in range(3):
                        last = dve.bn_stats(stats[:, i % 2, c, :], Cx[0:KC, i % NB, c, :])
                    last.then_inc(s_bn, 1)

                def row_stats_end(g, i):
                    for c in range(3):
                        last = dve.bn_aggr(mv[:, i % 4, c, :], stats[:, i % 2, c, :])
                    last.then_inc(s_stats, 1)

                def normed(g, i):
                    wait(dve, s_rstd, batch(g, i) + 1)
                    if not (isinstance(g, int) and batch(g, i) < 4):
                        wait(dve, s_hfull, keys_out(g, i - 4))
                        wait(dve, s_store[i % 4], (g * (NB // 4) + i // 4) * 32)
                    for c in range(3):
                        last = dve.tensor_scalar(Hat[:, i % 4, c, :], Cx[0:KC, i % NB, c, :],
                                                 mv[:, i % 4, c, 0:1], rstd[:, i % 4, c:c + 1],
                                                 ALU.subtract, ALU.mult)
                    last.then_inc(s_hat, 1)

                def softmax_max(g, j, bn=None):
                    wait(dve, s_s, unit(g, j) + 1)
                    if first:
                        wait(dve, s_exp, unit(g, j))
                        dve.tensor_scalar(Sc[:], S[par(j)][:, :, 0:KEYS], -10000.0, 10000.0, ALU.max,
                                          ALU.min).then_inc(s_clip, 1)
                        wait(dve, s_clip, unit(g, j) + 1)
                    if bn is not None:
                        wait(dve, s_bn, bn)
                    src = Sc if first else S[par(j)]
                    dve.tensor_reduce(NM[:, par(j), :], src[:, :, 0:KEYS], AX.X, ALU.max,
                                      negate=True).then_inc(s_max, 1)

                def recip(g, j):
                    wait(dve, s_exp, unit(g, j) + 1)
                    wait(dve, s_p, unit(g, j) - 1)
                    dve.reciprocal(RD[:, par(j), :], DEN[:, par(j), :]).then_inc(s_rd, 1)

                def keys_lo(g, i, before):
                    wait(dve, s_hhi, before + 1)
                    dve.tensor_tensor(KT[1][:, i % 2, 0:KEYS], Hp[:, 0:KEYS], KT[0][:, i % 2, 0:KEYS],
                                      ALU.subtract).then_inc(s_hfree, 1)

                def fold_lo(grp, n, before):
                    wait(dve, s_hhi, before + 1)
                    hi, lo = (x[:, grp % GB, :, 4 * n:4 * n + 4, :].rearrange("p b h l -> p h b l") for x in QF)
                    dve.tensor_tensor(lo, Hp[:, :].rearrange("p (h b l) -> p h b l", h=4, b=BT), hi,
                                      ALU.subtract).then_inc(s_hfree, 1)

                def probs_lo(g, j):
                    wait(dve, s_phi, unit(g, j) + 1)
                    src = Tp[0:KMAX].rearrange("p a (b c) -> p (a b) c", b=2)[:, 0:3, :]
                    dve.tensor_tensor(PT[1][:, par(j)], src, PT[0][:, par(j)], ALU.subtract).then_inc(s_pt, 1)

                def rows_hi(g, i):
                    wait(dve, s_aff, batch(g, i) + 1)
                    if not (isinstance(g, int) and batch(g, i) < 4):
                        wait(dve, s_zfull, z_before(g, (i - 4) * UB + UB - 1) + 1)
                    dve.tensor_copy(CV[0][:, i % 4], Cx[0:KMAX, i % NB]).then_inc(s_chi, 1)

                def rows_lo(g, i):
                    wait(dve, s_chi, batch(g, i) + 1)
                    dve.tensor_tensor(CV[1][:, i % 4], Cx[0:KMAX, i % NB], CV[0][:, i % 4],
                                      ALU.subtract).then_inc(s_clo, 1)

                if first:
                    dve.memset(Cx[64:KC, :, 2, :], 0.0).then_inc(s_zero, 1)
                    dve.memset(Tp[64:KC, 1, 0:256], 0.0)
                    for i in range(5):
                        row_stats(0, i)
                        dve.wait_ge(s_bn, i + 1)
                        row_stats_end(0, i)
                        if i >= 1:
                            normed(0, i - 1)
                else:
                    dve.memset(Cx[64:KMAX, :, 0:2, :], 0.0).then_inc(s_zero, 1)
                    dve.memset(Tp[64:KMAX, 0, :], 0.0)
                    for x in KT:
                        last = dve.memset(x[:, :, KEYS:KW].bitcast(F32), 0.0)
                    last.then_inc(s_pad, 1)
                    keys_lo(0, 0, 0)
                    keys_lo(0, 1, 1)
                    for n in range(pieces):
                        fold_lo(0, n, 2 + n)
                    rows_hi(0, 0)
                    rows_lo(0, 0)
                softmax_max(0, 0)
                softmax_max(0, 1)
                recip(0, 0)

                def body(g, is_first, is_last):
                    for j in range(NUB):
                        stats_ahead = first and not (is_last and j + 5 >= NB)
                        if stats_ahead:
                            row_stats(g, j + 5)
                        if not first and j % UB == 0 and not (is_last and j // UB + LA >= NB):
                            keys_lo(g, j // UB + LA, h_kt_before(g, j // UB))
                        if not (is_last and j == NUB - 1):
                            recip(g, j + 1)
                        more_rows = not first and j % UB == 0 and not (is_last and j // UB + 1 >= NB)
                        if not (is_last and j + 2 >= NUB):
                            softmax_max(g, j + 2, batch(g, j + 5) + 1 if stats_ahead else None)
                        if stats_ahead:
                            row_stats_end(g, j + 5)
                        if not first:
                            probs_lo(g, j)
                        if more_rows:
                            rows_hi(g, j // UB + 1)
                        grp, piece = j // NU, j % NU - fold_slot
                        if not first and 0 <= piece < pieces and not (is_last and grp == GB - 1):
                            fold_lo(grp + 1, piece, h_piece_before(g, grp, piece))
                        if more_rows:
                            rows_lo(g, j // UB + 1)
                        if first and not (is_last and j + 4 >= NB):
                            normed(g, j + 4)
                run(dve, body)

            @block.gpsimd
            def _(pool):
                def norm(g, j):
                    wait(pool, s_rd, unit(g, j) + 1)
                    pool.tensor_tensor(Pr[:, par(j)], Pr[:, par(j)],
                                       RD[:, par(j), :].rearrange("p (r o) -> p r o", o=1).to_broadcast([P, 2, KEYS]),
                                       ALU.mult).then_inc(s_p, 1)

                def rsqrt(g, i):
                    wait(pool, s_stats, batch(g, i) + 1)
                    pool.tensor_tensor(var[:, i % 2], mv[:, i % 4, :, 1], w["eps"][0:KC, 0:3],
                                       ALU.add).then_inc(s_var, 1)
                    wait(pool, s_var, batch(g, i) + 1)
                    wait(pool, s_hat, batch(g, i) - 3)
                    pool.tensor_tensor(rstd[:, i % 4], var[:, i % 2], w["minus_half"][0:KC, 0:3],
                                       ALU.pow).then_inc(s_rstd, 1)

                def key_rows(g, i):
                    n = i % NB
                    pool.wait_ge(s_ctx[n], CTX_DMAS * 16 * (g + i // NB + 1))
                    wide = [w[k][0:KC, :].rearrange("p (o d) -> p o d", o=1).to_broadcast([KC, 2, D])
                            for k in ("ln1_w", "ln1_b")]
                    a, b = Cx[0:KC, n, 0:2, :], Cx[0:KR, n, 2, :]
                    pool.tensor_tensor(a, a, wide[0], ALU.mult).then_inc(s_gain, 1)
                    pool.tensor_tensor(b, b, w["ln1_w"][0:KR, :], ALU.mult).then_inc(s_gain, 1)
                    wait(pool, s_gain, 2 * batch(g, i) + 2)
                    pool.tensor_tensor(a, a, wide[1], ALU.add)
                    pool.tensor_tensor(b, b, w["ln1_b"][0:KR, :], ALU.add).then_inc(s_aff, 1)

                if first:
                    for i in range(5):
                        rsqrt(0, i)
                else:
                    for i in range(3):
                        key_rows(0, i)
                norm(0, 0)

                def body(g, is_first, is_last):
                    for j in range(NUB):
                        if not (is_last and j == NUB - 1):
                            norm(g, j + 1)
                        if first and not (is_last and j + 5 >= NB):
                            rsqrt(g, j + 5)
                        if not first and j % UB == 0 and not (is_last and j // UB + 3 >= NB):
                            key_rows(g, j // UB + 3)
                run(pool, body)


Q = 4
TQ = NT // Q
NQ = T // Q


def spread(ap, n):
    return ap.rearrange("p (n o) -> p n o", o=1).to_broadcast([ap.shape[0], n, D])


def norm_stage(nc, w, tag, src, rows, dst_T, gain=None, shift=None, twice=False, add=None, row_affine=None,
               rows_out=None, rows_T=None, first=None):
    with ExitStack() as ctx:
        sb, ps, sem = place(nc, ctx, tag)
        stats = sb("stats", [P, NT, 6])
        mv = sb("mean_var", [P, NT, 2])
        var, factor, off = (sb(n, [P, NT]) for n in ("var_eps", "factor", "offset"))
        bank = [ps(f"rows_T_ps{q}", [P, NQ]) for q in range(Q)]
        s_add, s_bn, s_stats, s_pool, s_rstd, s_off, s_T, s_out, s_gain, s_st = (
            sem(n) for n in ("added", "bn_stats", "mean_var", "pool_chain", "rstd", "offset", "transposed", "out",
                             "gained", "stored"))
        s_rows = [sem(f"rows{q}") for q in range(Q)]
        s_aff = [sem(f"affine{q}") for q in range(Q)]
        ACT_QS = Q // 2

        def cut(q):
            return slice(q * TQ, (q + 1) * TQ)

        def affine(eng, q, link):
            g3, b3 = (x[:, :].rearrange("p (o d) -> p o d", o=1).to_broadcast([P, TQ, D]) for x in row_affine)
            eng.wait_ge(s_rows[q], 1)
            link(eng.tensor_tensor(rows_out[:, cut(q), :], rows[:, cut(q), :], g3, ALU.mult))
            eng.tensor_tensor(rows_out[:, cut(q), :], rows_out[:, cut(q), :], b3, ALU.add).then_inc(s_aff[q], 1)

        with nc.Block() as block:
            @block.vector
            def _(dve):
                for q in range(Q):
                    if add is not None:
                        dve.tensor_tensor(src[:, cut(q), :], src[:, cut(q), :], add[:, cut(q), :],
                                          ALU.add).then_inc(s_add, 1)
                        dve.wait_ge(s_add, q + 1)
                    for t in range(q * TQ, q * TQ + TQ):
                        last = dve.bn_stats(stats[:, t, :], src[:, t, :])
                    last.then_inc(s_bn, 1)
                    dve.wait_ge(s_bn, q + 1)
                    for t in range(q * TQ, q * TQ + TQ):
                        last = dve.bn_aggr(mv[:, t, :], stats[:, t, :])
                    last.then_inc(s_stats, 1)
                for q in range(ACT_QS, Q):
                    dve.wait_ge(s_rstd, q + 1)
                    for t in range(q * TQ, q * TQ + TQ):
                        last = dve.tensor_scalar(rows[:, t, :], src[:, t, :], mv[:, t, 0:1], factor[:, t:t + 1],
                                                 ALU.subtract, ALU.mult)
                    last.then_inc(s_rows[q], 1)
                if row_affine is not None:
                    link = chain(dve, s_gain)
                    for q in range(ACT_QS, Q):
                        affine(dve, q, link)

            @block.gpsimd
            def _(pool):
                link = chain(pool, s_pool)
                for q in range(Q):
                    pool.wait_ge(s_stats, q + 1)
                    link(pool.tensor_tensor(var[:, cut(q)], mv[:, cut(q), 1], w["eps"][:, 0:TQ], ALU.add))
                    if twice:
                        link(pool.tensor_tensor(var[:, cut(q)], var[:, cut(q)], w["eps"][:, 0:TQ], ALU.mult))
                        link(pool.tensor_tensor(var[:, cut(q)], var[:, cut(q)], mv[:, cut(q), 1], ALU.add))
                    pool.tensor_tensor(factor[:, cut(q)], var[:, cut(q)], w["minus_half"][:, 0:TQ],
                                       ALU.pow).then_inc(s_rstd, 1)
                    if q < ACT_QS:
                        pool.wait_ge(s_rstd, q + 1)
                        link(pool.tensor_tensor(off[:, cut(q)], mv[:, cut(q), 0], factor[:, cut(q)], ALU.mult))
                        pool.tensor_tensor(off[:, cut(q)], w["zero"][:, 0:TQ], off[:, cut(q)],
                                           ALU.subtract).then_inc(s_off, 1)
                if row_affine is not None:
                    for q in range(ACT_QS):
                        affine(pool, q, link)

            @block.tensor
            def _(pe):
                for q in range(Q):
                    pe.wait_ge(s_rows[q], 1)
                    for i in range(TQ):
                        last = pe.transpose(bank[q][:, i * P:(i + 1) * P], rows[:, q * TQ + i, :], w["ident"][:])
                    last.then_inc(s_T, 1)

            @block.scalar
            def _(act):
                for q in range(ACT_QS):
                    act.wait_ge(s_off, q + 1)
                    for t in range(q * TQ, q * TQ + TQ):
                        last = act.activation(rows[:, t, :], src[:, t, :], ACT.Identity, bias=off[:, t:t + 1],
                                              scale=factor[:, t:t + 1])
                    last.then_inc(s_rows[q], 1)
                for q in range(Q):
                    act.wait_ge(s_T, q + 1)
                    if gain is None:
                        act.activation(dst_T[:, q * NQ:(q + 1) * NQ], bank[q][:], ACT.Copy)
                    else:
                        act.activation(dst_T[:, q * NQ:(q + 1) * NQ], bank[q][:], ACT.Identity,
                                       bias=shift[:, 0:1], scale=gain[:, 0:1])

            @block.sync
            def _(sp):
                if first is not None:
                    first(sp)
                if rows_T is not None:
                    for q in range(Q):
                        sp.wait_ge(s_aff[q], 1)
                        sp.dma_start(rows_T[q * TQ:(q + 1) * TQ, :, :].rearrange("t p d -> p t d"),
                                     rows_out[:, q * TQ:(q + 1) * TQ, :]).then_inc(s_st, 16)
                    sp.wait_ge(s_st, 16 * Q)


def gelu_stage(nc, w):
    old = ended()
    with ExitStack() as ctx:
        sb, ps, sem = place(nc, ctx, "g0")
        G = sb("gelu", [P, NT, D])
        bank = ps("proj", [P, Q, NQ])
        s_mm, s_gelu, s_add = sem("proj"), sem("gelu"), sem("added")
        with nc.Block() as block:
            @block.gpsimd
            def _(pool):
                clear(pool, old)

            @block.tensor
            def _(pe):
                for q in range(Q):
                    for i in range(TQ):
                        t = q * TQ + i
                        last = pe.matmul(bank[:, q, i * D:(i + 1) * D], w["QT"][:, t * P:(t + 1) * P], w["Wo0"][:],
                                         start=True, stop=True)
                    last.then_inc(s_mm, 1)

            @block.scalar
            def _(act):
                for q in range(Q):
                    act.wait_ge(s_mm, q + 1)
                    act.activation(G[:, q * TQ:(q + 1) * TQ, :].rearrange("p t d -> p (t d)"), bank[:, q, :],
                                   ACT.Gelu).then_inc(s_gelu, 1)

            @block.vector
            def _(dve):
                for q in range(Q):
                    x = w["X"][:, q * TQ:(q + 1) * TQ, :]
                    dve.tensor_tensor(x, x, w["N"][:, q * TQ:(q + 1) * TQ, :], ALU.add).then_inc(s_add, 1)
                for q in range(Q):
                    x = w["X"][:, q * TQ:(q + 1) * TQ, :]
                    dve.wait_ge(s_gelu, q + 1)
                    dve.wait_ge(s_add, q + 1)
                    dve.tensor_tensor(x, x, G[:, q * TQ:(q + 1) * TQ, :], ALU.add)


def self_attention_weights(nc, ctx, ins):
    sb, ps, sem = place(nc, ctx, "saw")
    W = sb("weights_T", [D, 3, D])
    s_w = sem("weights")

    def first(sp):
        for n, name in enumerate(("L0_attn_wqT", "L0_attn_wkT", "L0_attn_wvT")):
            sp.dma_start(W[:, n, :], ins[name]).then_inc(s_w, 16)
    return {"W": W, "s_w": s_w, "first": first}


def self_attention_stage(nc, w, pre):
    W, s_w = pre["W"], pre["s_w"]
    with ExitStack() as ctx:
        sb, ps, sem = place(nc, ctx, "sa")
        qk = sb("qk_T", [D, 2, T])
        V = sb("v_rows", [P, NT, D])
        A = sb("probs", [P, NT, L])
        AT = sb("probs_T", [P, NT, L])
        BD = sb("probs_diagonal", [P, NT, P])
        M = sb("max", [P, NT])
        den = sb("den", [P, NT])
        rden = sb("recip_den", [P, NT])
        bank = ps("proj", [P, 4, NQ])
        Sb = ps("scores", [P, NT, L])
        s_mm, s_out, s_s, s_dve, s_exp, s_mask, s_bd, s_o = (
            sem(n) for n in ("proj_ps", "proj", "scores", "chain", "exp", "masked", "diagonal", "out_ps"))
        with nc.Block() as block:
            @block.tensor
            def _(pe):
                pe.wait_ge(s_w, 48)
                n = 0
                for m in range(2):
                    for q in range(Q):
                        if n >= 4:
                            pe.wait_ge(s_out, n - 3)
                        pe.matmul(bank[:, n % 4, :], W[:, m, :], w["QT"][:, q * NQ:(q + 1) * NQ], start=True,
                                  stop=True).then_inc(s_mm, 1)
                        n += 1
                for q in range(Q):
                    pe.wait_ge(s_out, n - 3)
                    for i in range(TQ):
                        t = q * TQ + i
                        last = pe.matmul(bank[:, n % 4, i * D:(i + 1) * D], w["QT"][:, t * P:(t + 1) * P], W[:, 2, :],
                                         start=True, stop=True)
                    last.then_inc(s_mm, 1)
                    n += 1
                for b in range(B):
                    c = slice(b * L, (b + 1) * L)
                    o = (b % BT) * L
                    last = pe.matmul(Sb[o:o + L, b // BT, :], qk[:, 1, c], qk[:, 0, c], start=True, stop=True)
                last.then_inc(s_s, 1)
                pe.wait_ge(s_out, 12)
                pe.wait_ge(s_bd, 1)
                for q in range(Q):
                    for i in range(TQ):
                        t = q * TQ + i
                        last = pe.matmul(bank[:, q, i * D:(i + 1) * D], BD[:, t, :], V[:, t, :], start=True, stop=True)
                    last.then_inc(s_o, 1)

            @block.scalar
            def _(act):
                for n in range(12):
                    act.wait_ge(s_mm, n + 1)
                    q = n % Q
                    dst = qk[:, n // Q, q * NQ:(q + 1) * NQ] if n < 8 else V[:, q * TQ:(q + 1) * TQ, :].rearrange(
                        "p t d -> p (t d)")
                    act.activation(dst, bank[:, n % 4, :], ACT.Copy).then_inc(s_out, 1)
                act.wait_ge(s_dve, 3)
                act.activation(A[:], A[:], ACT.Exp, scale=float(D) ** -0.5).then_inc(s_exp, 1)

            @block.gpsimd
            def _(pool):
                pool.wait_ge(s_dve, 6)
                for j in range(BT):
                    a = A[j * L:(j + 1) * L]
                    last = pool.affine_select(out=a, in_=a, compare_op=ALU.is_ge, fill=0.0, base=0,
                                              pattern=[[0, NT], [-1, L]], channel_multiplier=1)
                last.then_inc(s_mask, 1)

            @block.vector
            def _(dve):
                link = chain(dve, s_dve)
                link(dve.memset(BD[:], 0.0))
                dve.wait_ge(s_s, 1)
                link(dve.tensor_reduce(M[:], Sb[:], AX.X, ALU.max))
                over = lambda v: v[:, :].rearrange("p (t o) -> p t o", o=1).to_broadcast([P, NT, L])
                link(dve.tensor_tensor(A[:], Sb[:], over(M), ALU.subtract))
                dve.wait_ge(s_exp, 1)
                link(dve.tensor_reduce(den[:], A[:], AX.X, ALU.add))
                link(dve.reciprocal(rden[:], den[:]))
                link(dve.tensor_tensor(A[:], A[:], over(rden), ALU.mult))
                dve.wait_ge(s_mask, 1)
                link(dve.transpose(AT[:, :, :].rearrange("p t l -> p (t l)"), A[:, :, :].rearrange("p t l -> p (t l)")))
                for j in range(BT):
                    r = slice(j * L, (j + 1) * L)
                    last = dve.tensor_copy(BD[r, :, r], AT[r, :, :])
                last.then_inc(s_bd, 1)
                for q in range(Q):
                    dve.wait_ge(s_o, q + 1)
                    x = w["X"][:, q * TQ:(q + 1) * TQ, :]
                    dve.tensor_tensor(x, bank[:, q, :].rearrange("p (t d) -> p t d", d=D), x, ALU.add)


def moe_weights(nc, ctx, ins, layer):
    FF = 4 * D
    FC = FF // P
    NW = 2 if layer else 1
    tag = f"moe{layer}"
    sb, ps, sem = place(nc, ctx, f"{tag}w")
    R = sb("router_T", [D, 8])
    W1 = sb("w_in_T", [D, 2, NW, FF])
    W2 = sb("w_out_T", [P, 2, FC, D])
    s_r = sem("router")
    s_w = [sem(f"weights{i}") for i in range(2)]

    def load_in(sp, e, par):
        for n in range(NW):
            src = ins[f"{tag}_w_in_T"][bass.ds(e * NW + n, 1), :, :].rearrange("e d f -> (e d) f")
            sp.dma_start(W1[:, par, n, :], src).then_inc(s_w[par], 16)

    def load_out(sp, e, par):
        src = ins[f"{tag}_w_out_T"][bass.ds(e, 1), :, :].rearrange("e (c p) d -> p (e c) d", p=P)
        sp.dma_start(W2[:, par], src).then_inc(s_w[par], 16)

    def first(sp):
        sp.dma_start(R[:], ins[f"{tag}_router_T"]).then_inc(s_r, 16)
        for par in range(2):
            load_in(sp, par, par)
            load_out(sp, par, par)
    return {"R": R, "W1": W1, "W2": W2, "s_r": s_r, "s_w": s_w, "first": first, "load_in": load_in,
            "load_out": load_out}


def moe_stage(nc, w, pre, layer, old):
    E, FF = 8, 4 * D
    FC = FF // P
    tag = f"moe{layer}"
    gated = layer == 1
    NW = 2 if gated else 1
    PARTS = (("_hi", F32R), ("_lo", F32R))
    R, W1, W2, s_r, s_w = (pre[k] for k in ("R", "W1", "W2", "s_r", "s_w"))
    with ExitStack() as ctx:
        sb, ps, sem = place(nc, ctx, tag)
        W1h, W1l = (sb(f"w_in_T{n}", [D, 2, NW, FF], t) for n, t in PARTS)
        Hd = sb("hidden_T", [P, 2, FC, NQ])
        Qh, Ql = (sb(f"tokens_T{n}", [D, T], t) for n, t in PARTS)
        Rl = sb("relu", [P, 2, NQ]) if gated else None
        pr = sb("probs", [P, NT, E])
        gt = sb("greater", [P, NT, E, E])
        eq = sb("equal", [P, NT, E, E])
        low = sb("lower", [P, E, E])
        mx, den, rden = (sb(n, [P, NT]) for n in ("max", "den", "recip_den"))
        rank = sb("rank", [P, NT, E])
        Wt = sb("weights", [P, NT, E])
        We = sb("weights_e", [P, 2, NT])
        Hb = [ps(f"hidden_ps{i}", [P, NQ]) for i in range(4)]
        Yb = [ps(f"out_ps{i}", [P, NQ]) for i in range(2)]
        Rb = ps("router_ps", [P, NT, E])
        s_rm, s_dve, s_exp, s_low = (sem(n) for n in ("logits", "chain", "exp", "lower"))
        s_h, s_act, s_y, s_x, s_we, s_relu = (
            sem(n) for n in ("hidden_ps", "hidden", "out_ps", "added", "weights_e", "relu"))
        s_qh, s_ql, s_wh, s_wl = (sem(n) for n in ("tokens_hi", "tokens_lo", "weights_hi", "weights_lo"))

        with nc.Block() as block:
            @block.sync
            def _(sp):
                def load(e, par):
                    sp.wait_ge(s_wl, e - 1)
                    pre["load_in"](sp, e, par)
                    sp.wait_ge(s_y, (e - 1) * Q)
                    pre["load_out"](sp, e, par)
                with sp.Fori(1, E // 2) as i:
                    load(i * 2, 0)
                    load(i * 2 + 1, 1)

            WD = 16 * (NW + 1)

            def split_ahead(i, j, is_last):
                if j % Q != 1 or (is_last and j >= Q):
                    return None
                return (i, 1) if j < Q else (i + 1, 0)

            @block.tensor
            def _(pe):
                pe.wait_ge(s_r, 16)
                for t in range(NT):
                    last = pe.matmul(Rb[:, t, :], w["QT"][:, t * P:(t + 1) * P], R[:], start=True, stop=True)
                last.then_inc(s_rm, 1)

                def hidden(i, j, c):
                    i, j = i + j // (2 * Q), j % (2 * Q)
                    par, q = j // Q, j % Q
                    u = i * 2 * Q + j
                    if c == 0 and q == 0:
                        pe.wait_ge(s_wl, i * 2 + par + 1)
                    if c == 0 and isinstance(i, int) and u < Q:
                        pe.wait_ge(s_ql, q + 1)
                    if not gated:
                        wait(pe, s_act, u * FC + c - 3)
                        banks = [Hb[c]]
                    else:
                        wait(pe, s_act, u * FC + c - 1)
                        banks = Hb[2 * (c % 2):2 * (c % 2) + 2]
                    for k, hb in enumerate(banks):
                        for x, (wx, qx) in enumerate(((W1h, Qh), (W1h, Ql), (W1l, Qh))):
                            last = pe.matmul(hb[:], wx[:, par, k, c * P:(c + 1) * P],
                                             qx[:, q * NQ:(q + 1) * NQ], start=(x == 0), stop=(x == 2))
                    last.then_inc(s_h, 1)

                def output(i, j, t):
                    par, q = j // Q, j % Q
                    u = i * 2 * Q + j
                    if t == 0:
                        wait(pe, s_act, (u + 1) * FC)
                        wait(pe, s_x, u - 1)
                    for c in range(FC):
                        last = pe.matmul(Yb[j % 2][:, t * D:(t + 1) * D], Hd[:, j % 2, c, t * P:(t + 1) * P],
                                         W2[:, par, c, :], start=(c == 0), stop=(c == FC - 1))
                    if t == TQ - 1:
                        last.then_inc(s_y, 1)

                for c in range(FC):
                    hidden(0, 0, c)

                def body(i, is_last=False):
                    for j in range(2 * Q):
                        for n in range(FC):
                            if not (is_last and j == 2 * Q - 1):
                                hidden(i, j + 1, n)
                            output(i, j, n)
                body(0)
                with pe.Fori(1, E // 2 - 1) as i:
                    body(i)
                body(E // 2 - 1, True)

            @block.scalar
            def _(act):
                def weights_hi(i, par):
                    act.wait_ge(s_w[par], (i + 1) * WD)
                    wait(act, s_h, (i * 2 + par - 1) * Q * FC)
                    for n in range(NW):
                        last = act.activation(W1h[:, par, n], W1[:, par, n], ACT.Copy)
                    last.then_inc(s_wh, 1)

                for q in range(Q):
                    act.activation(Qh[:, q * NQ:(q + 1) * NQ], w["QT"][:, q * NQ:(q + 1) * NQ],
                                   ACT.Copy).then_inc(s_qh, 1)
                    if q == 0:
                        weights_hi(0, 0)
                act.wait_ge(s_dve, 2)
                act.activation(pr[:], pr[:], ACT.Exp).then_inc(s_exp, 1)

                def body(i, is_last=False):
                    for j in range(2 * Q):
                        u = i * 2 * Q + j
                        for c in range(FC):
                            n = u * FC + c
                            act.wait_ge(s_h, n + 1)
                            if gated:
                                wait(act, s_act, n - 1)
                                act.activation(Rl[:, c % 2, :], Hb[2 * (c % 2)][:], ACT.Relu).then_inc(s_relu, 1)
                            else:
                                wait(act, s_y, u - 1)
                                act.activation(Hd[:, j % 2, c, :], Hb[c][:], ACT.Gelu).then_inc(s_act, 1)
                        ahead = split_ahead(i, j, is_last)
                        if ahead:
                            weights_hi(*ahead)
                body(0)
                with act.Fori(1, E // 2 - 1) as i:
                    body(i)
                body(E // 2 - 1, True)

            @block.gpsimd
            def _(pool):
                pool.memset(low[:], 1.0).then_inc(s_low, 1)
                pool.wait_ge(s_low, 1)
                pool.affine_select(out=low[:], in_=low[:], compare_op=ALU.is_gt, fill=0.0, base=0,
                                   pattern=[[1, E], [-1, E]], channel_multiplier=0).then_inc(s_low, 1)

                def weights_lo(i, par):
                    pool.wait_ge(s_wh, i * 2 + par + 1)
                    pool.tensor_tensor(W1l[:, par], W1[:, par], W1h[:, par], ALU.subtract).then_inc(s_wl, 1)

                weights_lo(0, 0)
                clear(pool, old)

                def body(i, is_last=False):
                    for j in (1, Q + 1):
                        ahead = split_ahead(i, j, is_last)
                        if ahead:
                            weights_lo(*ahead)
                body(0)
                with pool.Fori(1, E // 2 - 1) as i:
                    body(i)
                body(E // 2 - 1, True)

            @block.vector
            def _(dve):
                link = chain(dve, s_dve)
                over = lambda v: v[:, :].rearrange("p (t o) -> p t o", o=1).to_broadcast([P, NT, E])
                for q in range(Q):
                    dve.wait_ge(s_qh, q + 1)
                    dve.tensor_tensor(Ql[:, q * NQ:(q + 1) * NQ], w["QT"][:, q * NQ:(q + 1) * NQ],
                                      Qh[:, q * NQ:(q + 1) * NQ], ALU.subtract).then_inc(s_ql, 1)
                dve.wait_ge(s_rm, 1)
                link(dve.tensor_reduce(mx[:], Rb[:], AX.X, ALU.max))
                link(dve.tensor_tensor(pr[:], Rb[:], over(mx), ALU.subtract))
                dve.wait_ge(s_exp, 1)
                link(dve.tensor_reduce(den[:], pr[:], AX.X, ALU.add))
                link(dve.reciprocal(rden[:], den[:]))
                link(dve.tensor_tensor(pr[:], pr[:], over(rden), ALU.mult))
                mine = pr[:, :, :].rearrange("p t (e o) -> p t e o", o=1).to_broadcast([P, NT, E, E])
                other = pr[:, :, :].rearrange("p t (o j) -> p t o j", o=1).to_broadcast([P, NT, E, E])
                dve.tensor_tensor(gt[:], other, mine, ALU.is_gt)
                link(dve.tensor_tensor(eq[:], other, mine, ALU.is_equal))
                dve.wait_ge(s_low, 2)
                link(dve.tensor_tensor(eq[:], eq[:], low[:, :, :].rearrange("p (o e) j -> p o e j", o=1).to_broadcast(
                    [P, NT, E, E]), ALU.mult))
                link(dve.tensor_tensor(gt[:], gt[:], eq[:], ALU.add))
                link(dve.tensor_reduce(rank[:], gt[:], AX.X, ALU.add))
                link(dve.scalar_tensor_tensor(out=Wt[:], in0=rank[:], scalar=1.5, in1=pr[:], op0=ALU.is_lt,
                                              op1=ALU.mult))
                if gated:
                    link(dve.tensor_reduce(den[:], Wt[:], AX.X, ALU.add))
                    link(dve.tensor_scalar(den[:], den[:], float(np.finfo(np.float32).eps), None, ALU.add))
                    link(dve.reciprocal(rden[:], den[:]))
                    link(dve.tensor_tensor(Wt[:], Wt[:], over(rden), ALU.mult))

                def gate(i, j):
                    u = i * 2 * Q + j
                    for c in range(FC):
                        n = u * FC + c
                        dve.wait_ge(s_relu, n + 1)
                        wait(dve, s_y, u - 1)
                        dve.tensor_tensor(Hd[:, j % 2, c, :], Hb[2 * (c % 2) + 1][:], Rl[:, c % 2, :],
                                          ALU.mult).then_inc(s_act, 1)

                def add(i, j):
                    par, q = j // Q, j % Q
                    u = i * 2 * Q + j
                    if q == 0:
                        dve.tensor_copy(We[:, par, :], Wt[:, :, bass.ds(i * 2 + par, 1)].rearrange(
                            "p t o -> p (t o)")).then_inc(s_we, 1)
                        dve.wait_ge(s_we, i * 2 + par + 1)
                    dve.wait_ge(s_y, u + 1)
                    for t in range(TQ):
                        n = q * TQ + t
                        last = dve.scalar_tensor_tensor(
                            out=w["X"][:, n, :], in0=Yb[j % 2][:, t * D:(t + 1) * D],
                            scalar=We[:, par, n:n + 1], in1=w["X"][:, n, :], op0=ALU.mult, op1=ALU.add)
                    last.then_inc(s_x, 1)

                if gated:
                    gate(0, 0)

                def body(i, is_last=False):
                    for j in range(2 * Q):
                        if gated and not (is_last and j == 2 * Q - 1):
                            gate(i + (j + 1) // (2 * Q), (j + 1) % (2 * Q))
                        add(i, j)
                body(0)
                with dve.Fori(1, E // 2 - 1) as i:
                    body(i)
                body(E // 2 - 1, True)


DI = 2 * D
NS = 16
RANK = 64
FD = 4 * D
BLK = 1024
ROUND = 1.5 * 2.0 ** 23


def ssm_weights(nc, ctx, ins):
    sb, ps, sem = place(nc, ctx, "ssmw")
    v = {"W": sb("in_T", [D, 2 * DI]), "WX": sb("x_T", [P, 2, RANK + 2 * NS]), "WD": sb("dt_T", [RANK, DI]),
         "cw": sb("conv_w", [P, 2, 4]), "cb": sb("conv_b", [P, 2]), "db": sb("dt_b", [P, 2]),
         "D": sb("D", [P, 2]), "a": sb("a", [P, 2, NS]), "WO": sb("out_T", [P, 2, D]),
         "ffn": sb("ffn_w", [P, 3, FD]), "s_w": sem("weights"), "s_wo": sem("ffn_weights")}
    s_w, s_wo = v["s_w"], v["s_wo"]

    def first(sp):
        sp.dma_start(v["W"][:], ins["in_proj_T"]).then_inc(s_w, 16)
        sp.dma_start(v["WX"][:], ins["x_proj_T"].rearrange("(h p) n -> p h n", p=P)).then_inc(s_w, 16)
        sp.dma_start(v["WD"][:], ins["dt_proj_T"]).then_inc(s_w, 16)
        sp.dma_start(v["cw"][:], ins["conv_w"].rearrange("(h p) n -> p h n", p=P)).then_inc(s_w, 16)
        with nc.allow_non_contiguous_dma(reason="one value per partition"):
            sp.dma_start(v["cb"][:], ins["conv_b"].rearrange("(h p) -> p h", p=P)).then_inc(s_w, 16)
            sp.dma_start(v["db"][:], ins["dt_proj_b"].rearrange("(h p) -> p h", p=P)).then_inc(s_w, 16)
            sp.dma_start(v["D"][:], ins["D"].rearrange("(h p) -> p h", p=P)).then_inc(s_w, 16)
        sp.dma_start(v["a"][:], ins["A_log"].rearrange("(h p) n -> p h n", p=P)).then_inc(s_w, 16)
        sp.dma_start(v["WO"][:], ins["out_proj_T"].rearrange("(h p) n -> p h n", p=P)).then_inc(s_wo, 16)
        sp.dma_start(v["ffn"][:, 0, :], ins["gate_T"]).then_inc(s_wo, 16)
        sp.dma_start(v["ffn"][:, 1, :], ins["up_T"]).then_inc(s_wo, 16)
        sp.dma_start(v["ffn"][:, 2, :].rearrange("p (c d) -> p c d", d=D),
                     ins["down_T"].rearrange("(c p) d -> p c d", p=P)).then_inc(s_wo, 16)
    v["first"] = first
    return v


def ssm_in_stage(nc, w, v, old):
    with ExitStack() as ctx:
        sb, ps, sem = place(nc, ctx, "si")
        W, WX, WD, cw, cb, db, s_w = (v[k] for k in ("W", "WX", "WD", "cw", "cb", "db", "s_w"))
        XD = sb("x_dbl", [RANK + 2 * NS, T])
        pre = v["delta"]
        z = v["du"]
        neg = sb("neg_abs", [P, 2, T])
        tiny = sb("tiny", [P, 2, T])
        mask = sb("mask", [P, 2, T], mybir.dt.uint8)
        bank = ps("proj", [P, 4, NQ])
        xb = ps("x_ps", [P, 2, NQ])
        zb = ps("z_ps", [P, 2, NQ])
        s_mm, s_out, s_dve, s_conv, s_u, s_xm, s_xd, s_zm, s_z, s_neg, s_e, s_ln, s_a, s_sp = (
            sem(n) for n in ("proj_ps", "proj", "chain", "conv", "u", "x_ps", "x_dbl", "z_ps", "z",
                               "neg_abs", "exp", "ln", "a", "softplus"))
        s_sel, s_p, s_one, s_wsum, s_wm = (sem(n) for n in ("selector", "pool", "ones", "w_abs_sum", "w_sum_ps"))
        raw, wq, wscale = v["ffn"], v["wq"], v["wscale"]
        wsum = sb("w_abs_sum", [P, 3])
        wrec = sb("w_recip", [P, 3])
        ones = sb("ones", [P, P])
        with nc.Block() as block:
            @block.tensor
            def _(pe):
                pe.wait_ge(s_w, 128)
                for m in range(4):
                    for q in range(Q):
                        n = 4 * m + q
                        if n >= 4:
                            pe.wait_ge(s_out, n - 3)
                        pe.matmul(bank[:, q, :], W[:, m * P:(m + 1) * P], w["QT"][:, q * NQ:(q + 1) * NQ],
                                  start=True, stop=True).then_inc(s_mm, 1)
                for q in range(Q):
                    c = slice(q * NQ, (q + 1) * NQ)
                    pe.wait_ge(s_u, 2)
                    if q >= 2:
                        pe.wait_ge(s_xd, q - 1)
                    for h in range(2):
                        last = pe.matmul(xb[0:RANK + 2 * NS, q % 2, :], WX[:, h, :], v["u"][:, h, c], start=(h == 0),
                                         stop=(h == 1))
                    last.then_inc(s_xm, 1)
                pe.wait_ge(s_one, 1)
                pe.wait_ge(s_wsum, 1)
                pe.wait_ge(s_out, 16)
                pe.matmul(bank[:, 0, 0:3], ones[:], wsum[:], start=True, stop=True).then_inc(s_wm, 1)
                for h in range(2):
                    for q in range(Q):
                        n = 4 * h + q
                        pe.wait_ge(s_xd, q + 1)
                        if n >= 2:
                            pe.wait_ge(s_z, n - 1)
                        pe.matmul(zb[:, n % 2, :], WD[:, h * P:(h + 1) * P], XD[0:RANK, q * NQ:(q + 1) * NQ],
                                  start=True, stop=True).then_inc(s_zm, 1)

            @block.scalar
            def _(act):
                for m in range(4):
                    for q in range(Q):
                        c = slice(q * NQ, (q + 1) * NQ)
                        act.wait_ge(s_mm, 4 * m + q + 1)
                        if m < 2:
                            act.activation(pre[:, m, c], bank[:, q, :], ACT.Copy).then_inc(s_out, 1)
                        else:
                            act.activation(v["gate"][:, m - 2, c], bank[:, q, :], ACT.Silu).then_inc(s_out, 1)
                for h in range(2):
                    act.wait_ge(s_conv, h + 1)
                    act.activation(v["u"][:, h, :], v["u"][:, h, :], ACT.Silu).then_inc(s_u, 1)
                act.activation(v["a"][:], v["a"][:], ACT.Exp).then_inc(s_a, 1)
                for q in range(Q):
                    c = slice(q * NQ, (q + 1) * NQ)
                    act.wait_ge(s_xm, q + 1)
                    act.activation(XD[:, c], xb[0:RANK + 2 * NS, q % 2, :], ACT.Copy).then_inc(s_xd, 1)
                for h in range(2):
                    for q in range(Q):
                        c = slice(q * NQ, (q + 1) * NQ)
                        act.wait_ge(s_zm, 4 * h + q + 1)
                        act.activation(z[:, h, c], zb[:, q % 2, :], ACT.Identity, bias=db[:, h:h + 1])
                        act.activation(neg[:, h, c], zb[:, q % 2, :], ACT.Abs, bias=db[:, h:h + 1]).then_inc(s_z, 1)
                    act.wait_ge(s_z, 4 * h + 4)
                    act.activation(neg[:, h, :], neg[:, h, :], ACT.Exp, scale=-1.0).then_inc(s_e, 1)
                    act.wait_ge(s_e, h + 1)
                    act.activation(tiny[:, h, :], neg[:, h, :], ACT.Copy, scale=-0.25).then_inc(s_neg, 1)
                    act.activation(v["delta"][:, h, :], neg[:, h, :], ACT.Ln, bias=1.0).then_inc(s_ln, 1)

            @block.gpsimd
            def _(pool):
                pool.memset(ones[:], 1.0).then_inc(s_one, 1)
                sel = v["sel32"]
                pool.memset(sel[:], 0.0).then_inc(s_p, 1)
                pool.wait_ge(s_p, 1)
                for o in (64, 96):
                    s = sel[o:o + 2 * NS]
                    last = pool.affine_select(out=s, in_=s, compare_op=ALU.not_equal, fill=1.0, base=0,
                                              pattern=[[-1, 2 * NS], [0, P]], channel_multiplier=1)
                last.then_inc(s_sel, 1)
                clear(pool, old)
                pool.wait_ge(s_sp, 1)
                pool.tensor_tensor(v["du"][:, 0, :], v["delta"][:, 0, :], v["u"][:, 0, :], ALU.mult)

            @block.vector
            def _(dve):
                link = chain(dve, s_dve)
                dve.wait_ge(s_w, 128)
                u3 = [v["u"][:, h, :].rearrange("p (b l) -> p b l", l=L) for h in range(2)]
                x3 = [pre[:, h, :].rearrange("p (b l) -> p b l", l=L) for h in range(2)]
                for h in range(2):
                    dve.wait_ge(s_out, 4 * h + 4)
                    link(dve.tensor_scalar(v["u"][:, h, :], pre[:, h, :], cw[:, h, 3:4], cb[:, h:h + 1], ALU.mult,
                                           ALU.add))
                    for s in range(1, 4):
                        last = dve.scalar_tensor_tensor(out=u3[h][:, :, s:], in0=x3[h][:, :, :L - s],
                                                        scalar=cw[:, h, 3 - s:4 - s], in1=u3[h][:, :, s:],
                                                        op0=ALU.mult, op1=ALU.add)
                        if s < 3:
                            link(last)
                    last.then_inc(s_conv, 1)
                dve.wait_ge(s_sel, 1)
                link(dve.tensor_copy(v["sel"][64:128], v["sel32"][64:128]))
                dve.wait_ge(s_a, 1)
                link(dve.tensor_scalar(v["a"][:], v["a"][:], -1.0, None, ALU.mult))
                dve.wait_ge(v["s_wo"], 64)
                dve.tensor_reduce(wsum[:], raw[:], AX.X, ALU.add, apply_absolute_value=True).then_inc(s_wsum, 1)
                dve.wait_ge(s_xd, Q)
                hi, lo = v["bc"][64:96, :], v["bc"][96:128, :]
                link(dve.tensor_copy(hi, XD[64:96, :]))
                dve.tensor_tensor(lo, XD[64:96, :], hi.bitcast(F32), ALU.subtract)
                dve.wait_ge(s_wm, 1)
                link(dve.tensor_scalar(wscale[:], bank[:, 0, 0:3], 1.0 / (D * FD), 1e-5, ALU.mult, ALU.max))
                link(dve.reciprocal(wrec[:], wscale[:]))
                for k in range(3):
                    last = dve.tensor_scalar(raw[:, k, :], raw[:, k, :], wrec[:, k:k + 1], ROUND, ALU.mult, ALU.add)
                link(last)
                link(dve.tensor_scalar(raw[:], raw[:], ROUND - 1.0, ROUND + 1.0, ALU.max, ALU.min))
                dve.tensor_scalar(wq[:], raw[:], ROUND, None, ALU.subtract)
                for h in range(2):
                    e, t = neg[:, h, :], tiny[:, h, :]
                    dve.wait_ge(s_e, h + 1)
                    dve.tensor_scalar(mask[:, h, :], e, 1.0 / 32, None, ALU.is_lt)
                    dve.wait_ge(s_neg, h + 1)
                    for add in (1.0 / 3, -0.5, 1.0):
                        link(dve.scalar_tensor_tensor(out=t, in0=t, scalar=add, in1=e, op0=ALU.add, op1=ALU.mult))
                    dve.wait_ge(s_ln, h + 1)
                    link(dve.copy_predicated(v["delta"][:, h, :], mask[:, h, :], t))
                    dve.scalar_tensor_tensor(out=v["delta"][:, h, :], in0=z[:, h, :], scalar=0.0,
                                             in1=v["delta"][:, h, :], op0=ALU.max, op1=ALU.add).then_inc(s_sp, 1)
                dve.wait_ge(s_sp, 2)
                dve.tensor_tensor(v["du"][:, 1, :], v["delta"][:, 1, :], v["u"][:, 1, :], ALU.mult)


def ssm_scan_stage(nc, w, v):
    NBK = T // BLK
    NBB = BLK // L
    with ExitStack() as ctx:
        sb, ps, sem = place(nc, ctx, "ss")
        bs = w["O"][:, :, :].rearrange("p (a t) d -> p a (t d)", a=2)
        cs = w["N"][:, :, :].rearrange("p (a t) d -> p a (t d)", a=2)
        dA = sb("decay", [P, 2, 2, BLK])
        dB = sb("drive", [P, 2, 2, BLK])
        H = sb("states", [P, 2, 2, BLK])
        HC = sb("states_c", [P, 2, 2, BLK])
        Bp = ps("b_ps", [P, BLK])
        Cp = ps("c_ps", [P, BLK])
        Yp = [ps(f"y_ps{h}", [P, BLK]) for h in range(2)]
        s_bm, s_cm, s_b, s_c, s_da, s_db, s_h, s_hc, s_y, s_yu, s_yg, s_z = (
            sem(n) for n in ("b_ps", "c_ps", "b_spread", "c_spread", "decay", "drive", "states", "states_c",
                               "y_ps", "y_u", "y_gated", "decay_zero"))
        steps = [(k, n) for k in range(NBK) for n in range(NS)]
        with nc.Block() as block:
            @block.tensor
            def _(pe):
                def spread_bc(i):
                    k, n = steps[i]
                    for dst, row, full, out in ((Bp, n, s_bm, s_b), (Cp, NS + n, s_cm, s_c)):
                        wait(pe, out, i)
                        for c in range(BLK // 512):
                            cols = slice(k * BLK + c * 512, k * BLK + (c + 1) * 512)
                            last = pe.matmul(dst[:, c * 512:(c + 1) * 512], v["sel"][64:128, row, :],
                                             v["bc"][64:128, cols], start=True, stop=True)
                        last.then_inc(full, 1)

                def add_up(i):
                    k, n = steps[i]
                    if n == 0 and k > 0:
                        pe.wait_ge(s_yu, 2 * k)
                    for h in range(2):
                        pe.wait_ge(s_hc, 2 * i + h + 1)
                        for c in range(BLK // 512):
                            last = pe.matmul(Yp[h][:, c * 512:(c + 1) * 512], w["ident"][:],
                                             HC[:, i % 2, h, c * 512:(c + 1) * 512], start=(n == 0), stop=(n == NS - 1))
                        last.then_inc(s_y, 1)
                spread_bc(0)
                spread_bc(1)
                for i in range(len(steps)):
                    if i + 2 < len(steps):
                        spread_bc(i + 2)
                    add_up(i)

            @block.scalar
            def _(act):
                act.wait_ge(s_z, 1)
                for i, (k, n) in enumerate(steps):
                    act.wait_ge(s_bm, i + 1)
                    wait(act, s_db, 2 * i - 2)
                    act.activation(bs[:, i % 2, :], Bp[:], ACT.Copy).then_inc(s_b, 1)
                    for h in range(2):
                        wait(act, s_h, 2 * (i - 2) + h + 1)
                        act.activation(dA[:, i % 2, h, :].rearrange("p (b l) -> p b l", l=L)[:, :, 1:],
                                       v["delta"][:, h, k * BLK:(k + 1) * BLK].rearrange("p (b l) -> p b l", l=L)[:, :, 1:],
                                       ACT.Exp, scale=v["a"][:, h, n:n + 1]).then_inc(s_da, 1)
                    act.wait_ge(s_cm, i + 1)
                    wait(act, s_hc, 2 * i - 2)
                    act.activation(cs[:, i % 2, :], Cp[:], ACT.Copy).then_inc(s_c, 1)

            @block.vector
            def _(dve):
                for i in range(2):
                    last = dve.memset(dA[:, i].rearrange("p h (b l) -> p (h b) l", l=L)[:, :, 0:1], 0.0)
                last.then_inc(s_z, 1)

                def finish(k):
                    dve.wait_ge(s_y, 2 * NS * (k + 1))
                    c = slice(k * BLK, (k + 1) * BLK)
                    for h in range(2):
                        dve.scalar_tensor_tensor(out=v["du"][:, h, c], in0=v["u"][:, h, c], scalar=v["D"][:, h:h + 1],
                                                 in1=Yp[h][:], op0=ALU.mult, op1=ALU.add).then_inc(s_yu, 1)
                    dve.wait_ge(s_yu, 2 * (k + 1))
                    for h in range(2):
                        dve.tensor_tensor(v["du"][:, h, c], v["du"][:, h, c], v["gate"][:, h, c], ALU.mult)

                for i, (k, n) in enumerate(steps):
                    for h in range(2):
                        dve.wait_ge(s_b, i + 1)
                        wait(dve, s_h, 2 * (i - 2) + h + 1)
                        dve.tensor_tensor(dB[:, i % 2, h, :], v["du"][:, h, k * BLK:(k + 1) * BLK], bs[:, i % 2, :],
                                          ALU.mult).then_inc(s_db, 1)
                    for h in range(2):
                        dve.wait_ge(s_da, 2 * i + h + 1)
                        dve.wait_ge(s_db, 2 * i + h + 1)
                        wait(dve, s_hc, 2 * (i - 2) + h + 1)
                        dve.tensor_tensor_scan(H[:, i % 2, h, :], dA[:, i % 2, h, :], dB[:, i % 2, h, :], 0.0,
                                               ALU.mult, ALU.add).then_inc(s_h, 1)
                    if n == 1 and k > 0:
                        finish(k - 1)
                finish(NBK - 1)

            @block.gpsimd
            def _(pool):
                for i in range(len(steps)):
                    pool.wait_ge(s_c, i + 1)
                    for h in range(2):
                        pool.wait_ge(s_h, 2 * i + h + 1)
                        wait(pool, s_y, 2 * (i - 2) + h + 1)
                        pool.tensor_tensor(HC[:, i % 2, h, :], H[:, i % 2, h, :], cs[:, i % 2, :],
                                           ALU.mult).then_inc(s_hc, 1)


def ssm_out_stage(nc, w, v, old):
    with ExitStack() as ctx:
        sb, ps, sem = place(nc, ctx, "so")
        WO, s_w = v["WO"], v["s_wo"]
        wq, wscale = v["wq"], v["wscale"]
        idb = sb("ident_bf16", [P, P], BF16)
        R = sb("rows", [P, NT, D])
        Hn = sb("normed", [P, NT, D])
        stats = sb("stats", [P, 2, NT, 6])
        mv = sb("mean_var", [P, 2, NT, 2])
        ms = sb("mean_square", [P, 2, NT])
        rs = sb("rsqrt", [P, 2, NT])
        am = sb("abs_max", [P, 2, NT])
        ar = sb("abs_recip", [P, 2, NT])
        sc = sb("scales", [P, 3, NT])
        qa = sb("q_in", [P, NT, D])
        qb = sb("q_in_bf16", [P, NT, D], BF16)
        qT = sb("q_in_T", [P, T], BF16)
        gate = sb("gate", [P, 2, FD])
        gu = sb("gate_up", [P, 2, FD])
        g2 = sb("gate_up_rounded", [P, 2, FD])
        gb = sb("gate_up_bf16", [P, 2, FD], BF16)
        gT = sb("gate_up_T", [P, 2, 4, P], BF16)
        yb = ps("y_ps", [P, 2, NQ])
        gp = ps("gate_ps", [P, FD])
        up = [ps(f"up_ps{i}", [P, FD]) for i in range(2)]
        tb = ps("T_ps", [P, 2, 2 * FD], BF16)
        s_y, s_yout, s_dve, s_ms, s_rs, s_q, s_tm, s_qT, s_id = (
            sem(n) for n in ("y_ps", "y_out", "chain", "mean_square", "rsqrt", "rounded", "T_ps", "rounded_T", "ident"))
        s_gm, s_um, s_gate, s_gu, s_gq, s_gtm, s_gT, s_dm, s_dout, s_ms2, s_rs2, s_po = (
            sem(n) for n in ("gate_ps", "up_ps", "gate", "gate_up", "gu_rounded", "gu_T_ps", "gu_T", "down_ps",
                               "down_out", "mean_square2", "rsqrt2", "pool"))
        s_root = sem("root_chain")
        eps = sb("eps", [P, TQ])
        with nc.Block() as block:
            @block.gpsimd
            def _(pool):
                clear(pool, old)
                pool.memset(eps[:], 1e-6).then_inc(s_po, 1)
                pool.wait_ge(s_po, 1)
                link = chain(pool, s_root)
                for k, measured, done in ((0, s_ms, s_rs), (1, s_ms2, s_rs2)):
                    for q in range(Q):
                        c = slice(q * TQ, (q + 1) * TQ)
                        pool.wait_ge(measured, q + 1)
                        link(pool.tensor_tensor(ms[:, k, c], mv[:, k, c, 0], mv[:, k, c, 0], ALU.mult))
                        link(pool.tensor_tensor(ms[:, k, c], ms[:, k, c], mv[:, k, c, 1], ALU.add))
                        link(pool.tensor_tensor(ms[:, k, c], ms[:, k, c], eps[:], ALU.add))
                        pool.tensor_tensor(rs[:, k, c], ms[:, k, c], w["minus_half"][:, 0:TQ],
                                           ALU.pow).then_inc(done, 1)

            @block.tensor
            def _(pe):
                pe.wait_ge(s_w, 64)
                for q in range(Q):
                    if q >= 2:
                        pe.wait_ge(s_yout, q - 1)
                    for i in range(TQ):
                        t = q * TQ + i
                        for h in range(2):
                            last = pe.matmul(yb[:, q % 2, i * D:(i + 1) * D], v["du"][:, h, t * P:(t + 1) * P],
                                             WO[:, h, :], start=(h == 0), stop=(h == 1))
                    last.then_inc(s_y, 1)
                pe.wait_ge(s_id, 1)
                pe.wait_ge(s_q, 1)
                for k in range(2):
                    for i in range(8):
                        t = 8 * k + i
                        last = pe.transpose(tb[:, k, i * P:(i + 1) * P], qb[:, t, :], idb[:])
                    last.then_inc(s_tm, 1)
                pe.wait_ge(s_qT, 2)

                def gate_up(t):
                    wait(pe, s_gate, t)
                    pe.matmul(gp[:], qT[:, t * P:(t + 1) * P], wq[:, 0, :], start=True, stop=True).then_inc(s_gm, 1)
                    wait(pe, s_gu, t - 1)
                    pe.matmul(up[t % 2][:], qT[:, t * P:(t + 1) * P], wq[:, 1, :], start=True,
                              stop=True).then_inc(s_um, 1)
                gate_up(0)
                gate_up(1)
                for t0 in range(0, NT, 2):
                    if t0 + 2 < NT:
                        gate_up(t0 + 2)
                        gate_up(t0 + 3)
                    pe.wait_ge(s_gq, t0 // 2 + 1)
                    for t in (t0, t0 + 1):
                        wait(pe, s_gT, t - 1)
                        for c in range(4):
                            last = pe.transpose(tb[:, t % 2, c * P:(c + 1) * P], gb[:, t % 2, c * P:(c + 1) * P], idb[:])
                        last.then_inc(s_gtm, 1)
                    for t in (t0, t0 + 1):
                        pe.wait_ge(s_gT, t + 1)
                        wait(pe, s_dout, t - 1)
                        for c in range(4):
                            last = pe.matmul(yb[:, t % 2, 0:D], gT[:, t % 2, c, :], wq[:, 2, c * D:(c + 1) * D],
                                             start=(c == 0), stop=(c == 3))
                        last.then_inc(s_dm, 1)

            @block.scalar
            def _(act):
                for k in range(2):
                    act.wait_ge(s_tm, k + 1)
                    act.activation(qT[:, k * BLK:(k + 1) * BLK], tb[:, k, :], ACT.Copy).then_inc(s_qT, 1)
                def gates(t):
                    act.wait_ge(s_gm, t + 1)
                    wait(act, s_gu, t - 1)
                    act.activation(gate[:, t % 2, :], gp[:], ACT.Sigmoid, scale=sc[:, 0, t:t + 1]).then_inc(s_gate, 1)
                gates(0)
                gates(1)
                for t0 in range(0, NT, 2):
                    if t0 + 2 < NT:
                        gates(t0 + 2)
                        gates(t0 + 3)
                    for t in (t0, t0 + 1):
                        act.wait_ge(s_gtm, t + 1)
                        wait(act, s_dm, t - 1)
                        act.activation(gT[:, t % 2].rearrange("p c t -> p (c t)"), tb[:, t % 2, 0:FD],
                                       ACT.Copy).then_inc(s_gT, 1)

            @block.vector
            def _(dve):
                link = chain(dve, s_dve)
                over = lambda x, n=NT: x.rearrange("p (t o) -> p t o", o=1).to_broadcast([P, n, D])
                dve.tensor_copy(idb[:], w["ident"][:]).then_inc(s_id, 1)

                def rounded(dst, src, width):
                    lo, hi = width
                    link(dve.tensor_scalar(src, src, ROUND + lo, ROUND + hi, ALU.max, ALU.min))
                    return dve.tensor_scalar(dst, src, ROUND, None, ALU.subtract)

                def measure(k, q, sem):
                    for t in range(q * TQ, q * TQ + TQ):
                        last = dve.bn_stats(stats[:, k, t, :], R[:, t, :])
                    link(last)
                    for t in range(q * TQ, q * TQ + TQ):
                        last = dve.bn_aggr(mv[:, k, t, :], stats[:, k, t, :])
                    last.then_inc(sem, 1)

                for q in range(Q):
                    a, b = q * TQ, q * TQ + TQ
                    dve.wait_ge(s_y, q + 1)
                    dve.tensor_tensor(R[:, a:b, :], yb[:, q % 2, :].rearrange("p (t d) -> p t d", d=D),
                                      w["Y"][:, a:b, :], ALU.add).then_inc(s_yout, 1)
                    dve.wait_ge(s_yout, q + 1)
                    measure(0, q, s_ms)
                for t in range(NT):
                    if t % TQ == 0:
                        dve.wait_ge(s_rs, t // TQ + 1)
                    last = dve.scalar_tensor_tensor(out=Hn[:, t, :], in0=R[:, t, :], scalar=rs[:, 0, t:t + 1],
                                                    in1=w["norm1_row"][:], op0=ALU.mult, op1=ALU.mult)
                link(last)
                link(dve.tensor_reduce(am[:, 0, :], Hn[:], AX.X, ALU.max, apply_absolute_value=True))
                link(dve.tensor_scalar(am[:, 0, :], am[:, 0, :], 1e-5, None, ALU.max))
                link(dve.reciprocal(ar[:, 0, :], am[:, 0, :]))
                link(dve.tensor_scalar(ar[:, 0, :], ar[:, 0, :], 127.0, None, ALU.mult))
                for t in range(NT):
                    last = dve.tensor_scalar(qa[:, t, :], Hn[:, t, :], ar[:, 0, t:t + 1], ROUND, ALU.mult, ALU.add)
                link(last)
                for k in range(2):
                    link(dve.tensor_scalar(sc[:, k, :], am[:, 0, :], wscale[:, k:k + 1], 1.0 / 127, ALU.mult, ALU.mult))
                rounded(qb[:], qa[:], (-128.0, 127.0)).then_inc(s_q, 1)

                def second(tiles):
                    t0 = tiles[0]
                    for t in tiles:
                        dve.wait_ge(s_gate, t + 1)
                        dve.wait_ge(s_um, t + 1)
                        dve.scalar_tensor_tensor(out=gu[:, t % 2, :], in0=up[t % 2][:], scalar=sc[:, 1, t:t + 1],
                                                 in1=gate[:, t % 2, :], op0=ALU.mult, op1=ALU.mult).then_inc(s_gu, 1)
                    a, r = am[:, 1, t0:t0 + 2], ar[:, 1, t0:t0 + 2]
                    dve.wait_ge(s_gu, t0 + 2)
                    link(dve.tensor_reduce(a, gu[:], AX.X, ALU.max, apply_absolute_value=True))
                    link(dve.tensor_scalar(a, a, 1e-5, None, ALU.max))
                    link(dve.reciprocal(r, a))
                    link(dve.tensor_scalar(r, r, 127.0, None, ALU.mult))
                    for t in tiles:
                        last = dve.tensor_scalar(g2[:, t % 2, :], gu[:, t % 2, :], ar[:, 1, t:t + 1], ROUND, ALU.mult,
                                                 ALU.add)
                    dve.tensor_scalar(sc[:, 2, t0:t0 + 2], a, wscale[:, 2:3], 1.0 / 127, ALU.mult, ALU.mult)
                    link(last)
                    wait(dve, s_gtm, t0)
                    rounded(gb[:], g2[:], (-128.0, 127.0)).then_inc(s_gq, 1)

                def third(t):
                    dve.wait_ge(s_dm, t + 1)
                    dve.scalar_tensor_tensor(out=R[:, t, :], in0=yb[:, t % 2, 0:D], scalar=sc[:, 2, t:t + 1],
                                             in1=Hn[:, t, :], op0=ALU.mult, op1=ALU.add).then_inc(s_dout, 1)
                for t in range(0, NT + 2, 2):
                    if t < NT:
                        second((t, t + 1))
                    if t >= 2:
                        third(t - 2)
                        third(t - 1)
                dve.wait_ge(s_dout, NT)
                for q in range(Q):
                    measure(1, q, s_ms2)
                for t in range(NT):
                    if t % TQ == 0:
                        dve.wait_ge(s_rs2, t // TQ + 1)
                    last = dve.scalar_tensor_tensor(out=Hn[:, t, :], in0=R[:, t, :], scalar=rs[:, 1, t:t + 1],
                                                    in1=w["norm2_row"][:], op0=ALU.mult, op1=ALU.mult)
                link(last)
                dve.tensor_tensor(w["X"][:], w["X"][:], Hn[:], ALU.add)


def ssm_stages(nc, w, pre):
    with ExitStack() as ctx:
        sb, ps, sem = place(nc, ctx, "ssm")
        v = dict(pre)
        v["wq"] = w["QT"][:, 0:3 * FD // 2].bitcast(BF16).rearrange("p (k f) -> p k f", k=3)
        v["wscale"] = sb("w_scale", [P, 3])
        for name in ("u", "gate", "delta", "du"):
            v[name] = sb(name, [P, 2, T])
        with ExitStack() as inner:
            sb, ps, sem = place(nc, inner, "ssmi")
            v["bc"] = sb("bc", [P, T], F32R)
            v["sel"] = sb("sel", [P, 2 * NS, P], F32R)
            with ExitStack() as tmp:
                v["sel32"] = place(nc, tmp, "ssmt")[0]("sel32", [P, 2 * NS, P])
                ssm_in_stage(nc, w, v, w["old"])
            old = [s for s in ended() if s is not v["s_wo"]]
            ssm_scan_stage(nc, w, v)
        ssm_out_stage(nc, w, v, old)


def prepare_stage(nc, w, ins):
    parts = {
        "M": ("L0_xattn_WqT", "L0_xattn_WkT", 16, 8, w["M0"]),
        "M1": ("L1_xattn_WqT", "L1_xattn_WkT", 64, 16, w["M1"]),
        "VO": ("L1_xattn_WvT", "L1_xattn_Wo", 64, 16, w["VO"]),
    }
    with ExitStack() as ctx:
        sb, ps, sem = place(nc, ctx, "prep")
        ops = {}
        for name, (a, b, k, h, _) in parts.items():
            ops[name] = (sb(f"{name}_a", [k, h, D]), sb(f"{name}_b", [k, h, D]))
        bank = [ps(f"fold{i}", [P, 512]) for i in range(2)]
        s_in = {name: sem(f"in_{name}") for name in parts}
        s_small, s_id, s_mm, s_out = sem("small"), sem("ident"), sem("folded_ps"), sem("folded")
        s_x = sem("x")
        small = []
        with nc.Block() as block:
            @block.sync
            def _(sp):
                for q in range(Q):
                    sp.dma_start(w["X"][:, q * TQ:(q + 1) * TQ, :],
                                 ins["x"].rearrange("(t a) l d -> (a l) t d", a=BT)[:, q * TQ:(q + 1) * TQ, :]).then_inc(s_x, 16)
                for name, (a, b, k, h, _) in parts.items():
                    for buf, src in zip(ops[name], (a, b)):
                        sp.dma_start(buf[:], ins[src].rearrange("h c d -> c h d")).then_inc(s_in[name], 16)
                sp.wait_ge(s_x, 16 * Q)

            @block.scalar
            def _(act):
                n = 0
                for key, src in (("pre_g", "L0_xattn_pre_g"), ("pre_b", "L0_xattn_pre_b"), ("ln_g", "L0_xattn_ln_g"),
                                 ("ln_b", "L0_xattn_ln_b"), ("ln2_w", "L1_xattn_ln2_w"), ("ln2_b", "L1_xattn_ln2_b")):
                    act.dma_start(w[key][:], ins[src].rearrange("(p o) -> p o", o=1)).then_inc(s_small, 16)
                    n += 1
                for key, src in (("ln1_w", "L1_xattn_ln1_w"), ("ln1_b", "L1_xattn_ln1_b"),
                                 ("ln_g_row", "L0_xattn_ln_g"), ("ln_b_row", "L0_xattn_ln_b"),
                                 ("ln2_w_row", "L1_xattn_ln2_w"), ("ln2_b_row", "L1_xattn_ln2_b"),
                                 ("norm1_row", "L1_attn_norm1_w"), ("norm2_row", "L1_attn_norm2_w")):
                    act.dma_start(w[key][:], ins[src].rearrange("(o d) -> o d", o=1).to_broadcast([P, D])).then_inc(s_small, 16)
                    n += 1
                for key, src in (("V0", "L0_xattn_Wv"), ("Wo0", "L0_xattn_Wo")):
                    act.dma_start(w[key][:], ins[src]).then_inc(s_small, 16)
                    n += 1
                k = 0
                for name, (_, _, _, h, dst) in parts.items():
                    for c in range(h // 4):
                        act.wait_ge(s_mm, k + 1)
                        act.activation(dst[:, 4 * c:4 * c + 4, :], bank[k % 2][:, :].rearrange("p (h d) -> p h d", h=4),
                                       ACT.Copy, scale=0.125 if name == "M1" else 1.0).then_inc(s_out, 1)
                        k += 1
                act.wait_ge(s_small, 16 * n)

            @block.tensor
            def _(pe):
                k = 0
                for name, (_, _, _, h, _) in parts.items():
                    a, b = ops[name]
                    pe.wait_ge(s_in[name], 32)
                    for c in range(h // 4):
                        if k >= 2:
                            pe.wait_ge(s_out, k - 1)
                        for i in range(4):
                            last = pe.matmul(bank[k % 2][:, i * D:(i + 1) * D], a[:, 4 * c + i, :], b[:, 4 * c + i, :],
                                             start=True, stop=True)
                        last.then_inc(s_mm, 1)
                        k += 1

            @block.gpsimd
            def _(pool):
                pool.memset(w["minus_half"][:], -0.5)
                pool.memset(w["eps"][:], EPS5)
                pool.memset(w["zero"][:], 0.0)
                pool.memset(w["ident"][:], 0.0).then_inc(s_id, 1)
                pool.wait_ge(s_id, 1)
                pool.affine_select(out=w["ident"][:], in_=w["ident"][:], compare_op=ALU.not_equal, fill=1.0, base=0,
                                   pattern=[[-1, P]], channel_multiplier=1).then_inc(s_id, 1)


def build(nc, ins, out, upto=99, dbg=None):
    with ExitStack() as ctx:
        sb, ps, sem = place(nc, ctx, "all")
        w = {}
        folded = ExitStack()
        del TAKEN[:]
        for name, shape in (("X", [P, NT, D]), ("O", [P, NT, D]), ("Y", [P, NT, D]), ("N", [P, NT, D]), ("QT", [P, T]),
                            ("ident", [P, P]), ("minus_half", [P, NT]), ("eps", [P, 4]), ("zero", [P, 4]), ("pre_g", [D, 1]), ("pre_b", [D, 1]),
                            ("ln_g", [D, 1]), ("ln_b", [D, 1]), ("ln2_w", [D, 1]), ("ln2_b", [D, 1]),
                            ("ln1_w", [P, D]), ("ln1_b", [P, D]), ("ln_g_row", [P, D]), ("ln_b_row", [P, D]),
                            ("ln2_w_row", [P, D]), ("ln2_b_row", [P, D]), ("norm1_row", [P, D]), ("norm2_row", [P, D])):
            w[name] = sb(name, shape)
        fold_sb, _, _ = place(nc, folded, "all")
        for name, shape in (("M0", [P, 8, D]), ("M1", [P, 16, D]), ("VO", [P, 16, D]), ("V0", [D, D]),
                            ("Wo0", [D, D])):
            w[name] = fold_sb(name, shape)
        dram = {
            "ctx": ins["ctx_1024"],
            "kv_a": nc.dram_tensor("kv_a", (B, KC, 2 * D), F32, kind="Internal").ap(),
            "kv_b": nc.dram_tensor("kv_b", (B, KR, D), F32, kind="Internal").ap(),
            "kv_lat": nc.dram_tensor("kv_lat", (B, L, D), F32, kind="Internal").ap(),
        }
        def finish(buf):
            s_done = sem("result_stored")
            with nc.Block() as block:
                @block.sync
                def _(sp):
                    for q in range(Q):
                        sp.dma_start(out.rearrange("(t a) l d -> (a l) t d", a=BT)[:, q * TQ:(q + 1) * TQ, :],
                                     buf[:, q * TQ:(q + 1) * TQ, :]).then_inc(s_done, 16)
                    sp.wait_ge(s_done, 16 * Q)

        prepare_stage(nc, w, ins)
        norm_stage(nc, w, "q0", w["X"], w["Y"], w["QT"], gain=w["pre_g"], shift=w["pre_b"], twice=True)
        w["M"], w["V"] = w["M0"], w["V0"]
        attention_stage(nc, w, 0, dram)
        if upto == 1:
            folded.close()
            return finish(w["O"][:])
        norm_stage(nc, w, "o0", w["O"], w["Y"], w["QT"], gain=w["ln_g"], shift=w["ln_b"],
                   row_affine=(w["ln_g_row"], w["ln_b_row"]), rows_out=w["N"])
        gelu_stage(nc, w)
        if upto == 2:
            folded.close()
            return finish(w["X"][:])
        with ExitStack() as pre:
            weights = self_attention_weights(nc, pre, ins)
            norm_stage(nc, w, "sa_n", w["X"], w["Y"], w["QT"], first=weights["first"])
            self_attention_stage(nc, w, weights)
        if upto == 3:
            folded.close()
            return finish(w["X"][:])
        old = ended()
        with ExitStack() as pre:
            weights = moe_weights(nc, pre, ins, 0)
            norm_stage(nc, w, "moe0_n", w["X"], w["Y"], w["QT"], first=weights["first"])
            moe_stage(nc, w, weights, 0, old)
        if upto == 4:
            folded.close()
            return finish(w["X"][:])
        norm_stage(nc, w, "q1", w["X"], w["Y"], w["QT"], gain=w["ln2_w"], shift=w["ln2_b"], twice=True,
                   row_affine=(w["ln2_w_row"], w["ln2_b_row"]), rows_out=w["N"],
                   rows_T=dram["kv_lat"].rearrange("(t a) l d -> t (a l) d", a=BT))
        w["M"], w["V"] = w["M1"], w["VO"]
        attention_stage(nc, w, 1, dram)
        folded.close()
        w["old"] = ended()
        with ExitStack() as pre:
            weights = ssm_weights(nc, pre, ins)
            norm_stage(nc, w, "ssm_n", w["X"], w["Y"], w["QT"], add=w["O"], first=weights["first"])
            if upto == 5:
                return finish(w["X"][:])
            ssm_stages(nc, w, weights)
        if upto == 6:
            return finish(w["X"][:])
        with ExitStack() as pre:
            weights = moe_weights(nc, pre, ins, 1)
            norm_stage(nc, w, "moe1_n", w["X"], w["Y"], w["QT"], first=weights["first"])
            moe_stage(nc, w, weights, 1, [])
        finish(w["X"][:])


def layout(inputs):
    a = {k: np.asarray(v) for k, v in inputs.items()}
    wkv = a["L1_xattn_Wkv"]
    inner = wkv.shape[1] // 2

    def heads(m, h):
        return np.ascontiguousarray(m.T.reshape(h, -1, m.shape[0]))

    out = {
        "x": a["x"], "ctx_1024": a["ctx_1024"],
        "L0_xattn_WqT": heads(a["L0_xattn_Wq"], 8), "L0_xattn_WkT": heads(a["L0_xattn_Wk"], 8),
        "L1_xattn_WqT": heads(a["L1_xattn_Wq"], 16), "L1_xattn_WkT": heads(wkv[:, :inner], 16),
        "L1_xattn_WvT": heads(wkv[:, inner:], 16), "L1_xattn_Wo": a["L1_xattn_Wo"].reshape(16, 64, D),
    }
    for k in ("L0_xattn_Wv", "L0_xattn_Wo", "L0_xattn_pre_g", "L0_xattn_pre_b", "L0_xattn_ln_g", "L0_xattn_ln_b",
              "L1_xattn_ln1_w", "L1_xattn_ln1_b", "L1_xattn_ln2_w", "L1_xattn_ln2_b", "L1_attn_norm1_w",
              "L1_attn_norm2_w"):
        out[k] = a[k]
    for k in ("q", "k", "v"):
        out[f"L0_attn_w{k}T"] = a[f"L0_attn_w{k}"].T
    out["moe0_router_T"], out["moe1_router_T"] = a["L0_ffn_router_w"].T, a["L1_ffn_Wr"].T
    out["moe0_w_in_T"] = a["L0_ffn_w1"].transpose(0, 2, 1)
    out["moe0_w_out_T"] = a["L0_ffn_w2"].transpose(0, 2, 1)
    out["moe1_w_in_T"] = np.stack([a["L1_ffn_Wg"], a["L1_ffn_Wu"]], 1).transpose(0, 1, 3, 2).reshape(16, D, 4 * D)
    out["moe1_w_out_T"] = a["L1_ffn_Wd"].transpose(0, 2, 1)
    out["in_proj_T"], out["out_proj_T"] = a["L1_attn_in_proj_w"].T, a["L1_attn_out_proj_w"].T
    out["x_proj_T"], out["dt_proj_T"] = a["L1_attn_x_proj_w"].T, a["L1_attn_dt_proj_w"].T
    for k in ("gate", "up", "down"):
        out[f"{k}_T"] = a[f"L1_attn_{k}_w"].T
    for k in ("conv_w", "conv_b", "dt_proj_b", "A_log", "D"):
        out[k] = a[f"L1_attn_{k}"]
    return {k: np.ascontiguousarray(v) for k, v in out.items()}


def kernel(**inputs):
    import concourse.bacc as _bacc
    from concourse.bass_utils import run_bass_kernel_spmd as _run

    nc = _bacc.Bacc("TRN2", target_bir_lowering=False, num_devices=1)
    arrays, ins = {}, {}
    for name, a in layout(inputs).items():
        arrays[f"in_{name}"] = a
        ins[name] = nc.dram_tensor(f"in_{name}", a.shape, mybir.dt.from_np(a.dtype), kind="ExternalInput").ap()
    out = nc.dram_tensor("out_x", (B, L, D), F32, kind="ExternalOutput").ap()
    build(nc, ins, out)
    r = _run(nc, [arrays], core_ids=[0])
    return r.results[0]["out_x"]
```

```python
from contextlib import ExitStack

import numpy as np

import concourse.bass as bass
from concourse import mybir

F32 = mybir.dt.float32
F32R = mybir.dt.float32r
BF16 = mybir.dt.bfloat16
I32 = mybir.dt.int32
ALU = mybir.AluOpType
ACT = mybir.ActivationFunctionType
AX = mybir.AxisListType

P = 128
D = 128
B = 64
L = 32
T = B * L
NT = T // P
BT = P // L
S_CTX = 257
KC = 86
KR = S_CTX - 2 * KC
EPS5 = 1e-5


def chain(eng, sem):
    count = [0]

    def link(ins):
        ins.then_inc(sem, 1)
        count[0] += 1
        eng.wait_ge(sem, count[0])
    return link


TAKEN = []


def place(nc, ctx, tag):
    def sb(name, shape, dt=F32):
        return ctx.enter_context(nc.sbuf_tensor(f"{tag}_{name}", shape, dt))

    def ps(name, shape, dt=F32):
        return ctx.enter_context(nc.psum_tensor(f"{tag}_{name}", shape, dt))

    def sem(name):
        s = ctx.enter_context(nc.semaphore(f"{tag}_{name}"))
        if tag != "all":
            TAKEN.append(s)
        return s
    return sb, ps, sem


def ended():
    old = list(TAKEN)
    del TAKEN[:]
    return old


def clear(pool, old):
    for s in old:
        pool.sem_clear(s)


def wait(eng, sem, value):
    if isinstance(value, int) and value <= 0:
        return
    eng.wait_ge(sem, value)


def attention_stage(nc, w, cross, dram):
    first = cross == 0
    tag = f"x{cross}"
    UB = 1 if first else 2
    NU = BT * UB
    GB = 2
    NUB = NU * GB
    NB = BT * GB
    TURNS = NT // GB
    KEYS = S_CTX if first else S_CTX + L
    rows = [KC, KC, KR if first else KR + L]
    cols = [0, KC, 2 * KC]
    pieces = 2 * UB
    HPG = BT + pieces
    ZPG = NU + 1
    scale = float(D) ** -0.5 if first else 1.0
    LA = 3 if first else 2
    H0 = LA + pieces
    CTX_DMAS = 2 if first else 3
    fold_slot = 0 if first else 1

    with ExitStack() as ctx:
        sb, ps, sem = place(nc, ctx, tag)
        KMAX = KC if first else rows[2]
        Cx = sb("ctx_rows", [max(KMAX, KC), NB, 3, D])
        PARTS = (("", F32),) if first else (("_hi", F32R), ("_lo", F32R))
        KW = KEYS + KEYS % 2 if not first else KEYS
        KT = [sb(f"keys_T{n}", [P, 2, KW], t) for n, t in PARTS]
        QF = [sb(f"folded_q{n}", [P, GB, BT, 8 * UB, L], t) for n, t in PARTS]
        Pr = sb("probs", [P, 2, 2, KEYS])
        PT = [sb(f"probs_T{n}", [max(KMAX, KC), 2, 3, 256], t) for n, t in PARTS]
        CV = [Cx] if first else [sb(f"ctx_rows{n}", [KMAX, 4, 3, D], t) for n, t in PARTS]
        PAIRS = ((0, 0),) if first else ((0, 0), (0, 1), (1, 0))
        ZT = sb("values_T", [P, 8 * UB, BT, L])
        NM = sb("neg_max", [P, 2, 2])
        DEN = sb("denominator", [P, 2, 2])
        RD = sb("recip_den", [P, 2, 2])
        S = [ps(f"scores{i}", [P, 2, 512]) for i in range(2)]
        Tp = ps("probs_T_ps", [P, 2, 512])
        Hp = ps("keys_T_ps", [P, 512])
        Zp = ps("values_ps", [P, 512])
        s_ctx = [sem(f"ctx_loaded{i}") for i in range(NB)]
        s_hfull, s_hfree = sem("h_bank_full"), sem("h_bank_free")
        s_zfull, s_zfree = sem("z_bank_full"), sem("z_bank_free")
        s_s, s_max, s_exp, s_rd, s_p = (sem(n) for n in ("scores", "max", "exp", "recip", "probs"))
        s_t, s_pt, s_zero = sem("probs_T_ps"), sem("probs_T"), sem("ctx_zeroed")
        if first:
            Hat = sb("normed_rows", [KC, 4, 3, D])
            Sc = sb("clipped", [P, 2, KEYS])
            stats = sb("stats", [KC, 2, 3, 6])
            mv = sb("mean_var", [KC, 4, 3, 2])
            var = sb("var_eps", [KC, 2, 3])
            rstd = sb("rstd", [KC, 4, 3])
            s_clip, s_bn, s_stats, s_var, s_rstd, s_hat = (
                sem(n) for n in ("clipped", "bn_stats", "mean_var", "var_eps", "rstd", "normed"))
            s_store = [sem(f"rows_stored{i}") for i in range(4)]
        else:
            s_gain, s_aff = sem("rows_gained"), sem("key_rows")
            s_hhi, s_phi, s_chi, s_clo, s_pad = (
                sem(n) for n in ("h_bank_hi", "probs_T_hi", "ctx_hi", "ctx_lo", "keys_padded"))

        def unit(g, j):
            return g * NUB + j

        def batch(g, i):
            return g * NB + i

        def z_before(g, j):
            return g * (ZPG * GB) + j + j // NU

        def o_before(g, grp):
            return g * (ZPG * GB) + grp * ZPG - 1

        def h_kt_before(g, i):
            grp, r = i // BT, i % BT
            skip = min(r, 2) if first else (0, 1, 3, 4)[r]
            if isinstance(g, int) and g * GB + grp == NT - 1:
                skip = 0
            return g * (HPG * GB) + grp * HPG + r + skip + H0

        def h_piece_before(g, grp, n):
            return g * (HPG * GB) + grp * HPG + H0 + n + (n + 1 if first else (n + 1) // 2 + 1)

        def keys_out(g, i):
            if isinstance(g, int) and g * NB + i < LA:
                n = g * NB + i
                return pieces + n + 1
            if i >= LA:
                return h_kt_before(g, i - LA) + 1
            return h_kt_before(g - 1, i - LA + NB) + 1

        def run(eng, body):
            body(0, True, False)
            with eng.Fori(1, TURNS - 1) as g:
                body(g, False, False)
            body(TURNS - 1, False, True)

        def par(j):
            return j % 2

        with nc.Block() as block:

            @block.sync
            def _(sp):
                def load(g, i):
                    n = i % NB
                    b = batch(g, i)
                    if not (isinstance(g, int) and g * NB + i < NB):
                        wait(sp, s_zfull, z_before(g, (i - NB) * UB + UB - 1) + 1)
                    if isinstance(b, int) and b < NB:
                        sp.wait_ge(s_zero, 1)
                    if first:
                        src = dram["ctx"][bass.ds(b, 1), 0:2 * KC, :].rearrange("b (c p) d -> (b p) c d", p=KC)
                        sp.dma_start(Cx[0:KC, n, 0:2, :], src).then_inc(s_ctx[n], 16)
                        src = dram["ctx"][bass.ds(b, 1), 2 * KC:S_CTX, :].rearrange("b p d -> (b p) d")
                        sp.dma_start(Cx[0:KR, n, 2, :], src).then_inc(s_ctx[n], 16)
                    else:
                        src = dram["kv_a"][bass.ds(b, 1), :, :].rearrange("b p (c d) -> (b p) c d", c=2)
                        sp.dma_start(Cx[0:KC, n, 0:2, :], src).then_inc(s_ctx[n], 16)
                        src = dram["kv_b"][bass.ds(b, 1), :, :].rearrange("b p d -> (b p) d")
                        sp.dma_start(Cx[0:KR, n, 2, :], src).then_inc(s_ctx[n], 16)
                        src = dram["kv_lat"][bass.ds(b, 1), :, :].rearrange("b p d -> (b p) d")
                        sp.dma_start(Cx[KR:KR + L, n, 2, :], src).then_inc(s_ctx[n], 16)

                def store(g, i):
                    b = batch(g, i)
                    wait(sp, s_hat, b + 1)
                    sp.dma_start(dram["kv_a"][bass.ds(b, 1), :, :].rearrange("b p (c d) -> (b p) c d", c=2),
                                 Hat[:, i % 4, 0:2, :]).then_inc(s_store[i % 4], 16)
                    sp.dma_start(dram["kv_b"][bass.ds(b, 1), :, :].rearrange("b p d -> (b p) d"),
                                 Hat[0:KR, i % 4, 2, :]).then_inc(s_store[i % 4], 16)

                ahead = 6 if first else 3
                for i in range(ahead):
                    load(0, i)
                if first:
                    for i in range(4):
                        store(0, i)

                def body(g, is_first, is_last):
                    for i in range(NB):
                        if not (is_last and i + ahead >= NB):
                            load(g, i + ahead)
                        if first and not (is_last and i + 4 >= NB):
                            store(g, i + 4)
                run(sp, body)
                if first:
                    for q in s_store:
                        sp.wait_ge(q, 32 * B // 4)

            @block.tensor
            def _(pe):
                def keys_T(g, i, before):
                    wait(pe, s_hat if first else s_aff, batch(g, i) + 1)
                    wait(pe, s_hfree, before)
                    src = Hat[:, i % 4] if first else Cx[:, i % NB]
                    for c in range(3):
                        last = pe.transpose(Hp[:, cols[c]:cols[c] + rows[c]], src[0:rows[c], c, :],
                                            w["ident"][0:rows[c], 0:rows[c]])
                    last.then_inc(s_hfull, 1)

                def fold_q(g, grp, n, before):
                    wait(pe, s_hfree, before)
                    rhs = w["QT"][:, bass.ds((g * GB + grp) * P, P)]
                    for h in range(4):
                        last = pe.matmul(Hp[:, h * P:(h + 1) * P], w["M"][:, 4 * n + h, :], rhs,
                                         start=True, stop=True)
                    last.then_inc(s_hfull, 1)

                def scores(g, j):
                    i = j // UB
                    if j % UB == 0:
                        wait(pe, s_hfree, keys_out(g, i))
                    if j % NU == 0:
                        wait(pe, s_hfree, fold_done(g, j // NU))
                    wait(pe, s_clip if first else s_exp, unit(g, j) - 1)
                    for r in range(2):
                        h0 = 8 * (j % UB) + 4 * r
                        for n, (a, b) in enumerate(PAIRS):
                            lhsT = QF[a][:, j // NU % GB, i % BT, h0:h0 + 4, :].rearrange("p h l -> p (h l)")
                            last = pe.matmul(S[par(j)][:, r, 0:KW], lhsT, KT[b][:, i % 2, :], start=(n == 0),
                                             stop=(n == len(PAIRS) - 1))
                    last.then_inc(s_s, 1)

                def fold_done(g, grp):
                    if isinstance(g, int) and g == 0 and grp == 0:
                        return pieces
                    if grp >= 1:
                        return h_piece_before(g, grp - 1, pieces - 1) + 1
                    return h_piece_before(g - 1, GB - 1, pieces - 1) + 1

                def probs_T(g, j):
                    wait(pe, s_p, unit(g, j) + 1)
                    wait(pe, s_pt, unit(g, j))
                    for r in range(2):
                        for c in range(3):
                            o = c * 256 + r * P
                            last = pe.transpose(Tp[0:rows[c], o // 512, o % 512:o % 512 + P],
                                                Pr[:, par(j), r, cols[c]:cols[c] + rows[c]], w["ident"][:])
                    last.then_inc(s_t, 1)

                def values(g, j):
                    i = j // UB
                    wait(pe, s_pt, unit(g, j) + 1)
                    wait(pe, s_zfree, z_before(g, j))
                    if not first:
                        wait(pe, s_clo, batch(g, i) + 1)
                    for c in range(3):
                        for n, (a, b) in enumerate(PAIRS):
                            last = pe.matmul(Zp[:, 0:256], CV[a][0:rows[c], i % (NB if first else 4), c, :],
                                             PT[b][0:rows[c], par(j), c, :], start=(c == 0 and n == 0),
                                             stop=(c == 2 and n == len(PAIRS) - 1))
                    last.then_inc(s_zfull, 1)

                def outputs(g, grp):
                    wait(pe, s_zfree, o_before(g, grp))
                    for h in range(8 * UB):
                        lhsT = ZT[:, h].rearrange("p b l -> p (b l)")
                        if first:
                            last = pe.matmul(Zp[:, 16 * h:16 * h + 16], lhsT, w["V"][:, 16 * h:16 * h + 16],
                                             start=True, stop=True)
                        else:
                            last = pe.matmul(Zp[:, 0:D], lhsT, w["V"][:, h, :], start=(h == 0),
                                             stop=(h == 8 * UB - 1))
                    last.then_inc(s_zfull, 1)

                for n in range(pieces):
                    fold_q(0, 0, n, n)
                keys_T(0, 0, pieces)
                keys_T(0, 1, pieces + 1)
                if not first:
                    pe.wait_ge(s_pad, 1)
                scores(0, 0)
                if LA == 3:
                    keys_T(0, 2, 2 + pieces)
                scores(0, 1)

                def body(g, is_first, is_last):
                    for j in range(NUB):
                        grp, r = j // NU, j % NU
                        more_groups = not (is_last and grp == GB - 1)
                        piece = r - fold_slot
                        folds = more_groups and 0 <= piece < pieces
                        early = not first or piece == pieces - 1

                        def keys_ahead():
                            if j % UB == 0 and not (is_last and j // UB + LA >= NB):
                                keys_T(g, j // UB + LA, h_kt_before(g, j // UB))

                        def scores_ahead():
                            if not (is_last and j + 2 >= NUB):
                                scores(g, j + 2)
                        if first:
                            probs_T(g, j)
                            scores_ahead()
                            keys_ahead()
                        else:
                            keys_ahead()
                            scores_ahead()
                            probs_T(g, j)
                        if r == 1 and not (is_first and grp == 0):
                            outputs(g, grp)
                        if folds and early:
                            fold_q(g, grp + 1, piece, h_piece_before(g, grp, piece))
                        if not (is_first and j == 0):
                            values(g, j - 1)
                        if folds and not early:
                            fold_q(g, grp + 1, piece, h_piece_before(g, grp, piece))
                run(pe, body)
                values(TURNS - 1, NUB - 1)
                outputs(TURNS, 0)

            @block.scalar
            def _(act):
                def keys_T(g, i, before):
                    wait(act, s_hfull, before + 1)
                    wait(act, s_s, unit(g, (i - 2) * UB + UB - 1) + 1)
                    if first:
                        act.activation(KT[0][:, i % 2, :], Hp[:, 0:KEYS], ACT.Identity, bias=w["pre_b"][:, 0:1],
                                       scale=w["pre_g"][:, 0:1]).then_inc(s_hfree, 1)
                    else:
                        act.activation(KT[0][:, i % 2, 0:KEYS], Hp[:, 0:KEYS], ACT.Copy).then_inc(s_hhi, 1)

                def fold_q(grp, n, before):
                    wait(act, s_hfull, before + 1)
                    act.activation(QF[0][:, grp % GB, :, 4 * n:4 * n + 4, :].rearrange("p b h l -> p h b l"),
                                   Hp[:, :].rearrange("p (h b l) -> p h b l", h=4, b=BT), ACT.Copy,
                                   scale=scale).then_inc(s_hfree if first else s_hhi, 1)

                def exps(g, j):
                    wait(act, s_max, unit(g, j) + 1)
                    wait(act, s_t, unit(g, j) - 1)
                    src = Sc if first else S[par(j)]
                    for r in range(2):
                        last = act.activation(Pr[:, par(j), r, :], src[:, r, 0:KEYS], ACT.Exp,
                                              bias=NM[:, par(j), r:r + 1], accum_out=DEN[:, par(j), r:r + 1])
                    last.then_inc(s_exp, 1)

                def probs_T(g, j):
                    wait(act, s_t, unit(g, j) + 1)
                    wait(act, s_zfull, z_before(g, j - 2) + 1)
                    src = Tp[0:KMAX].rearrange("p a (b c) -> p (a b) c", b=2)[:, 0:3, :]
                    act.activation(PT[0][:, par(j)], src, ACT.Copy).then_inc(s_pt if first else s_phi, 1)

                def values(g, j):
                    wait(act, s_zfull, z_before(g, j) + 1)
                    h0 = 8 * (j % UB)
                    act.activation(ZT[:, h0:h0 + 8, (j // UB) % BT, :],
                                   Zp[:, 0:256].rearrange("p (h l) -> p h l", h=8), ACT.Copy).then_inc(s_zfree, 1)

                def outputs(g, grp):
                    wait(act, s_zfull, o_before(g, grp) + 1)
                    act.activation(w["O"][:, bass.ds(g * GB + grp - 1, 1), :].rearrange("p a d -> p (a d)"),
                                   Zp[:, 0:D], ACT.Copy).then_inc(s_zfree, 1)

                for n in range(pieces):
                    fold_q(0, n, n)
                keys_T(0, 0, pieces)
                keys_T(0, 1, pieces + 1)
                if LA == 3:
                    keys_T(0, 2, 2 + pieces)
                exps(0, 0)
                exps(0, 1)

                def body(g, is_first, is_last):
                    for j in range(NUB):
                        grp, r = j // NU, j % NU
                        more_groups = not (is_last and grp == GB - 1)
                        piece = r - fold_slot
                        folds = more_groups and 0 <= piece < pieces

                        def keys_ahead():
                            if j % UB == 0 and not (is_last and j // UB + LA >= NB):
                                keys_T(g, j // UB + LA, h_kt_before(g, j // UB))

                        def exps_ahead():
                            if not (is_last and j + 2 >= NUB):
                                exps(g, j + 2)

                        def values_behind():
                            if not (is_first and j == 0):
                                values(g, j - 1)

                        def fold():
                            if folds:
                                fold_q(grp + 1, piece, h_piece_before(g, grp, piece))
                        if first:
                            probs_T(g, j)
                            keys_ahead()
                        else:
                            keys_ahead()
                            probs_T(g, j)
                        if r == 1:
                            exps_ahead()
                            if not (is_first and grp == 0):
                                outputs(g, grp)
                            fold()
                            values_behind()
                        elif first:
                            values_behind()
                            exps_ahead()
                            fold()
                        else:
                            fold()
                            exps_ahead()
                            values_behind()
                run(act, body)
                values(TURNS - 1, NUB - 1)
                outputs(TURNS, 0)

            @block.vector
            def _(dve):
                def row_stats(g, i):
                    dve.wait_ge(s_ctx[i % NB], CTX_DMAS * 16 * (g + i // NB + 1))
                    wait(dve, s_rstd, batch(g, i) - 1)
                    for c in range(3):
                        last = dve.bn_stats(stats[:, i % 2, c, :], Cx[0:KC, i % NB, c, :])
                    last.then_inc(s_bn, 1)

                def row_stats_end(g, i):
                    for c in range(3):
                        last = dve.bn_aggr(mv[:, i % 4, c, :], stats[:, i % 2, c, :])
                    last.then_inc(s_stats, 1)

                def normed(g, i):
                    wait(dve, s_rstd, batch(g, i) + 1)
                    if not (isinstance(g, int) and batch(g, i) < 4):
                        wait(dve, s_hfull, keys_out(g, i - 4))
                        wait(dve, s_store[i % 4], (g * (NB // 4) + i // 4) * 32)
                    for c in range(3):
                        last = dve.tensor_scalar(Hat[:, i % 4, c, :], Cx[0:KC, i % NB, c, :],
                                                 mv[:, i % 4, c, 0:1], rstd[:, i % 4, c:c + 1],
                                                 ALU.subtract, ALU.mult)
                    last.then_inc(s_hat, 1)

                def softmax_max(g, j, bn=None):
                    wait(dve, s_s, unit(g, j) + 1)
                    if first:
                        wait(dve, s_exp, unit(g, j))
                        dve.tensor_scalar(Sc[:], S[par(j)][:, :, 0:KEYS], -10000.0, 10000.0, ALU.max,
                                          ALU.min).then_inc(s_clip, 1)
                        wait(dve, s_clip, unit(g, j) + 1)
                    if bn is not None:
                        wait(dve, s_bn, bn)
                    src = Sc if first else S[par(j)]
                    dve.tensor_reduce(NM[:, par(j), :], src[:, :, 0:KEYS], AX.X, ALU.max,
                                      negate=True).then_inc(s_max, 1)

                def recip(g, j):
                    wait(dve, s_exp, unit(g, j) + 1)
                    wait(dve, s_p, unit(g, j) - 1)
                    dve.reciprocal(RD[:, par(j), :], DEN[:, par(j), :]).then_inc(s_rd, 1)

                def keys_lo(g, i, before):
                    wait(dve, s_hhi, before + 1)
                    dve.tensor_tensor(KT[1][:, i % 2, 0:KEYS], Hp[:, 0:KEYS], KT[0][:, i % 2, 0:KEYS],
                                      ALU.subtract).then_inc(s_hfree, 1)

                def fold_lo(grp, n, before):
                    wait(dve, s_hhi, before + 1)
                    hi, lo = (x[:, grp % GB, :, 4 * n:4 * n + 4, :].rearrange("p b h l -> p h b l") for x in QF)
                    dve.tensor_tensor(lo, Hp[:, :].rearrange("p (h b l) -> p h b l", h=4, b=BT), hi,
                                      ALU.subtract).then_inc(s_hfree, 1)

                def probs_lo(g, j):
                    wait(dve, s_phi, unit(g, j) + 1)
                    src = Tp[0:KMAX].rearrange("p a (b c) -> p (a b) c", b=2)[:, 0:3, :]
                    dve.tensor_tensor(PT[1][:, par(j)], src, PT[0][:, par(j)], ALU.subtract).then_inc(s_pt, 1)

                def rows_hi(g, i):
                    wait(dve, s_aff, batch(g, i) + 1)
                    if not (isinstance(g, int) and batch(g, i) < 4):
                        wait(dve, s_zfull, z_before(g, (i - 4) * UB + UB - 1) + 1)
                    dve.tensor_copy(CV[0][:, i % 4], Cx[0:KMAX, i % NB]).then_inc(s_chi, 1)

                def rows_lo(g, i):
                    wait(dve, s_chi, batch(g, i) + 1)
                    dve.tensor_tensor(CV[1][:, i % 4], Cx[0:KMAX, i % NB], CV[0][:, i % 4],
                                      ALU.subtract).then_inc(s_clo, 1)

                if first:
                    dve.memset(Cx[64:KC, :, 2, :], 0.0).then_inc(s_zero, 1)
                    dve.memset(Tp[64:KC, 1, 0:256], 0.0)
                    for i in range(5):
                        row_stats(0, i)
                        dve.wait_ge(s_bn, i + 1)
                        row_stats_end(0, i)
                        if i >= 1:
                            normed(0, i - 1)
                else:
                    dve.memset(Cx[64:KMAX, :, 0:2, :], 0.0).then_inc(s_zero, 1)
                    dve.memset(Tp[64:KMAX, 0, :], 0.0)
                    for x in KT:
                        last = dve.memset(x[:, :, KEYS:KW].bitcast(F32), 0.0)
                    last.then_inc(s_pad, 1)
                    for n in range(pieces):
                        fold_lo(0, n, n)
                    keys_lo(0, 0, pieces)
                    keys_lo(0, 1, pieces + 1)
                    rows_hi(0, 0)
                    rows_lo(0, 0)
                softmax_max(0, 0)
                softmax_max(0, 1)
                recip(0, 0)

                def body(g, is_first, is_last):
                    for j in range(NUB):
                        stats_ahead = first and not (is_last and j + 5 >= NB)
                        if stats_ahead:
                            row_stats(g, j + 5)
                        if not first and j % UB == 0 and not (is_last and j // UB + LA >= NB):
                            keys_lo(g, j // UB + LA, h_kt_before(g, j // UB))
                        if not (is_last and j == NUB - 1):
                            recip(g, j + 1)
                        more_rows = not first and j % UB == 0 and not (is_last and j // UB + 1 >= NB)
                        if not (is_last and j + 2 >= NUB):
                            softmax_max(g, j + 2, batch(g, j + 5) + 1 if stats_ahead else None)
                        if stats_ahead:
                            row_stats_end(g, j + 5)
                        if not first:
                            probs_lo(g, j)
                        if more_rows:
                            rows_hi(g, j // UB + 1)
                        grp, piece = j // NU, j % NU - fold_slot
                        if not first and 0 <= piece < pieces and not (is_last and grp == GB - 1):
                            fold_lo(grp + 1, piece, h_piece_before(g, grp, piece))
                        if more_rows:
                            rows_lo(g, j // UB + 1)
                        if first and not (is_last and j + 4 >= NB):
                            normed(g, j + 4)
                run(dve, body)

            @block.gpsimd
            def _(pool):
                def norm(g, j):
                    wait(pool, s_rd, unit(g, j) + 1)
                    pool.tensor_tensor(Pr[:, par(j)], Pr[:, par(j)],
                                       RD[:, par(j), :].rearrange("p (r o) -> p r o", o=1).to_broadcast([P, 2, KEYS]),
                                       ALU.mult).then_inc(s_p, 1)

                def rsqrt(g, i):
                    wait(pool, s_stats, batch(g, i) + 1)
                    pool.tensor_tensor(var[:, i % 2], mv[:, i % 4, :, 1], w["eps"][0:KC, 0:3],
                                       ALU.add).then_inc(s_var, 1)
                    wait(pool, s_var, batch(g, i) + 1)
                    wait(pool, s_hat, batch(g, i) - 3)
                    pool.tensor_tensor(rstd[:, i % 4], var[:, i % 2], w["minus_half"][0:KC, 0:3],
                                       ALU.pow).then_inc(s_rstd, 1)

                def key_rows(g, i):
                    n = i % NB
                    pool.wait_ge(s_ctx[n], CTX_DMAS * 16 * (g + i // NB + 1))
                    wide = [w[k][0:KC, :].rearrange("p (o d) -> p o d", o=1).to_broadcast([KC, 2, D])
                            for k in ("ln1_w", "ln1_b")]
                    a, b = Cx[0:KC, n, 0:2, :], Cx[0:KR, n, 2, :]
                    pool.tensor_tensor(a, a, wide[0], ALU.mult).then_inc(s_gain, 1)
                    pool.tensor_tensor(b, b, w["ln1_w"][0:KR, :], ALU.mult).then_inc(s_gain, 1)
                    wait(pool, s_gain, 2 * batch(g, i) + 2)
                    pool.tensor_tensor(a, a, wide[1], ALU.add)
                    pool.tensor_tensor(b, b, w["ln1_b"][0:KR, :], ALU.add).then_inc(s_aff, 1)

                if first:
                    for i in range(5):
                        rsqrt(0, i)
                else:
                    for i in range(3):
                        key_rows(0, i)
                norm(0, 0)

                def body(g, is_first, is_last):
                    for j in range(NUB):
                        if not (is_last and j == NUB - 1):
                            norm(g, j + 1)
                        if first and not (is_last and j + 5 >= NB):
                            rsqrt(g, j + 5)
                        if not first and j % UB == 0 and not (is_last and j // UB + 3 >= NB):
                            key_rows(g, j // UB + 3)
                run(pool, body)


Q = 4
TQ = NT // Q
NQ = T // Q


def spread(ap, n):
    return ap.rearrange("p (n o) -> p n o", o=1).to_broadcast([ap.shape[0], n, D])


def norm_stage(nc, w, tag, src, rows, dst_T, gain=None, shift=None, twice=False, add=None, row_affine=None,
               rows_out=None, rows_T=None, first=None, head=None):
    with ExitStack() as ctx:
        sb, ps, sem = place(nc, ctx, tag)
        stats = sb("stats", [P, NT, 6])
        mv = sb("mean_var", [P, NT, 2])
        var, factor, off = (sb(n, [P, NT]) for n in ("var_eps", "factor", "offset"))
        parts = head(sb, ps, sem) if head is not None else {}

        def part(name, eng):
            if name in parts:
                parts[name](eng)
        bank = list(parts.get("banks", ()))
        while len(bank) < 2:
            bank.append(ps(f"rows_T_ps{len(bank)}", [P, NQ]))
        s_add, s_bn, s_stats, s_pool, s_rstd, s_off, s_T, s_out, s_gain, s_st = (
            sem(n) for n in ("added", "bn_stats", "mean_var", "pool_chain", "rstd", "offset", "transposed", "out",
                             "gained", "stored"))
        s_rows = [sem(f"rows{q}") for q in range(Q)]
        s_aff = [sem(f"affine{q}") for q in range(Q)]
        ACT_QS = Q // 2

        def cut(q):
            return slice(q * TQ, (q + 1) * TQ)

        def affine(eng, q, link):
            g3, b3 = (x[:, :].rearrange("p (o d) -> p o d", o=1).to_broadcast([P, TQ, D]) for x in row_affine)
            eng.wait_ge(s_rows[q], 1)
            link(eng.tensor_tensor(rows_out[:, cut(q), :], rows[:, cut(q), :], g3, ALU.mult))
            eng.tensor_tensor(rows_out[:, cut(q), :], rows_out[:, cut(q), :], b3, ALU.add).then_inc(s_aff[q], 1)

        with nc.Block() as block:
            @block.vector
            def _(dve):
                part("vector", dve)
                for q in range(Q):
                    if "add" in parts:
                        parts["add"](dve, q)
                    if add is not None:
                        dve.tensor_tensor(src[:, cut(q), :], src[:, cut(q), :], add[:, cut(q), :],
                                          ALU.add).then_inc(s_add, 1)
                        dve.wait_ge(s_add, q + 1)
                    for t in range(q * TQ, q * TQ + TQ):
                        last = dve.bn_stats(stats[:, t, :], src[:, t, :])
                    last.then_inc(s_bn, 1)
                    dve.wait_ge(s_bn, q + 1)
                    for t in range(q * TQ, q * TQ + TQ):
                        last = dve.bn_aggr(mv[:, t, :], stats[:, t, :])
                    last.then_inc(s_stats, 1)
                for q in range(ACT_QS, Q):
                    dve.wait_ge(s_rstd, q + 1)
                    for t in range(q * TQ, q * TQ + TQ):
                        last = dve.tensor_scalar(rows[:, t, :], src[:, t, :], mv[:, t, 0:1], factor[:, t:t + 1],
                                                 ALU.subtract, ALU.mult)
                    last.then_inc(s_rows[q], 1)
                if row_affine is not None:
                    link = chain(dve, s_gain)
                    for q in range(ACT_QS, Q):
                        affine(dve, q, link)

            @block.gpsimd
            def _(pool):
                part("gpsimd", pool)
                link = chain(pool, s_pool)
                for q in range(Q):
                    pool.wait_ge(s_stats, q + 1)
                    link(pool.tensor_tensor(var[:, cut(q)], mv[:, cut(q), 1], w["eps"][:, 0:TQ], ALU.add))
                    if twice:
                        link(pool.tensor_tensor(var[:, cut(q)], var[:, cut(q)], w["eps"][:, 0:TQ], ALU.mult))
                        link(pool.tensor_tensor(var[:, cut(q)], var[:, cut(q)], mv[:, cut(q), 1], ALU.add))
                    pool.tensor_tensor(factor[:, cut(q)], var[:, cut(q)], w["minus_half"][:, 0:TQ],
                                       ALU.pow).then_inc(s_rstd, 1)
                    if q < ACT_QS:
                        pool.wait_ge(s_rstd, q + 1)
                        link(pool.tensor_tensor(off[:, cut(q)], mv[:, cut(q), 0], factor[:, cut(q)], ALU.mult))
                        pool.tensor_tensor(off[:, cut(q)], w["zero"][:, 0:TQ], off[:, cut(q)],
                                           ALU.subtract).then_inc(s_off, 1)
                if row_affine is not None:
                    for q in range(ACT_QS):
                        affine(pool, q, link)

            @block.tensor
            def _(pe):
                part("tensor", pe)
                for q in range(Q):
                    pe.wait_ge(s_rows[q], 1)
                    wait(pe, s_out, q - 1)
                    for i in range(TQ):
                        last = pe.transpose(bank[q % 2][:, i * P:(i + 1) * P], rows[:, q * TQ + i, :], w["ident"][:])
                    last.then_inc(s_T, 1)

            @block.scalar
            def _(act):
                part("scalar", act)
                for q in range(ACT_QS):
                    act.wait_ge(s_off, q + 1)
                    for t in range(q * TQ, q * TQ + TQ):
                        last = act.activation(rows[:, t, :], src[:, t, :], ACT.Identity, bias=off[:, t:t + 1],
                                              scale=factor[:, t:t + 1])
                    last.then_inc(s_rows[q], 1)
                for q in range(Q):
                    act.wait_ge(s_T, q + 1)
                    if gain is None:
                        act.activation(dst_T[:, q * NQ:(q + 1) * NQ], bank[q % 2][:], ACT.Copy).then_inc(s_out, 1)
                    else:
                        act.activation(dst_T[:, q * NQ:(q + 1) * NQ], bank[q % 2][:], ACT.Identity,
                                       bias=shift[:, 0:1], scale=gain[:, 0:1]).then_inc(s_out, 1)

            @block.sync
            def _(sp):
                part("sync", sp)
                if first is not None:
                    first(sp)
                if rows_T is not None:
                    for q in range(Q):
                        sp.wait_ge(s_aff[q], 1)
                        sp.dma_start(rows_T[q * TQ:(q + 1) * TQ, :, :].rearrange("t p d -> p t d"),
                                     rows_out[:, q * TQ:(q + 1) * TQ, :]).then_inc(s_st, 16)
                    sp.wait_ge(s_st, 16 * Q)


def gelu_part(w, old):
    def head(sb, ps, sem):
        G = sb("gelu", [P, NT, D])
        bank = ps("proj", [P, Q, NQ])
        s_mm, s_gelu, s_add, s_sum = sem("proj"), sem("gelu"), sem("on_added"), sem("gelu_added")

        def tensor(pe):
            for q in range(Q):
                for i in range(TQ):
                    t = q * TQ + i
                    last = pe.matmul(bank[:, q, i * D:(i + 1) * D], w["QT"][:, t * P:(t + 1) * P], w["Wo0"][:],
                                     start=True, stop=True)
                last.then_inc(s_mm, 1)

        def scalar(act):
            for q in range(Q):
                act.wait_ge(s_mm, q + 1)
                act.activation(G[:, q * TQ:(q + 1) * TQ, :].rearrange("p t d -> p (t d)"), bank[:, q, :],
                               ACT.Gelu).then_inc(s_gelu, 1)

        def vector(dve):
            for q in range(Q):
                x = w["X"][:, q * TQ:(q + 1) * TQ, :]
                dve.tensor_tensor(x, x, w["N"][:, q * TQ:(q + 1) * TQ, :], ALU.add).then_inc(s_add, 1)

        def add(dve, q):
            x = w["X"][:, q * TQ:(q + 1) * TQ, :]
            dve.wait_ge(s_gelu, q + 1)
            dve.wait_ge(s_add, q + 1)
            dve.tensor_tensor(x, x, G[:, q * TQ:(q + 1) * TQ, :], ALU.add).then_inc(s_sum, 1)
            dve.wait_ge(s_sum, q + 1)
        return {"tensor": tensor, "scalar": scalar, "vector": vector, "add": add, "gpsimd": lambda pool: clear(pool, old)}
    return head


def self_attention_weights(nc, ctx, ins):
    sb, ps, sem = place(nc, ctx, "saw")
    W = sb("weights_T", [D, 3, D])
    s_w, s_f = sem("weights"), sem("to_fold")
    names = ("L1_xattn_WqT", "L1_xattn_WkT", "L1_xattn_WvT", "L1_xattn_Wo")
    fold = [sb(name, [64, 16, D]) for name in names]

    def first(sp):
        for n, name in enumerate(("L0_attn_wqT", "L0_attn_wkT", "L0_attn_wvT")):
            sp.dma_start(W[:, n, :], ins[name]).then_inc(s_w, 16)
        for buf, name in zip(fold, names):
            sp.dma_start(buf[:], ins[name].rearrange("h c d -> c h d")).then_inc(s_f, 16)
    return {"W": W, "s_w": s_w, "s_f": s_f, "fold": fold, "first": first}


def self_attention_part(w, pre):
    W, s_w = pre["W"], pre["s_w"]

    def head(sb, ps, sem):
        qk = sb("qk_T", [D, 2, T])
        V = sb("v_rows", [P, NT, D])
        A = sb("probs", [P, NT, L])
        AT = sb("probs_T", [P, NT, L])
        BD = sb("probs_diagonal", [P, NT, P])
        M = sb("max", [P, NT])
        den = sb("den", [P, NT])
        rden = sb("recip_den", [P, NT])
        bank = ps("proj", [P, 4, NQ])
        Sb = ps("scores", [P, NT, L])
        s_mm, s_out, s_s, s_dve, s_exp, s_mask, s_bd, s_o = (
            sem(n) for n in ("proj_ps", "proj", "scores", "chain", "exp", "masked", "diagonal", "out_ps"))
        s_sum, s_fold, s_folded = sem("x_added"), sem("folded_ps"), sem("folded")
        def tensor(pe):
            pe.wait_ge(s_w, 48)
            n = 0
            for m in range(2):
                for q in range(Q):
                    if n >= 4:
                        pe.wait_ge(s_out, n - 3)
                    pe.matmul(bank[:, n % 4, :], W[:, m, :], w["QT"][:, q * NQ:(q + 1) * NQ], start=True,
                              stop=True).then_inc(s_mm, 1)
                    n += 1
            for q in range(Q):
                pe.wait_ge(s_out, n - 3)
                for i in range(TQ):
                    t = q * TQ + i
                    last = pe.matmul(bank[:, n % 4, i * D:(i + 1) * D], w["QT"][:, t * P:(t + 1) * P], W[:, 2, :],
                                     start=True, stop=True)
                last.then_inc(s_mm, 1)
                n += 1
            for b in range(B):
                c = slice(b * L, (b + 1) * L)
                o = (b % BT) * L
                last = pe.matmul(Sb[o:o + L, b // BT, :], qk[:, 1, c], qk[:, 0, c], start=True, stop=True)
            last.then_inc(s_s, 1)
            pe.wait_ge(s_out, 12)
            pe.wait_ge(pre["s_f"], 64)
            for k in range(8):
                wait(pe, s_folded, k - 3)
                a, b = pre["fold"][2 * (k // 4):2 * (k // 4) + 2]
                for i in range(4):
                    h = 4 * (k % 4) + i
                    last = pe.matmul(bank[:, k % 4, i * D:(i + 1) * D], a[:, h, :], b[:, h, :], start=True, stop=True)
                last.then_inc(s_fold, 1)
            pe.wait_ge(s_folded, 8)
            pe.wait_ge(s_bd, 1)
            for q in range(Q):
                for i in range(TQ):
                    t = q * TQ + i
                    last = pe.matmul(bank[:, q, i * D:(i + 1) * D], BD[:, t, :], V[:, t, :], start=True, stop=True)
                last.then_inc(s_o, 1)

        def scalar(act):
            for n in range(12):
                act.wait_ge(s_mm, n + 1)
                q = n % Q
                dst = qk[:, n // Q, q * NQ:(q + 1) * NQ] if n < 8 else V[:, q * TQ:(q + 1) * TQ, :].rearrange(
                    "p t d -> p (t d)")
                act.activation(dst, bank[:, n % 4, :], ACT.Copy).then_inc(s_out, 1)
            act.wait_ge(s_dve, 3)
            act.activation(A[:], A[:], ACT.Exp, scale=float(D) ** -0.5).then_inc(s_exp, 1)
            for k in range(8):
                act.wait_ge(s_fold, k + 1)
                act.activation((w["M1"] if k < 4 else w["VO"])[:, 4 * (k % 4):4 * (k % 4) + 4, :],
                               bank[:, k % 4, :].rearrange("p (h d) -> p h d", h=4), ACT.Copy,
                               scale=0.125 if k < 4 else 1.0).then_inc(s_folded, 1)

        def gpsimd(pool):
            pool.wait_ge(s_dve, 6)
            for j in range(BT):
                a = A[j * L:(j + 1) * L]
                last = pool.affine_select(out=a, in_=a, compare_op=ALU.is_ge, fill=0.0, base=0,
                                          pattern=[[0, NT], [-1, L]], channel_multiplier=1)
            last.then_inc(s_mask, 1)

        def vector(dve):
            link = chain(dve, s_dve)
            link(dve.memset(BD[:], 0.0))
            dve.wait_ge(s_s, 1)
            link(dve.tensor_reduce(M[:], Sb[:], AX.X, ALU.max))
            over = lambda v: v[:, :].rearrange("p (t o) -> p t o", o=1).to_broadcast([P, NT, L])
            link(dve.tensor_tensor(A[:], Sb[:], over(M), ALU.subtract))
            dve.wait_ge(s_exp, 1)
            link(dve.tensor_reduce(den[:], A[:], AX.X, ALU.add))
            link(dve.reciprocal(rden[:], den[:]))
            link(dve.tensor_tensor(A[:], A[:], over(rden), ALU.mult))
            dve.wait_ge(s_mask, 1)
            link(dve.transpose(AT[:, :, :].rearrange("p t l -> p (t l)"), A[:, :, :].rearrange("p t l -> p (t l)")))
            for j in range(BT):
                r = slice(j * L, (j + 1) * L)
                last = dve.tensor_copy(BD[r, :, r], AT[r, :, :])
            last.then_inc(s_bd, 1)

        def add(dve, q):
            dve.wait_ge(s_o, q + 1)
            x = w["X"][:, q * TQ:(q + 1) * TQ, :]
            dve.tensor_tensor(x, bank[:, q, :].rearrange("p (t d) -> p t d", d=D), x, ALU.add).then_inc(s_sum, 1)
            dve.wait_ge(s_sum, q + 1)
        return {"tensor": tensor, "scalar": scalar, "gpsimd": gpsimd, "vector": vector, "add": add}
    return head


def moe_weights(nc, ctx, ins, layer):
    FF = 4 * D
    FC = FF // P
    NW = 2 if layer else 1
    tag = f"moe{layer}"
    sb, ps, sem = place(nc, ctx, f"{tag}w")
    R = sb("router_T", [D, 8])
    W1 = sb("w_in_T", [D, 2, NW, FF])
    W2 = sb("w_out_T", [P, 2, FC, D])
    s_r = sem("router")
    s_w = [sem(f"weights{i}") for i in range(2)]

    def load_in(sp, e, par):
        for n in range(NW):
            src = ins[f"{tag}_w_in_T"][bass.ds(e * NW + n, 1), :, :].rearrange("e d f -> (e d) f")
            sp.dma_start(W1[:, par, n, :], src).then_inc(s_w[par], 16)

    def load_out(sp, e, par):
        src = ins[f"{tag}_w_out_T"][bass.ds(e, 1), :, :].rearrange("e (c p) d -> p (e c) d", p=P)
        sp.dma_start(W2[:, par], src).then_inc(s_w[par], 16)

    def first(sp):
        sp.dma_start(R[:], ins[f"{tag}_router_T"]).then_inc(s_r, 16)
        for par in range(2):
            load_in(sp, par, par)
            load_out(sp, par, par)
    return {"R": R, "W1": W1, "W2": W2, "s_r": s_r, "s_w": s_w, "first": first, "load_in": load_in,
            "load_out": load_out}


def token_tiles(x, q):
    return x.rearrange("(t a) l d -> (a l) t d", a=BT)[:, q * TQ:(q + 1) * TQ, :]


def moe_part(w, pre, layer, old, out=None):
    E, FF = 8, 4 * D
    FC = FF // P
    tag = f"moe{layer}"
    gated = layer == 1
    NW = 2 if gated else 1
    PARTS = (("_hi", F32R), ("_lo", F32R))
    R, W1, W2, s_r, s_w = (pre[k] for k in ("R", "W1", "W2", "s_r", "s_w"))

    def head(sb, ps, sem):
        W1h, W1l = (sb(f"w_in_T{n}", [D, 2, NW, FF], t) for n, t in PARTS)
        Hd = sb("hidden_T", [P, 2, FC, NQ])
        Qh, Ql = (sb(f"tokens_T{n}", [D, T], t) for n, t in PARTS)
        Rl = sb("relu", [P, 2, NQ]) if gated else None
        pr = sb("probs", [P, NT, E])
        gt = sb("greater", [P, NT, E, E])
        eq = sb("equal", [P, NT, E, E])
        low = sb("lower", [P, E, E])
        mx, den, rden = (sb(n, [P, NT]) for n in ("max", "den", "recip_den"))
        rank = sb("rank", [P, NT, E])
        Wt = sb("weights", [P, NT, E])
        We = sb("weights_e", [P, 2, NT])
        Hb = [ps(f"hidden_ps{i}", [P, NQ]) for i in range(4)]
        Yb = [ps(f"out_ps{i}", [P, NQ]) for i in range(2)]
        Rbank = ps("router_ps", [P, NQ])
        Rb = Rbank[:, 0:NT * E].rearrange("p (t e) -> p t e", e=E)
        s_rm, s_dve, s_exp, s_low, s_done = (sem(n) for n in ("logits", "chain", "exp", "lower", "result_stored"))
        s_h, s_act, s_y, s_x, s_we, s_relu = (
            sem(n) for n in ("hidden_ps", "hidden", "out_ps", "unit_added", "weights_e", "relu"))
        s_qh, s_ql, s_wh, s_wl = (sem(n) for n in ("tokens_hi", "tokens_lo", "weights_hi", "weights_lo"))

        def sync(sp):
            def load(e, par):
                sp.wait_ge(s_wl, e - 1)
                pre["load_in"](sp, e, par)
                sp.wait_ge(s_y, (e - 1) * Q)
                pre["load_out"](sp, e, par)
            with sp.Fori(1, E // 2) as i:
                load(i * 2, 0)
                load(i * 2 + 1, 1)
            if out is not None:
                for q in range(Q):
                    sp.wait_ge(s_x, (E - 1) * Q + q + 1)
                    sp.dma_start(token_tiles(out, q), w["X"][:, q * TQ:(q + 1) * TQ, :]).then_inc(s_done, 16)
                sp.wait_ge(s_done, 16 * Q)

        WD = 16 * (NW + 1)

        def split_ahead(i, j, is_last):
            if j % Q != 1 or (is_last and j >= Q):
                return None
            return (i, 1) if j < Q else (i + 1, 0)

        def tensor(pe):
            def hidden(i, j, c):
                i, j = i + j // (2 * Q), j % (2 * Q)
                par, q = j // Q, j % Q
                u = i * 2 * Q + j
                if c == 0 and q == 0:
                    pe.wait_ge(s_wl, i * 2 + par + 1)
                if c == 0 and isinstance(i, int) and u < Q:
                    pe.wait_ge(s_ql, q + 1)
                if not gated:
                    wait(pe, s_act, u * FC + c - 3)
                    banks = [Hb[c]]
                else:
                    wait(pe, s_act, u * FC + c - 1)
                    banks = Hb[2 * (c % 2):2 * (c % 2) + 2]
                for k, hb in enumerate(banks):
                    for x, (wx, qx) in enumerate(((W1h, Qh), (W1h, Ql), (W1l, Qh))):
                        last = pe.matmul(hb[:], wx[:, par, k, c * P:(c + 1) * P],
                                         qx[:, q * NQ:(q + 1) * NQ], start=(x == 0), stop=(x == 2))
                last.then_inc(s_h, 1)

            def output(i, j, t):
                par, q = j // Q, j % Q
                u = i * 2 * Q + j
                if t == 0:
                    wait(pe, s_act, (u + 1) * FC)
                    wait(pe, s_x, u - 1)
                for c in range(FC):
                    last = pe.matmul(Yb[j % 2][:, t * D:(t + 1) * D], Hd[:, j % 2, c, t * P:(t + 1) * P],
                                     W2[:, par, c, :], start=(c == 0), stop=(c == FC - 1))
                if t == TQ - 1:
                    last.then_inc(s_y, 1)

            pe.wait_ge(s_r, 16)
            for t in range(NT):
                last = pe.matmul(Rb[:, t, :], w["QT"][:, t * P:(t + 1) * P], R[:], start=True, stop=True)
            last.then_inc(s_rm, 1)
            for c in range(FC):
                hidden(0, 0, c)

            def body(i, is_last=False):
                for j in range(2 * Q):
                    for n in range(FC):
                        if not (is_last and j == 2 * Q - 1):
                            hidden(i, j + 1, n)
                        output(i, j, n)
            body(0)
            with pe.Fori(1, E // 2 - 1) as i:
                body(i)
            body(E // 2 - 1, True)

        def scalar(act):
            def weights_hi(i, par):
                act.wait_ge(s_w[par], (i + 1) * WD)
                wait(act, s_h, (i * 2 + par - 1) * Q * FC)
                for n in range(NW):
                    last = act.activation(W1h[:, par, n], W1[:, par, n], ACT.Copy)
                last.then_inc(s_wh, 1)

            weights_hi(0, 0)
            for q in range(Q):
                act.activation(Qh[:, q * NQ:(q + 1) * NQ], w["QT"][:, q * NQ:(q + 1) * NQ],
                               ACT.Copy).then_inc(s_qh, 1)
            act.wait_ge(s_dve, 2)
            act.activation(pr[:], pr[:], ACT.Exp).then_inc(s_exp, 1)

            def body(i, is_last=False):
                for j in range(2 * Q):
                    u = i * 2 * Q + j
                    for c in range(FC):
                        n = u * FC + c
                        act.wait_ge(s_h, n + 1)
                        if gated:
                            wait(act, s_act, n - 1)
                            act.activation(Rl[:, c % 2, :], Hb[2 * (c % 2)][:], ACT.Relu).then_inc(s_relu, 1)
                        else:
                            wait(act, s_y, u - 1)
                            act.activation(Hd[:, j % 2, c, :], Hb[c][:], ACT.Gelu).then_inc(s_act, 1)
                    ahead = split_ahead(i, j, is_last)
                    if ahead:
                        weights_hi(*ahead)
            body(0)
            with act.Fori(1, E // 2 - 1) as i:
                body(i)
            body(E // 2 - 1, True)

        def gpsimd(pool):
            pool.memset(low[:], 1.0).then_inc(s_low, 1)
            pool.wait_ge(s_low, 1)
            pool.affine_select(out=low[:], in_=low[:], compare_op=ALU.is_gt, fill=0.0, base=0,
                               pattern=[[1, E], [-1, E]], channel_multiplier=0).then_inc(s_low, 1)

            def weights_lo(i, par):
                pool.wait_ge(s_wh, i * 2 + par + 1)
                pool.tensor_tensor(W1l[:, par], W1[:, par], W1h[:, par], ALU.subtract).then_inc(s_wl, 1)

            weights_lo(0, 0)
            clear(pool, old)

            def body(i, is_last=False):
                for j in (1, Q + 1):
                    ahead = split_ahead(i, j, is_last)
                    if ahead:
                        weights_lo(*ahead)
            body(0)
            with pool.Fori(1, E // 2 - 1) as i:
                body(i)
            body(E // 2 - 1, True)

        def add_unit(dve, i, j):
            par, q = j // Q, j % Q
            u = i * 2 * Q + j
            if q == 0:
                dve.tensor_copy(We[:, par, :], Wt[:, :, bass.ds(i * 2 + par, 1)].rearrange(
                    "p t o -> p (t o)")).then_inc(s_we, 1)
                dve.wait_ge(s_we, i * 2 + par + 1)
            dve.wait_ge(s_y, u + 1)
            for t in range(TQ):
                n = q * TQ + t
                last = dve.scalar_tensor_tensor(
                    out=w["X"][:, n, :], in0=Yb[j % 2][:, t * D:(t + 1) * D],
                    scalar=We[:, par, n:n + 1], in1=w["X"][:, n, :], op0=ALU.mult, op1=ALU.add)
            last.then_inc(s_x, 1)

        def vector(dve):
            link = chain(dve, s_dve)
            over = lambda v: v[:, :].rearrange("p (t o) -> p t o", o=1).to_broadcast([P, NT, E])
            for q in range(Q):
                dve.wait_ge(s_qh, q + 1)
                dve.tensor_tensor(Ql[:, q * NQ:(q + 1) * NQ], w["QT"][:, q * NQ:(q + 1) * NQ],
                                  Qh[:, q * NQ:(q + 1) * NQ], ALU.subtract).then_inc(s_ql, 1)
            dve.wait_ge(s_rm, 1)
            link(dve.tensor_reduce(mx[:], Rb, AX.X, ALU.max))
            link(dve.tensor_tensor(pr[:], Rb, over(mx), ALU.subtract))
            dve.wait_ge(s_exp, 1)
            link(dve.tensor_reduce(den[:], pr[:], AX.X, ALU.add))
            link(dve.reciprocal(rden[:], den[:]))
            link(dve.tensor_tensor(pr[:], pr[:], over(rden), ALU.mult))
            def gate(i, j):
                u = i * 2 * Q + j
                for c in range(FC):
                    n = u * FC + c
                    dve.wait_ge(s_relu, n + 1)
                    wait(dve, s_y, u - 1)
                    dve.tensor_tensor(Hd[:, j % 2, c, :], Hb[2 * (c % 2) + 1][:], Rl[:, c % 2, :],
                                      ALU.mult).then_inc(s_act, 1)

            if gated:
                gate(0, 0)
            mine = pr[:, :, :].rearrange("p t (e o) -> p t e o", o=1).to_broadcast([P, NT, E, E])
            other = pr[:, :, :].rearrange("p t (o j) -> p t o j", o=1).to_broadcast([P, NT, E, E])
            dve.tensor_tensor(gt[:], other, mine, ALU.is_gt)
            link(dve.tensor_tensor(eq[:], other, mine, ALU.is_equal))
            dve.wait_ge(s_low, 2)
            link(dve.tensor_tensor(eq[:], eq[:], low[:, :, :].rearrange("p (o e) j -> p o e j", o=1).to_broadcast(
                [P, NT, E, E]), ALU.mult))
            link(dve.tensor_tensor(gt[:], gt[:], eq[:], ALU.add))
            link(dve.tensor_reduce(rank[:], gt[:], AX.X, ALU.add))
            link(dve.scalar_tensor_tensor(out=Wt[:], in0=rank[:], scalar=1.5, in1=pr[:], op0=ALU.is_lt,
                                          op1=ALU.mult))
            if gated:
                link(dve.tensor_reduce(den[:], Wt[:], AX.X, ALU.add))
                link(dve.tensor_scalar(den[:], den[:], float(np.finfo(np.float32).eps), None, ALU.add))
                link(dve.reciprocal(rden[:], den[:]))
                link(dve.tensor_tensor(Wt[:], Wt[:], over(rden), ALU.mult))

            def body(i, is_last=False):
                for j in range(2 * Q):
                    if gated and not (is_last and j == 2 * Q - 1):
                        gate(i + (j + 1) // (2 * Q), (j + 1) % (2 * Q))
                    if not (is_last and j >= Q and not gated):
                        add_unit(dve, i, j)
            body(0)
            with dve.Fori(1, E // 2 - 1) as i:
                body(i)
            body(E // 2 - 1, True)

        def add(dve, q):
            add_unit(dve, E // 2 - 1, Q + q)
            dve.wait_ge(s_x, (E - 1) * Q + q + 1)
        return {"sync": sync, "tensor": tensor, "scalar": scalar, "gpsimd": gpsimd, "vector": vector, "add": add,
                "banks": (Rbank,)}
    return head


def run_stage(nc, head, tag):
    with ExitStack() as ctx:
        parts = head(*place(nc, ctx, tag))
        with nc.Block() as block:
            block.sync(parts["sync"])
            block.tensor(parts["tensor"])
            block.scalar(parts["scalar"])
            block.gpsimd(parts["gpsimd"])
            block.vector(parts["vector"])


DI = 2 * D
NS = 16
RANK = 64
FD = 4 * D
BLK = 1024
ROUND = 1.5 * 2.0 ** 23


def ssm_weights(nc, ctx, ins):
    sb, ps, sem = place(nc, ctx, "ssmw")
    v = {"W": sb("in_T", [D, 2 * DI]), "WX": sb("x_T", [P, 2, RANK + 2 * NS]), "WD": sb("dt_T", [RANK, DI]),
         "cw": sb("conv_w", [P, 2, 4]), "cb": sb("conv_b", [P, 2]), "db": sb("dt_b", [P, 2]),
         "D": sb("D", [P, 2]), "a": sb("a", [P, 2, NS]), "WO": sb("out_T", [P, 2, D]),
         "ffn": sb("ffn_w", [P, 3, FD]), "s_w": sem("weights"), "s_wo": sem("ffn_weights")}
    s_w, s_wo = v["s_w"], v["s_wo"]

    def first(sp):
        sp.dma_start(v["W"][:], ins["in_proj_T"]).then_inc(s_w, 16)
        sp.dma_start(v["WX"][:], ins["x_proj_T"].rearrange("(h p) n -> p h n", p=P)).then_inc(s_w, 16)
        sp.dma_start(v["WD"][:], ins["dt_proj_T"]).then_inc(s_w, 16)
        sp.dma_start(v["cw"][:], ins["conv_w"].rearrange("(h p) n -> p h n", p=P)).then_inc(s_w, 16)
        with nc.allow_non_contiguous_dma(reason="one value per partition"):
            sp.dma_start(v["cb"][:], ins["conv_b"].rearrange("(h p) -> p h", p=P)).then_inc(s_w, 16)
            sp.dma_start(v["db"][:], ins["dt_proj_b"].rearrange("(h p) -> p h", p=P)).then_inc(s_w, 16)
            sp.dma_start(v["D"][:], ins["D"].rearrange("(h p) -> p h", p=P)).then_inc(s_w, 16)
        sp.dma_start(v["a"][:], ins["A_log"].rearrange("(h p) n -> p h n", p=P)).then_inc(s_w, 16)
        sp.dma_start(v["WO"][:], ins["out_proj_T"].rearrange("(h p) n -> p h n", p=P)).then_inc(s_wo, 16)
        sp.dma_start(v["ffn"][:, 0, :], ins["gate_T"]).then_inc(s_wo, 16)
        sp.dma_start(v["ffn"][:, 1, :], ins["up_T"]).then_inc(s_wo, 16)
        sp.dma_start(v["ffn"][:, 2, :].rearrange("p (c d) -> p c d", d=D),
                     ins["down_T"].rearrange("(c p) d -> p c d", p=P)).then_inc(s_wo, 16)
    v["first"] = first
    return v


def ssm_in_stage(nc, w, v, old):
    with ExitStack() as ctx:
        sb, ps, sem = place(nc, ctx, "si")
        W, WX, WD, cw, cb, db, s_w = (v[k] for k in ("W", "WX", "WD", "cw", "cb", "db", "s_w"))
        XD = sb("x_dbl", [RANK + 2 * NS, T])
        pre = v["delta"]
        z = v["du"]
        neg = sb("neg_abs", [P, 2, T])
        tiny = sb("tiny", [P, 2, T])
        mask = sb("mask", [P, 2, T], mybir.dt.uint8)
        bank = ps("proj", [P, 4, NQ])
        xb = ps("x_ps", [P, 2, NQ])
        zb = ps("z_ps", [P, 2, NQ])
        s_mm, s_out, s_dve, s_conv, s_u, s_xm, s_xd, s_zm, s_z, s_neg, s_e, s_ln, s_a, s_sp = (
            sem(n) for n in ("proj_ps", "proj", "chain", "conv", "u", "x_ps", "x_dbl", "z_ps", "z",
                               "neg_abs", "exp", "ln", "a", "softplus"))
        s_sel, s_p, s_one, s_wsum, s_wm = (sem(n) for n in ("selector", "pool", "ones", "w_abs_sum", "w_sum_ps"))
        raw, wq, wscale = v["ffn"], v["wq"], v["wscale"]
        wsum = sb("w_abs_sum", [P, 3])
        wrec = sb("w_recip", [P, 3])
        ones = sb("ones", [P, P])
        with nc.Block() as block:
            @block.tensor
            def _(pe):
                pe.wait_ge(s_w, 128)
                for m in range(4):
                    for q in range(Q):
                        n = 4 * m + q
                        if n >= 4:
                            pe.wait_ge(s_out, n - 3)
                        pe.matmul(bank[:, q, :], W[:, m * P:(m + 1) * P], w["QT"][:, q * NQ:(q + 1) * NQ],
                                  start=True, stop=True).then_inc(s_mm, 1)
                for q in range(Q):
                    c = slice(q * NQ, (q + 1) * NQ)
                    pe.wait_ge(s_u, 2)
                    if q >= 2:
                        pe.wait_ge(s_xd, q - 1)
                    for h in range(2):
                        last = pe.matmul(xb[0:RANK + 2 * NS, q % 2, :], WX[:, h, :], v["u"][:, h, c], start=(h == 0),
                                         stop=(h == 1))
                    last.then_inc(s_xm, 1)
                pe.wait_ge(s_one, 1)
                pe.wait_ge(s_wsum, 1)
                pe.wait_ge(s_out, 16)
                pe.matmul(bank[:, 0, 0:3], ones[:], wsum[:], start=True, stop=True).then_inc(s_wm, 1)
                for h in range(2):
                    for q in range(Q):
                        n = 4 * h + q
                        pe.wait_ge(s_xd, q + 1)
                        if n >= 2:
                            pe.wait_ge(s_z, n - 1)
                        pe.matmul(zb[:, n % 2, :], WD[:, h * P:(h + 1) * P], XD[0:RANK, q * NQ:(q + 1) * NQ],
                                  start=True, stop=True).then_inc(s_zm, 1)

            @block.scalar
            def _(act):
                for m in range(4):
                    for q in range(Q):
                        c = slice(q * NQ, (q + 1) * NQ)
                        act.wait_ge(s_mm, 4 * m + q + 1)
                        if m < 2:
                            act.activation(pre[:, m, c], bank[:, q, :], ACT.Copy).then_inc(s_out, 1)
                        else:
                            act.activation(v["gate"][:, m - 2, c], bank[:, q, :], ACT.Silu).then_inc(s_out, 1)
                for h in range(2):
                    act.wait_ge(s_conv, h + 1)
                    act.activation(v["u"][:, h, :], v["u"][:, h, :], ACT.Silu).then_inc(s_u, 1)
                act.activation(v["a"][:], v["a"][:], ACT.Exp).then_inc(s_a, 1)
                for q in range(Q):
                    c = slice(q * NQ, (q + 1) * NQ)
                    act.wait_ge(s_xm, q + 1)
                    act.activation(XD[:, c], xb[0:RANK + 2 * NS, q % 2, :], ACT.Copy).then_inc(s_xd, 1)
                for h in range(2):
                    for q in range(Q):
                        c = slice(q * NQ, (q + 1) * NQ)
                        act.wait_ge(s_zm, 4 * h + q + 1)
                        act.activation(z[:, h, c], zb[:, q % 2, :], ACT.Identity, bias=db[:, h:h + 1])
                        act.activation(neg[:, h, c], zb[:, q % 2, :], ACT.Abs, bias=db[:, h:h + 1]).then_inc(s_z, 1)
                    act.wait_ge(s_z, 4 * h + 4)
                    act.activation(neg[:, h, :], neg[:, h, :], ACT.Exp, scale=-1.0).then_inc(s_e, 1)
                    act.wait_ge(s_e, h + 1)
                    act.activation(tiny[:, h, :], neg[:, h, :], ACT.Copy, scale=-0.25).then_inc(s_neg, 1)
                    act.activation(v["delta"][:, h, :], neg[:, h, :], ACT.Ln, bias=1.0).then_inc(s_ln, 1)

            @block.gpsimd
            def _(pool):
                pool.memset(ones[:], 1.0).then_inc(s_one, 1)
                sel = v["sel32"]
                pool.memset(sel[:], 0.0).then_inc(s_p, 1)
                pool.wait_ge(s_p, 1)
                for o in (64, 96):
                    s = sel[o:o + 2 * NS]
                    last = pool.affine_select(out=s, in_=s, compare_op=ALU.not_equal, fill=1.0, base=0,
                                              pattern=[[-1, 2 * NS], [0, P]], channel_multiplier=1)
                last.then_inc(s_sel, 1)
                clear(pool, old)
                pool.wait_ge(s_sp, 1)
                pool.tensor_tensor(v["du"][:, 0, :], v["delta"][:, 0, :], v["u"][:, 0, :], ALU.mult)

            @block.vector
            def _(dve):
                link = chain(dve, s_dve)
                dve.wait_ge(s_w, 128)
                u3 = [v["u"][:, h, :].rearrange("p (b l) -> p b l", l=L) for h in range(2)]
                x3 = [pre[:, h, :].rearrange("p (b l) -> p b l", l=L) for h in range(2)]
                for h in range(2):
                    dve.wait_ge(s_out, 4 * h + 4)
                    link(dve.tensor_scalar(v["u"][:, h, :], pre[:, h, :], cw[:, h, 3:4], cb[:, h:h + 1], ALU.mult,
                                           ALU.add))
                    for s in range(1, 4):
                        last = dve.scalar_tensor_tensor(out=u3[h][:, :, s:], in0=x3[h][:, :, :L - s],
                                                        scalar=cw[:, h, 3 - s:4 - s], in1=u3[h][:, :, s:],
                                                        op0=ALU.mult, op1=ALU.add)
                        if s < 3:
                            link(last)
                    last.then_inc(s_conv, 1)
                dve.wait_ge(s_sel, 1)
                link(dve.tensor_copy(v["sel"][64:128], v["sel32"][64:128]))
                dve.wait_ge(s_a, 1)
                link(dve.tensor_scalar(v["a"][:], v["a"][:], -1.0, None, ALU.mult))
                dve.wait_ge(v["s_wo"], 64)
                dve.tensor_reduce(wsum[:], raw[:], AX.X, ALU.add, apply_absolute_value=True).then_inc(s_wsum, 1)
                dve.wait_ge(s_xd, Q)
                hi, lo = v["bc"][64:96, :], v["bc"][96:128, :]
                link(dve.tensor_copy(hi, XD[64:96, :]))
                dve.tensor_tensor(lo, XD[64:96, :], hi.bitcast(F32), ALU.subtract)
                dve.wait_ge(s_wm, 1)
                link(dve.tensor_scalar(wscale[:], bank[:, 0, 0:3], 1.0 / (D * FD), 1e-5, ALU.mult, ALU.max))
                link(dve.reciprocal(wrec[:], wscale[:]))
                for k in range(3):
                    last = dve.tensor_scalar(raw[:, k, :], raw[:, k, :], wrec[:, k:k + 1], ROUND, ALU.mult, ALU.add)
                link(last)
                link(dve.tensor_scalar(raw[:], raw[:], ROUND - 1.0, ROUND + 1.0, ALU.max, ALU.min))
                dve.tensor_scalar(wq[:], raw[:], ROUND, None, ALU.subtract)
                for h in range(2):
                    e, t = neg[:, h, :], tiny[:, h, :]
                    dve.wait_ge(s_e, h + 1)
                    dve.tensor_scalar(mask[:, h, :], e, 1.0 / 32, None, ALU.is_lt)
                    dve.wait_ge(s_neg, h + 1)
                    for add in (1.0 / 3, -0.5, 1.0):
                        link(dve.scalar_tensor_tensor(out=t, in0=t, scalar=add, in1=e, op0=ALU.add, op1=ALU.mult))
                    dve.wait_ge(s_ln, h + 1)
                    link(dve.copy_predicated(v["delta"][:, h, :], mask[:, h, :], t))
                    dve.scalar_tensor_tensor(out=v["delta"][:, h, :], in0=z[:, h, :], scalar=0.0,
                                             in1=v["delta"][:, h, :], op0=ALU.max, op1=ALU.add).then_inc(s_sp, 1)
                dve.wait_ge(s_sp, 2)
                dve.tensor_tensor(v["du"][:, 1, :], v["delta"][:, 1, :], v["u"][:, 1, :], ALU.mult)


def ssm_scan_stage(nc, w, v):
    NBK = T // BLK
    NBB = BLK // L
    with ExitStack() as ctx:
        sb, ps, sem = place(nc, ctx, "ss")
        bs = w["O"][:, :, :].rearrange("p (a t) d -> p a (t d)", a=2)
        cs = w["N"][:, :, :].rearrange("p (a t) d -> p a (t d)", a=2)
        dA = sb("decay", [P, 2, 2, BLK])
        dB = sb("drive", [P, 2, 2, BLK])
        H = sb("states", [P, 2, 2, BLK])
        HC = sb("states_c", [P, 2, 2, BLK])
        Bp = ps("b_ps", [P, BLK])
        Cp = ps("c_ps", [P, BLK])
        Yp = [ps(f"y_ps{h}", [P, BLK]) for h in range(2)]
        s_bm, s_cm, s_b, s_c, s_da, s_db, s_h, s_hc, s_y, s_yu, s_yg, s_z = (
            sem(n) for n in ("b_ps", "c_ps", "b_spread", "c_spread", "decay", "drive", "states", "states_c",
                               "y_ps", "y_u", "y_gated", "decay_zero"))
        steps = [(k, n) for k in range(NBK) for n in range(NS)]
        with nc.Block() as block:
            @block.tensor
            def _(pe):
                def spread_bc(i):
                    k, n = steps[i]
                    for dst, row, full, out in ((Bp, n, s_bm, s_b), (Cp, NS + n, s_cm, s_c)):
                        wait(pe, out, i)
                        for c in range(BLK // 512):
                            cols = slice(k * BLK + c * 512, k * BLK + (c + 1) * 512)
                            last = pe.matmul(dst[:, c * 512:(c + 1) * 512], v["sel"][64:128, row, :],
                                             v["bc"][64:128, cols], start=True, stop=True)
                        last.then_inc(full, 1)

                def add_up(i):
                    k, n = steps[i]
                    if n == 0 and k > 0:
                        pe.wait_ge(s_yu, 2 * k)
                    for h in range(2):
                        pe.wait_ge(s_hc, 2 * i + h + 1)
                        for c in range(BLK // 512):
                            last = pe.matmul(Yp[h][:, c * 512:(c + 1) * 512], w["ident"][:],
                                             HC[:, i % 2, h, c * 512:(c + 1) * 512], start=(n == 0), stop=(n == NS - 1))
                        last.then_inc(s_y, 1)
                spread_bc(0)
                spread_bc(1)
                for i in range(len(steps)):
                    if i + 2 < len(steps):
                        spread_bc(i + 2)
                    add_up(i)

            @block.scalar
            def _(act):
                act.wait_ge(s_z, 1)
                for i, (k, n) in enumerate(steps):
                    act.wait_ge(s_bm, i + 1)
                    wait(act, s_db, 2 * i - 2)
                    act.activation(bs[:, i % 2, :], Bp[:], ACT.Copy).then_inc(s_b, 1)
                    for h in range(2):
                        wait(act, s_h, 2 * (i - 2) + h + 1)
                        act.activation(dA[:, i % 2, h, :].rearrange("p (b l) -> p b l", l=L)[:, :, 1:],
                                       v["delta"][:, h, k * BLK:(k + 1) * BLK].rearrange("p (b l) -> p b l", l=L)[:, :, 1:],
                                       ACT.Exp, scale=v["a"][:, h, n:n + 1]).then_inc(s_da, 1)
                    act.wait_ge(s_cm, i + 1)
                    wait(act, s_hc, 2 * i - 2)
                    act.activation(cs[:, i % 2, :], Cp[:], ACT.Copy).then_inc(s_c, 1)

            @block.vector
            def _(dve):
                for i in range(2):
                    last = dve.memset(dA[:, i].rearrange("p h (b l) -> p (h b) l", l=L)[:, :, 0:1], 0.0)
                last.then_inc(s_z, 1)

                def finish(k):
                    dve.wait_ge(s_y, 2 * NS * (k + 1))
                    c = slice(k * BLK, (k + 1) * BLK)
                    for h in range(2):
                        dve.scalar_tensor_tensor(out=v["du"][:, h, c], in0=v["u"][:, h, c], scalar=v["D"][:, h:h + 1],
                                                 in1=Yp[h][:], op0=ALU.mult, op1=ALU.add).then_inc(s_yu, 1)
                    dve.wait_ge(s_yu, 2 * (k + 1))
                    for h in range(2):
                        dve.tensor_tensor(v["du"][:, h, c], v["du"][:, h, c], v["gate"][:, h, c], ALU.mult)

                for i, (k, n) in enumerate(steps):
                    for h in range(2):
                        dve.wait_ge(s_b, i + 1)
                        wait(dve, s_h, 2 * (i - 2) + h + 1)
                        dve.tensor_tensor(dB[:, i % 2, h, :], v["du"][:, h, k * BLK:(k + 1) * BLK], bs[:, i % 2, :],
                                          ALU.mult).then_inc(s_db, 1)
                    for h in range(2):
                        dve.wait_ge(s_da, 2 * i + h + 1)
                        dve.wait_ge(s_db, 2 * i + h + 1)
                        wait(dve, s_hc, 2 * (i - 2) + h + 1)
                        dve.tensor_tensor_scan(H[:, i % 2, h, :], dA[:, i % 2, h, :], dB[:, i % 2, h, :], 0.0,
                                               ALU.mult, ALU.add).then_inc(s_h, 1)
                    if n == 1 and k > 0:
                        finish(k - 1)
                finish(NBK - 1)

            @block.gpsimd
            def _(pool):
                for i in range(len(steps)):
                    pool.wait_ge(s_c, i + 1)
                    for h in range(2):
                        pool.wait_ge(s_h, 2 * i + h + 1)
                        wait(pool, s_y, 2 * (i - 2) + h + 1)
                        pool.tensor_tensor(HC[:, i % 2, h, :], H[:, i % 2, h, :], cs[:, i % 2, :],
                                           ALU.mult).then_inc(s_hc, 1)


def ssm_out_part(w, v, old):
    def head(sb, ps, sem):
        WO, s_w = v["WO"], v["s_wo"]
        wq, wscale = v["wq"], v["wscale"]
        idb = sb("ident_bf16", [P, P], BF16)
        R = sb("rows", [P, NT, D])
        Hn = sb("normed", [P, NT, D])
        stats = sb("out_stats", [P, 2, NT, 6])
        mv = sb("out_mean_var", [P, 2, NT, 2])
        ms = sb("mean_square", [P, 2, NT])
        rs = sb("rsqrt", [P, 2, NT])
        am = sb("abs_max", [P, 2, NT])
        ar = sb("abs_recip", [P, 2, NT])
        sc = sb("scales", [P, 3, NT])
        qa = sb("q_in", [P, NT, D])
        qb = sb("q_in_bf16", [P, NT, D], BF16)
        qT = sb("q_in_T", [P, T], BF16)
        gate = sb("gate", [P, 2, FD])
        gu = sb("gate_up", [P, 2, FD])
        g2 = sb("gate_up_rounded", [P, 2, FD])
        gb = sb("gate_up_bf16", [P, 2, FD], BF16)
        gT = sb("gate_up_T", [P, 2, 4, P], BF16)
        yb = ps("y_ps", [P, 2, NQ])
        gp = ps("gate_ps", [P, FD])
        up = [ps(f"up_ps{i}", [P, FD]) for i in range(2)]
        tb = ps("T_ps", [P, 2, 2 * FD], BF16)
        s_y, s_yout, s_dve, s_ms, s_rs, s_q, s_tm, s_qT, s_id = (
            sem(n) for n in ("y_ps", "y_out", "chain", "mean_square", "rsqrt", "rounded", "T_ps", "rounded_T", "ident"))
        s_gm, s_um, s_gate, s_gu, s_gq, s_gtm, s_gT, s_dm, s_dout, s_ms2, s_rs2, s_po = (
            sem(n) for n in ("gate_ps", "up_ps", "gate", "gate_up", "gu_rounded", "gu_T_ps", "gu_T", "down_ps",
                               "down_out", "mean_square2", "rsqrt2", "pool"))
        s_root, s_hn, s_sum = sem("root_chain"), sem("second_norm"), sem("x_added")
        eps = sb("eps", [P, TQ])
        def gpsimd(pool):
            clear(pool, old)
            pool.memset(eps[:], 1e-6).then_inc(s_po, 1)
            pool.wait_ge(s_po, 1)
            link = chain(pool, s_root)
            for k, measured, done in ((0, s_ms, s_rs), (1, s_ms2, s_rs2)):
                for q in range(Q):
                    c = slice(q * TQ, (q + 1) * TQ)
                    pool.wait_ge(measured, q + 1)
                    link(pool.tensor_tensor(ms[:, k, c], mv[:, k, c, 0], mv[:, k, c, 0], ALU.mult))
                    link(pool.tensor_tensor(ms[:, k, c], ms[:, k, c], mv[:, k, c, 1], ALU.add))
                    link(pool.tensor_tensor(ms[:, k, c], ms[:, k, c], eps[:], ALU.add))
                    pool.tensor_tensor(rs[:, k, c], ms[:, k, c], w["minus_half"][:, 0:TQ],
                                       ALU.pow).then_inc(done, 1)

        def tensor(pe):
            pe.wait_ge(s_w, 64)
            for q in range(Q):
                if q >= 2:
                    pe.wait_ge(s_yout, q - 1)
                for i in range(TQ):
                    t = q * TQ + i
                    for h in range(2):
                        last = pe.matmul(yb[:, q % 2, i * D:(i + 1) * D], v["du"][:, h, t * P:(t + 1) * P],
                                         WO[:, h, :], start=(h == 0), stop=(h == 1))
                last.then_inc(s_y, 1)
            pe.wait_ge(s_id, 1)
            pe.wait_ge(s_q, 1)
            for k in range(2):
                for i in range(8):
                    t = 8 * k + i
                    last = pe.transpose(tb[:, k, i * P:(i + 1) * P], qb[:, t, :], idb[:])
                last.then_inc(s_tm, 1)
            pe.wait_ge(s_qT, 2)

            def gate_up(t):
                wait(pe, s_gate, t)
                pe.matmul(gp[:], qT[:, t * P:(t + 1) * P], wq[:, 0, :], start=True, stop=True).then_inc(s_gm, 1)
                wait(pe, s_gu, t - 1)
                pe.matmul(up[t % 2][:], qT[:, t * P:(t + 1) * P], wq[:, 1, :], start=True,
                          stop=True).then_inc(s_um, 1)
            gate_up(0)
            gate_up(1)
            for t0 in range(0, NT, 2):
                if t0 + 2 < NT:
                    gate_up(t0 + 2)
                    gate_up(t0 + 3)
                pe.wait_ge(s_gq, t0 // 2 + 1)
                for t in (t0, t0 + 1):
                    wait(pe, s_gT, t - 1)
                    for c in range(4):
                        last = pe.transpose(tb[:, t % 2, c * P:(c + 1) * P], gb[:, t % 2, c * P:(c + 1) * P], idb[:])
                    last.then_inc(s_gtm, 1)
                for t in (t0, t0 + 1):
                    pe.wait_ge(s_gT, t + 1)
                    wait(pe, s_dout, t - 1)
                    for c in range(4):
                        last = pe.matmul(yb[:, t % 2, 0:D], gT[:, t % 2, c, :], wq[:, 2, c * D:(c + 1) * D],
                                         start=(c == 0), stop=(c == 3))
                    last.then_inc(s_dm, 1)

        def scalar(act):
            for k in range(2):
                act.wait_ge(s_tm, k + 1)
                act.activation(qT[:, k * BLK:(k + 1) * BLK], tb[:, k, :], ACT.Copy).then_inc(s_qT, 1)
            def gates(t):
                act.wait_ge(s_gm, t + 1)
                wait(act, s_gu, t - 1)
                act.activation(gate[:, t % 2, :], gp[:], ACT.Sigmoid, scale=sc[:, 0, t:t + 1]).then_inc(s_gate, 1)
            gates(0)
            gates(1)
            for t0 in range(0, NT, 2):
                if t0 + 2 < NT:
                    gates(t0 + 2)
                    gates(t0 + 3)
                for t in (t0, t0 + 1):
                    act.wait_ge(s_gtm, t + 1)
                    wait(act, s_dm, t - 1)
                    act.activation(gT[:, t % 2].rearrange("p c t -> p (c t)"), tb[:, t % 2, 0:FD],
                                   ACT.Copy).then_inc(s_gT, 1)

        def vector(dve):
            link = chain(dve, s_dve)
            over = lambda x, n=NT: x.rearrange("p (t o) -> p t o", o=1).to_broadcast([P, n, D])
            dve.tensor_copy(idb[:], w["ident"][:]).then_inc(s_id, 1)

            def rounded(dst, src, width):
                lo, hi = width
                link(dve.tensor_scalar(src, src, ROUND + lo, ROUND + hi, ALU.max, ALU.min))
                return dve.tensor_scalar(dst, src, ROUND, None, ALU.subtract)

            def measure(k, q, sem):
                for t in range(q * TQ, q * TQ + TQ):
                    last = dve.bn_stats(stats[:, k, t, :], R[:, t, :])
                link(last)
                for t in range(q * TQ, q * TQ + TQ):
                    last = dve.bn_aggr(mv[:, k, t, :], stats[:, k, t, :])
                last.then_inc(sem, 1)

            for q in range(Q):
                a, b = q * TQ, q * TQ + TQ
                dve.wait_ge(s_y, q + 1)
                dve.tensor_tensor(R[:, a:b, :], yb[:, q % 2, :].rearrange("p (t d) -> p t d", d=D),
                                  w["Y"][:, a:b, :], ALU.add).then_inc(s_yout, 1)
                dve.wait_ge(s_yout, q + 1)
                measure(0, q, s_ms)
            for t in range(NT):
                if t % TQ == 0:
                    dve.wait_ge(s_rs, t // TQ + 1)
                last = dve.scalar_tensor_tensor(out=Hn[:, t, :], in0=R[:, t, :], scalar=rs[:, 0, t:t + 1],
                                                in1=w["norm1_row"][:], op0=ALU.mult, op1=ALU.mult)
            link(last)
            link(dve.tensor_reduce(am[:, 0, :], Hn[:], AX.X, ALU.max, apply_absolute_value=True))
            link(dve.tensor_scalar(am[:, 0, :], am[:, 0, :], 1e-5, None, ALU.max))
            link(dve.reciprocal(ar[:, 0, :], am[:, 0, :]))
            link(dve.tensor_scalar(ar[:, 0, :], ar[:, 0, :], 127.0, None, ALU.mult))
            for t in range(NT):
                last = dve.tensor_scalar(qa[:, t, :], Hn[:, t, :], ar[:, 0, t:t + 1], ROUND, ALU.mult, ALU.add)
            link(last)
            for k in range(2):
                link(dve.tensor_scalar(sc[:, k, :], am[:, 0, :], wscale[:, k:k + 1], 1.0 / 127, ALU.mult, ALU.mult))
            rounded(qb[:], qa[:], (-128.0, 127.0)).then_inc(s_q, 1)

            def second(tiles):
                t0 = tiles[0]
                for t in tiles:
                    dve.wait_ge(s_gate, t + 1)
                    dve.wait_ge(s_um, t + 1)
                    dve.scalar_tensor_tensor(out=gu[:, t % 2, :], in0=up[t % 2][:], scalar=sc[:, 1, t:t + 1],
                                             in1=gate[:, t % 2, :], op0=ALU.mult, op1=ALU.mult).then_inc(s_gu, 1)
                a, r = am[:, 1, t0:t0 + 2], ar[:, 1, t0:t0 + 2]
                dve.wait_ge(s_gu, t0 + 2)
                link(dve.tensor_reduce(a, gu[:], AX.X, ALU.max, apply_absolute_value=True))
                link(dve.tensor_scalar(a, a, 1e-5, None, ALU.max))
                link(dve.reciprocal(r, a))
                link(dve.tensor_scalar(r, r, 127.0, None, ALU.mult))
                for t in tiles:
                    last = dve.tensor_scalar(g2[:, t % 2, :], gu[:, t % 2, :], ar[:, 1, t:t + 1], ROUND, ALU.mult,
                                             ALU.add)
                dve.tensor_scalar(sc[:, 2, t0:t0 + 2], a, wscale[:, 2:3], 1.0 / 127, ALU.mult, ALU.mult)
                link(last)
                wait(dve, s_gtm, t0)
                rounded(gb[:], g2[:], (-128.0, 127.0)).then_inc(s_gq, 1)

            def third(t):
                dve.wait_ge(s_dm, t + 1)
                dve.scalar_tensor_tensor(out=R[:, t, :], in0=yb[:, t % 2, 0:D], scalar=sc[:, 2, t:t + 1],
                                         in1=Hn[:, t, :], op0=ALU.mult, op1=ALU.add).then_inc(s_dout, 1)
            for t in range(0, NT + 2, 2):
                if t < NT:
                    second((t, t + 1))
                if t >= 2:
                    third(t - 2)
                    third(t - 1)
            dve.wait_ge(s_dout, NT)
            for q in range(Q):
                measure(1, q, s_ms2)

        def add(dve, q):
            dve.wait_ge(s_rs2, q + 1)
            for t in range(q * TQ, q * TQ + TQ):
                last = dve.scalar_tensor_tensor(out=Hn[:, t, :], in0=R[:, t, :], scalar=rs[:, 1, t:t + 1],
                                                in1=w["norm2_row"][:], op0=ALU.mult, op1=ALU.mult)
            last.then_inc(s_hn, 1)
            dve.wait_ge(s_hn, q + 1)
            x = w["X"][:, q * TQ:(q + 1) * TQ, :]
            dve.tensor_tensor(x, x, Hn[:, q * TQ:(q + 1) * TQ, :], ALU.add).then_inc(s_sum, 1)
            dve.wait_ge(s_sum, q + 1)
        return {"tensor": tensor, "scalar": scalar, "gpsimd": gpsimd, "vector": vector, "add": add, "banks": (gp,)}
    return head


def ssm_stages(nc, w, pre, ctx):
    sb, ps, sem = place(nc, ctx, "ssm")
    v = dict(pre)
    v["wq"] = w["QT"][:, 0:3 * FD // 2].bitcast(BF16).rearrange("p (k f) -> p k f", k=3)
    v["wscale"] = sb("w_scale", [P, 3])
    for name in ("u", "gate", "delta", "du"):
        v[name] = sb(name, [P, 2, T])
    with ExitStack() as inner:
        sb, ps, sem = place(nc, inner, "ssmi")
        v["bc"] = sb("bc", [P, T], F32R)
        v["sel"] = sb("sel", [P, 2 * NS, P], F32R)
        with ExitStack() as tmp:
            v["sel32"] = place(nc, tmp, "ssmt")[0]("sel32", [P, 2 * NS, P])
            ssm_in_stage(nc, w, v, w["old"])
        old = ended()
        old.remove(v["s_wo"])
        ssm_scan_stage(nc, w, v)
    return ssm_out_part(w, v, old)


def fold_part(ins, dst, a_name, b_name, k, h, scale=1.0):
    def head(sb, ps, sem):
        a, b = sb("fold_a", [k, h, D]), sb("fold_b", [k, h, D])
        bank = [ps(f"fold{i}", [P, 512]) for i in range(2)]
        s_in, s_mm, s_folded = sem("fold_in"), sem("folded_ps"), sem("folded")

        def sync(sp):
            for buf, src in ((a, a_name), (b, b_name)):
                sp.dma_start(buf[:], ins[src].rearrange("h c d -> c h d")).then_inc(s_in, 16)

        def tensor(pe):
            pe.wait_ge(s_in, 32)
            for c in range(h // 4):
                wait(pe, s_folded, c - 1)
                for i in range(4 * c, 4 * c + 4):
                    last = pe.matmul(bank[c % 2][:, i % 4 * D:(i % 4 + 1) * D], a[:, i, :], b[:, i, :], start=True,
                                     stop=True)
                last.then_inc(s_mm, 1)

        def scalar(act):
            for c in range(h // 4):
                act.wait_ge(s_mm, c + 1)
                act.activation(dst[:, 4 * c:4 * c + 4, :], bank[c % 2][:, :].rearrange("p (h d) -> p h d", h=4),
                               ACT.Copy, scale=scale).then_inc(s_folded, 1)
        return {"sync": sync, "tensor": tensor, "scalar": scalar}
    return head


def prepare_part(w, ins):
    def head(sb, ps, sem):
        fold = fold_part(ins, w["M0"], "L0_xattn_WqT", "L0_xattn_WkT", 16, 8)(sb, ps, sem)
        s_affine, s_small, s_id = (sem(n) for n in ("gain_shift", "small", "ident"))
        s_x = [sem(f"x{q}") for q in range(Q)]
        small = [(key, ins[src].rearrange("(p o) -> p o", o=1)) for key, src in (
            ("ln_g", "L0_xattn_ln_g"), ("ln_b", "L0_xattn_ln_b"), ("ln2_w", "L1_xattn_ln2_w"), ("ln2_b", "L1_xattn_ln2_b"))]
        small += [(key, ins[src].rearrange("(o d) -> o d", o=1).to_broadcast([P, D])) for key, src in (
            ("ln1_w", "L1_xattn_ln1_w"), ("ln1_b", "L1_xattn_ln1_b"), ("ln_g_row", "L0_xattn_ln_g"),
            ("ln_b_row", "L0_xattn_ln_b"), ("ln2_w_row", "L1_xattn_ln2_w"), ("ln2_b_row", "L1_xattn_ln2_b"),
            ("norm1_row", "L1_attn_norm1_w"), ("norm2_row", "L1_attn_norm2_w"))]
        small += [("V0", ins["L0_xattn_Wv"]), ("Wo0", ins["L0_xattn_Wo"])]

        def sync(sp):
            for q in range(Q):
                sp.dma_start(w["X"][:, q * TQ:(q + 1) * TQ, :], token_tiles(ins["x"], q)).then_inc(s_x[q], 16)
            for key, src in small:
                sp.dma_start(w[key][:], src).then_inc(s_small, 16)
            sp.wait_ge(s_small, 16 * len(small))

        def scalar(act):
            fold["sync"](act)
            for key, src in (("pre_g", "L0_xattn_pre_g"), ("pre_b", "L0_xattn_pre_b")):
                act.dma_start(w[key][:], ins[src].rearrange("(p o) -> p o", o=1)).then_inc(s_affine, 16)
            fold["scalar"](act)
            act.wait_ge(s_affine, 32)

        def tensor(pe):
            fold["tensor"](pe)
            pe.wait_ge(s_id, 2)

        def gpsimd(pool):
            pool.memset(w["minus_half"][:], -0.5)
            pool.memset(w["eps"][:], EPS5)
            pool.memset(w["zero"][:], 0.0)
            pool.memset(w["ident"][:], 0.0).then_inc(s_id, 1)
            pool.wait_ge(s_id, 1)
            pool.affine_select(out=w["ident"][:], in_=w["ident"][:], compare_op=ALU.not_equal, fill=1.0, base=0,
                               pattern=[[-1, P]], channel_multiplier=1).then_inc(s_id, 1)

        def add(dve, q):
            dve.wait_ge(s_x[q], 16)
        return {"sync": sync, "scalar": scalar, "tensor": tensor, "gpsimd": gpsimd, "add": add}
    return head


def build(nc, ins, out):
    with ExitStack() as ctx:
        sb, ps, sem = place(nc, ctx, "all")
        w = {}
        folded = ExitStack()
        del TAKEN[:]
        for name, shape in (("X", [P, NT, D]), ("O", [P, NT, D]), ("Y", [P, NT, D]), ("N", [P, NT, D]), ("QT", [P, T]),
                            ("ident", [P, P]), ("minus_half", [P, NT]), ("eps", [P, 4]), ("zero", [P, 4]), ("pre_g", [D, 1]), ("pre_b", [D, 1]),
                            ("ln_g", [D, 1]), ("ln_b", [D, 1]), ("ln2_w", [D, 1]), ("ln2_b", [D, 1]),
                            ("ln1_w", [P, D]), ("ln1_b", [P, D]), ("ln_g_row", [P, D]), ("ln_b_row", [P, D]),
                            ("ln2_w_row", [P, D]), ("ln2_b_row", [P, D]), ("norm1_row", [P, D]), ("norm2_row", [P, D])):
            w[name] = sb(name, shape)
        fold_sb, _, _ = place(nc, folded, "all")
        for name, shape in (("M0", [P, 8, D]), ("M1", [P, 16, D]), ("VO", [P, 16, D]), ("V0", [D, D]),
                            ("Wo0", [D, D])):
            w[name] = fold_sb(name, shape)
        dram = {
            "ctx": ins["ctx_1024"],
            "kv_a": nc.dram_tensor("kv_a", (B, KC, 2 * D), F32, kind="Internal").ap(),
            "kv_b": nc.dram_tensor("kv_b", (B, KR, D), F32, kind="Internal").ap(),
            "kv_lat": nc.dram_tensor("kv_lat", (B, L, D), F32, kind="Internal").ap(),
        }
        norm_stage(nc, w, "q0", w["X"], w["Y"], w["QT"], gain=w["pre_g"], shift=w["pre_b"], twice=True,
                   head=prepare_part(w, ins))
        w["M"], w["V"] = w["M0"], w["V0"]
        attention_stage(nc, w, 0, dram)
        norm_stage(nc, w, "o0", w["O"], w["Y"], w["QT"], gain=w["ln_g"], shift=w["ln_b"],
                   row_affine=(w["ln_g_row"], w["ln_b_row"]), rows_out=w["N"])
        old = ended()
        with ExitStack() as pre:
            weights = self_attention_weights(nc, pre, ins)
            norm_stage(nc, w, "sa_n", w["X"], w["Y"], w["QT"], first=weights["first"], head=gelu_part(w, old))
            attention = self_attention_part(w, weights)
            old = ended()
            for k in ("s_w", "s_f"):
                old.remove(weights[k])
                TAKEN.append(weights[k])
            weights = moe_weights(nc, pre, ins, 0)
            norm_stage(nc, w, "moe0_n", w["X"], w["Y"], w["QT"], first=weights["first"], head=attention)
            norm_stage(nc, w, "q1", w["X"], w["Y"], w["QT"], gain=w["ln2_w"], shift=w["ln2_b"], twice=True,
                       row_affine=(w["ln2_w_row"], w["ln2_b_row"]), rows_out=w["N"],
                       rows_T=dram["kv_lat"].rearrange("(t a) l d -> t (a l) d", a=BT),
                       head=moe_part(w, weights, 0, old))
        w["M"], w["V"] = w["M1"], w["VO"]
        attention_stage(nc, w, 1, dram)
        folded.close()
        w["old"] = ended()
        with ExitStack() as pre:
            weights = ssm_weights(nc, pre, ins)
            norm_stage(nc, w, "ssm_n", w["X"], w["Y"], w["QT"], add=w["O"], first=weights["first"])
            tail = ssm_stages(nc, w, weights, pre)
            weights = moe_weights(nc, pre, ins, 1)
            norm_stage(nc, w, "moe1_n", w["X"], w["Y"], w["QT"], first=weights["first"], head=tail)
            run_stage(nc, moe_part(w, weights, 1, [], out), "moe1")


def layout(inputs):
    a = {k: np.asarray(v) for k, v in inputs.items()}
    wkv = a["L1_xattn_Wkv"]
    inner = wkv.shape[1] // 2

    def heads(m, h):
        return np.ascontiguousarray(m.T.reshape(h, -1, m.shape[0]))

    out = {
        "x": a["x"], "ctx_1024": a["ctx_1024"],
        "L0_xattn_WqT": heads(a["L0_xattn_Wq"], 8), "L0_xattn_WkT": heads(a["L0_xattn_Wk"], 8),
        "L1_xattn_WqT": heads(a["L1_xattn_Wq"], 16), "L1_xattn_WkT": heads(wkv[:, :inner], 16),
        "L1_xattn_WvT": heads(wkv[:, inner:], 16), "L1_xattn_Wo": a["L1_xattn_Wo"].reshape(16, 64, D),
    }
    for k in ("L0_xattn_Wv", "L0_xattn_Wo", "L0_xattn_pre_g", "L0_xattn_pre_b", "L0_xattn_ln_g", "L0_xattn_ln_b",
              "L1_xattn_ln1_w", "L1_xattn_ln1_b", "L1_xattn_ln2_w", "L1_xattn_ln2_b", "L1_attn_norm1_w",
              "L1_attn_norm2_w"):
        out[k] = a[k]
    for k in ("q", "k", "v"):
        out[f"L0_attn_w{k}T"] = a[f"L0_attn_w{k}"].T
    out["moe0_router_T"], out["moe1_router_T"] = a["L0_ffn_router_w"].T, a["L1_ffn_Wr"].T
    out["moe0_w_in_T"] = a["L0_ffn_w1"].transpose(0, 2, 1)
    out["moe0_w_out_T"] = a["L0_ffn_w2"].transpose(0, 2, 1)
    out["moe1_w_in_T"] = np.stack([a["L1_ffn_Wg"], a["L1_ffn_Wu"]], 1).transpose(0, 1, 3, 2).reshape(16, D, 4 * D)
    out["moe1_w_out_T"] = a["L1_ffn_Wd"].transpose(0, 2, 1)
    out["in_proj_T"], out["out_proj_T"] = a["L1_attn_in_proj_w"].T, a["L1_attn_out_proj_w"].T
    out["x_proj_T"], out["dt_proj_T"] = a["L1_attn_x_proj_w"].T, a["L1_attn_dt_proj_w"].T
    for k in ("gate", "up", "down"):
        out[f"{k}_T"] = a[f"L1_attn_{k}_w"].T
    for k in ("conv_w", "conv_b", "dt_proj_b", "A_log", "D"):
        out[k] = a[f"L1_attn_{k}"]
    return {k: np.ascontiguousarray(v) for k, v in out.items()}


def kernel(**inputs):
    import concourse.bacc as _bacc
    from concourse.bass_utils import run_bass_kernel_spmd as _run

    nc = _bacc.Bacc("TRN2", target_bir_lowering=False, num_devices=1)
    arrays, ins = {}, {}
    for name, a in layout(inputs).items():
        arrays[f"in_{name}"] = a
        ins[name] = nc.dram_tensor(f"in_{name}", a.shape, mybir.dt.from_np(a.dtype), kind="ExternalInput").ap()
    out = nc.dram_tensor("out_x", (B, L, D), F32, kind="ExternalOutput").ap()
    build(nc, ins, out)
    r = _run(nc, [arrays], core_ids=[0])
    return r.results[0]["out_x"]
```
